# Optimizing a Trainium2 kernel written in Bass

```python
import numpy as np
import jax
import jax.numpy as jnp

def _softmax(x, axis=-1):
    return jax.nn.softmax(x, axis=axis)

def _gelu(x):
    return jax.nn.gelu(x, approximate=True)

def _silu(x):
    return jax.nn.silu(x)

def _sigmoid(x):
    return jax.nn.sigmoid(x)

def _layernorm(x, axis=-1, eps=1e-05):
    m = jnp.mean(x, axis=axis, keepdims=True)
    v = jnp.var(x, axis=axis, keepdims=True)
    return (x - m) / jnp.sqrt(v + eps)

def _scatter_add(tgt, idx, src, axis=0):
    return tgt.at[idx].add(src)

def _segment_sum(src, seg, n):
    return jax.ops.segment_sum(src, seg, n)
kernel_name = 'mk_adj_ffn_d2_adj_r2_73438f'

def setup_inputs(seed: int=0):
    np.random.seed(seed)
    _w = jnp.asarray

    def _rec_inputs():
        import jax
        import jax.numpy as jnp
        _gk = jax.random.key(seed)
        x = -0.0005207 + 1.001 * jax.random.normal(jax.random.fold_in(_gk, 1), (128, 128, 128), jnp.float32)
        _a = jax.random.bernoulli(jax.random.fold_in(_gk, 2), 0.03125, (128, 128, 128))
        _a = jnp.logical_or(_a, jnp.swapaxes(_a, -1, -2))
        _a = jnp.logical_or(_a, jnp.eye(128, dtype=bool))
        adj = _a.astype(jnp.int32)
        return (x, adj)
    x, adj = _rec_inputs()

    def _L0_gnn_setup():
        import jax, jax.numpy as jnp
        import numpy as np
        B, N, D, H = (4, 1024, 128, 8)
        HD = D // H
        DFF = 4 * D
        EPS = 1e-05

        def layer_norm(x, gamma, beta):
            mu = jnp.mean(x, axis=-1, keepdims=True)
            var = jnp.mean(jnp.square(x - mu), axis=-1, keepdims=True)
            return (x - mu) * jax.lax.rsqrt(var + EPS) * gamma + beta
        key = jax.random.key(seed)
        ks = jax.random.split(key, 10)
        x = jax.random.normal(ks[0], (B, N, D), dtype=jnp.float32)
        adj = jax.random.randint(ks[1], (B, N, N), 0, 2).astype(jnp.int32)
        idx = jnp.arange(N)
        adj = adj.at[:, idx, idx].set(1)
        gamma1 = 1.0 + 0.02 * jax.random.normal(ks[2], (D,), dtype=jnp.float32)
        beta1 = 0.02 * jax.random.normal(ks[3], (D,), dtype=jnp.float32)
        gamma2 = 1.0 + 0.02 * jax.random.normal(ks[4], (D,), dtype=jnp.float32)
        beta2 = 0.02 * jax.random.normal(ks[5], (D,), dtype=jnp.float32)
        W1 = 0.02 * jax.random.normal(ks[6], (D, DFF), dtype=jnp.float32)
        b1 = 0.01 * jax.random.normal(ks[7], (DFF,), dtype=jnp.float32)
        W2 = 0.02 * jax.random.normal(ks[8], (DFF, D), dtype=jnp.float32)
        b2 = 0.01 * jax.random.normal(ks[9], (D,), dtype=jnp.float32)
        return {'x': x, 'adj_matrix': adj, 'gamma1': gamma1, 'beta1': beta1, 'gamma2': gamma2, 'beta2': beta2, 'W1': W1, 'b1': b1, 'W2': W2, 'b2': b2}
    _L0_gnn_all = _L0_gnn_setup()
    _L0_gnn_in = {k: v for k, v in _L0_gnn_all.items() if k in ('gamma1', 'beta1', 'gamma2', 'beta2', 'W1', 'b1', 'W2', 'b2')}
    del _L0_gnn_all

    def _L0_ffn_setup():
        import jax, jax.numpy as jnp
        import numpy as np
        DIM = 128
        H = 8
        D = 64
        G = 64
        INNER = H * D
        SCALE = D ** (-0.5)
        key = jax.random.key(seed)
        ks = jax.random.split(key, 12)
        B, N = (4, 8192)
        x = jax.random.normal(ks[0], (B, N, DIM), dtype=jnp.float32)
        s = lambda fan_in: 1.0 / np.sqrt(fan_in)
        W_fx = jax.random.normal(ks[1], (DIM, INNER), dtype=jnp.float32) * s(DIM)
        b_fx = jnp.zeros((INNER,), dtype=jnp.float32)
        W_x = jax.random.normal(ks[2], (DIM, INNER), dtype=jnp.float32) * s(DIM)
        b_x = jnp.zeros((INNER,), dtype=jnp.float32)
        A = jax.random.normal(ks[3], (G, D), dtype=jnp.float32)
        Q, _ = jnp.linalg.qr(A.T)
        W_slice = Q[:, :G].astype(jnp.float32)
        b_slice = jnp.zeros((G,), dtype=jnp.float32)
        W_q = jax.random.normal(ks[4], (D, D), dtype=jnp.float32) * s(D)
        W_k = jax.random.normal(ks[5], (D, D), dtype=jnp.float32) * s(D)
        W_v = jax.random.normal(ks[6], (D, D), dtype=jnp.float32) * s(D)
        W_out = jax.random.normal(ks[7], (INNER, DIM), dtype=jnp.float32) * s(INNER)
        b_out = jnp.zeros((DIM,), dtype=jnp.float32)
        temperature = jnp.ones((1, H, 1, 1), dtype=jnp.float32) * 0.5
        return {'x': x, 'W_fx': W_fx, 'b_fx': b_fx, 'W_x': W_x, 'b_x': b_x, 'W_slice': W_slice, 'b_slice': b_slice, 'W_q': W_q, 'W_k': W_k, 'W_v': W_v, 'W_out': W_out, 'b_out': b_out, 'temperature': temperature}
    _L0_ffn_all = _L0_ffn_setup()
    _L0_ffn_in = {k: v for k, v in _L0_ffn_all.items() if k in ('W_fx', 'b_fx', 'W_x', 'b_x', 'W_slice', 'b_slice', 'W_q', 'W_k', 'W_v', 'W_out', 'b_out', 'temperature')}
    del _L0_ffn_all

    def _L1_gnn_setup():
        import jax, jax.numpy as jnp
        import numpy as np
        BS, N, D, R = (16, 256, 128, 2)
        key = jax.random.key(seed)
        ks = jax.random.split(key, 9)
        s = 1.0 / np.sqrt(D)
        return {'encoded_spans': jax.random.normal(ks[0], (BS, N, D), dtype=jnp.float32), 'w_rel1': jax.random.normal(ks[1], (R, D, D), dtype=jnp.float32) * s, 'w_root1': jax.random.normal(ks[2], (D, D), dtype=jnp.float32) * s, 'b1': jnp.zeros((D,), dtype=jnp.float32), 'w_rel2': jax.random.normal(ks[3], (R, D, D), dtype=jnp.float32) * s, 'w_root2': jax.random.normal(ks[4], (D, D), dtype=jnp.float32) * s, 'b2': jnp.zeros((D,), dtype=jnp.float32), 'aug_adj': jax.random.randint(ks[5], (BS, N, N), 0, 16, dtype=jnp.int64), 'punct_graph': jax.random.randint(ks[6], (BS, N, N), 0, 16, dtype=jnp.int64)}
    _L1_gnn_all = _L1_gnn_setup()
    _L1_gnn_in = {k: v for k, v in _L1_gnn_all.items() if k in ('w_rel1', 'w_root1', 'b1', 'w_rel2', 'w_root2', 'b2')}
    del _L1_gnn_all

    def _L1_ffn_setup():
        import jax, jax.numpy as jnp
        import numpy as np
        B, S, D, F, E, K = (8, 1024, 128, 512, 8, 2)
        key = jax.random.key(seed)
        ks = jax.random.split(key, 10)
        s = 0.02
        return {'x': jax.random.normal(ks[0], (B, S, D), dtype=jnp.float32), 'Wr': jax.random.normal(ks[1], (D, E), dtype=jnp.float32) * s, 'W1s': jax.random.normal(ks[2], (D, F), dtype=jnp.float32) * s, 'b1s': jnp.zeros((F,), dtype=jnp.float32), 'W2s': jax.random.normal(ks[3], (F, D), dtype=jnp.float32) * s, 'b2s': jnp.zeros((D,), dtype=jnp.float32), 'W1p': jax.random.normal(ks[4], (E, D, F), dtype=jnp.float32) * s, 'b1p': jnp.zeros((E, F), dtype=jnp.float32), 'W2p': jax.random.normal(ks[5], (E, F, D), dtype=jnp.float32) * s, 'b2p': jnp.zeros((E, D), dtype=jnp.float32)}
    _L1_ffn_all = _L1_ffn_setup()
    _L1_ffn_in = {k: v for k, v in _L1_ffn_all.items() if k in ('Wr', 'W1s', 'b1s', 'W2s', 'b2s', 'W1p', 'b1p', 'W2p', 'b2p')}
    del _L1_ffn_all
    return {'x': x, 'adj': adj, 'L0_gnn_gamma1': _L0_gnn_in['gamma1'], 'L0_gnn_beta1': _L0_gnn_in['beta1'], 'L0_gnn_gamma2': _L0_gnn_in['gamma2'], 'L0_gnn_beta2': _L0_gnn_in['beta2'], 'L0_gnn_W1': _L0_gnn_in['W1'], 'L0_gnn_b1': _L0_gnn_in['b1'], 'L0_gnn_W2': _L0_gnn_in['W2'], 'L0_gnn_b2': _L0_gnn_in['b2'], 'L0_ffn_W_fx': _L0_ffn_in['W_fx'], 'L0_ffn_b_fx': _L0_ffn_in['b_fx'], 'L0_ffn_W_x': _L0_ffn_in['W_x'], 'L0_ffn_b_x': _L0_ffn_in['b_x'], 'L0_ffn_W_slice': _L0_ffn_in['W_slice'], 'L0_ffn_b_slice': _L0_ffn_in['b_slice'], 'L0_ffn_W_q': _L0_ffn_in['W_q'], 'L0_ffn_W_k': _L0_ffn_in['W_k'], 'L0_ffn_W_v': _L0_ffn_in['W_v'], 'L0_ffn_W_out': _L0_ffn_in['W_out'], 'L0_ffn_b_out': _L0_ffn_in['b_out'], 'L0_ffn_temperature': _L0_ffn_in['temperature'], 'L1_gnn_w_rel1': _L1_gnn_in['w_rel1'], 'L1_gnn_w_root1': _L1_gnn_in['w_root1'], 'L1_gnn_b1': _L1_gnn_in['b1'], 'L1_gnn_w_rel2': _L1_gnn_in['w_rel2'], 'L1_gnn_w_root2': _L1_gnn_in['w_root2'], 'L1_gnn_b2': _L1_gnn_in['b2'], 'L1_ffn_Wr': _L1_ffn_in['Wr'], 'L1_ffn_W1s': _L1_ffn_in['W1s'], 'L1_ffn_b1s': _L1_ffn_in['b1s'], 'L1_ffn_W2s': _L1_ffn_in['W2s'], 'L1_ffn_b2s': _L1_ffn_in['b2s'], 'L1_ffn_W1p': _L1_ffn_in['W1p'], 'L1_ffn_b1p': _L1_ffn_in['b1p'], 'L1_ffn_W2p': _L1_ffn_in['W2p'], 'L1_ffn_b2p': _L1_ffn_in['b2p']}

def reference(x, adj, L0_gnn_gamma1, L0_gnn_beta1, L0_gnn_gamma2, L0_gnn_beta2, L0_gnn_W1, L0_gnn_b1, L0_gnn_W2, L0_gnn_b2, L0_ffn_W_fx, L0_ffn_b_fx, L0_ffn_W_x, L0_ffn_b_x, L0_ffn_W_slice, L0_ffn_b_slice, L0_ffn_W_q, L0_ffn_W_k, L0_ffn_W_v, L0_ffn_W_out, L0_ffn_b_out, L0_ffn_temperature, L1_gnn_w_rel1, L1_gnn_w_root1, L1_gnn_b1, L1_gnn_w_rel2, L1_gnn_w_root2, L1_gnn_b2, L1_ffn_Wr, L1_ffn_W1s, L1_ffn_b1s, L1_ffn_W2s, L1_ffn_b2s, L1_ffn_W1p, L1_ffn_b1p, L1_ffn_W2p, L1_ffn_b2p):
    import jax
    import jax.numpy as jnp

    def _L0_gnn_ref(x, adj_matrix, gamma1, beta1, gamma2, beta2, W1, b1, W2, b2):
        import jax, jax.numpy as jnp
        import numpy as np
        B, N, D, H = (4, 1024, 128, 8)
        HD = D // H
        DFF = 4 * D
        EPS = 1e-05

        def layer_norm(x, gamma, beta):
            mu = jnp.mean(x, axis=-1, keepdims=True)
            var = jnp.mean(jnp.square(x - mu), axis=-1, keepdims=True)
            return (x - mu) * jax.lax.rsqrt(var + EPS) * gamma + beta
        b_, n_, d_ = x.shape
        normed = layer_norm(x, gamma1, beta1)
        qkv = normed.reshape(b_, n_, H, HD).transpose(0, 2, 1, 3)
        scale = 1.0 / jnp.sqrt(jnp.asarray(HD, dtype=x.dtype))
        scores = jnp.einsum('bhqd,bhkd->bhqk', qkv, qkv) * scale
        mask = adj_matrix[:, None, :, :] > 0
        masked = jnp.where(mask, scores, -jnp.inf)
        attn = jax.nn.softmax(masked, axis=-1)
        out = jnp.einsum('bhqk,bhkd->bhqd', attn, qkv)
        out = out.transpose(0, 2, 1, 3).reshape(b_, n_, d_)
        x = x + out
        y = layer_norm(x, gamma2, beta2)
        mlp = jax.nn.gelu(y @ W1 + b1, approximate=False) @ W2 + b2
        return x + mlp

    def _L0_ffn_ref(x, W_fx, b_fx, W_x, b_x, W_slice, b_slice, W_q, W_k, W_v, W_out, b_out, temperature):
        import jax, jax.numpy as jnp
        import numpy as np
        DIM = 128
        H = 8
        D = 64
        G = 64
        INNER = H * D
        SCALE = D ** (-0.5)
        B, N, _ = x.shape
        fx_mid = (x @ W_fx + b_fx).reshape(B, N, H, D).transpose(0, 2, 1, 3)
        x_mid = (x @ W_x + b_x).reshape(B, N, H, D).transpose(0, 2, 1, 3)
        temp = jnp.clip(temperature, 0.1, 5.0)
        slice_weights = jax.nn.softmax((x_mid @ W_slice + b_slice) / temp, axis=-1)
        slice_norm = slice_weights.sum(axis=2)
        slice_token = jnp.einsum('bhnc,bhng->bhgc', fx_mid, slice_weights)
        slice_token = slice_token / (slice_norm[..., None] + 1e-05)
        q = slice_token @ W_q
        k = slice_token @ W_k
        v = slice_token @ W_v
        attn = jax.nn.softmax(jnp.einsum('bhgc,bhkc->bhgk', q, k) * SCALE, axis=-1)
        out_slice = jnp.einsum('bhgk,bhkc->bhgc', attn, v)
        out_x = jnp.einsum('bhgc,bhng->bhnc', out_slice, slice_weights)
        out_x = out_x.transpose(0, 2, 1, 3).reshape(B, N, INNER)
        return out_x @ W_out + b_out

    def _L1_gnn_ref(encoded_spans, w_rel1, w_root1, b1, w_rel2, w_root2, b2, aug_adj, punct_graph):
        import jax, jax.numpy as jnp
        import numpy as np
        BS, N, D, R = (16, 256, 128, 2)
        mask_punct = (punct_graph == 1) & (aug_adj != 1)
        mask_aug = aug_adj == 1
        masks = jnp.stack([mask_punct, mask_aug]).astype(encoded_spans.dtype)
        deg = jnp.maximum(masks.sum(axis=2), 1.0)[..., None]

        def conv(x, w_rel, w_root, b):
            out = jnp.einsum('bnd,de->bne', x, w_root) + b
            for r in range(R):
                agg = jnp.einsum('bij,bid->bjd', masks[r], x) / deg[r]
                out = out + jnp.einsum('bjd,de->bje', agg, w_rel[r])
            return out
        h = jax.nn.elu(conv(encoded_spans, w_rel1, w_root1, b1))
        h = jax.nn.elu(conv(h, w_rel2, w_root2, b2))
        return h

    def _L1_ffn_ref(x, Wr, W1s, b1s, W2s, b2s, W1p, b1p, W2p, b2p):
        import jax, jax.numpy as jnp
        import numpy as np
        B, S, D, F, E, K = (8, 1024, 128, 512, 8, 2)
        gelu = lambda t: jax.nn.gelu(t, approximate=False)
        shared = gelu(x @ W1s + b1s) @ W2s + b2s
        rw = jax.nn.softmax(x @ Wr, axis=-1)
        topw, topi = jax.lax.top_k(rw, K)
        topw = topw / jnp.sum(topw, axis=-1, keepdims=True)
        mask = jnp.sum(jax.nn.one_hot(topi, E, dtype=topw.dtype) * topw[..., None], axis=-2)
        h = gelu(jnp.einsum('bsd,edf->bsef', x, W1p) + b1p)
        priv = jnp.einsum('bsef,efd->bsed', h, W2p) + b2p
        routed = jnp.einsum('bsed,bse->bsd', priv, mask)
        return shared + routed
    x = x + _L0_gnn_ref(_layernorm(x, axis=-1), adj, L0_gnn_gamma1, L0_gnn_beta1, L0_gnn_gamma2, L0_gnn_beta2, L0_gnn_W1, L0_gnn_b1, L0_gnn_W2, L0_gnn_b2)
    x = x + _L0_ffn_ref(_layernorm(x, axis=-1), L0_ffn_W_fx, L0_ffn_b_fx, L0_ffn_W_x, L0_ffn_b_x, L0_ffn_W_slice, L0_ffn_b_slice, L0_ffn_W_q, L0_ffn_W_k, L0_ffn_W_v, L0_ffn_W_out, L0_ffn_b_out, L0_ffn_temperature)
    x = x + _L1_gnn_ref(_layernorm(x, axis=-1), L1_gnn_w_rel1, L1_gnn_w_root1, L1_gnn_b1, L1_gnn_w_rel2, L1_gnn_w_root2, L1_gnn_b2, adj, adj)
    x = x + _L1_ffn_ref(_layernorm(x, axis=-1), L1_ffn_Wr, L1_ffn_W1s, L1_ffn_b1s, L1_ffn_W2s, L1_ffn_b2s, L1_ffn_W1p, L1_ffn_b1p, L1_ffn_W2p, L1_ffn_b2p)
    return x

_drawn_inputs = setup_inputs


def setup_inputs(seed=0):
    import zlib

    import numpy as np

    out = dict(_drawn_inputs(seed))
    spreads = {'L0_ffn_b_fx': (0.0, 0.1),
     'L0_ffn_b_x': (0.0, 0.8),
     'L0_ffn_b_slice': (0.0, 0.8),
     'L0_ffn_b_out': (0.0, 0.577),
     'L0_ffn_temperature': (0.5, 0.6),
     'L1_gnn_b1': (0.0, 0.657),
     'L1_gnn_b2': (0.0, 0.614),
     'L1_ffn_b1s': (0.0, 0.8),
     'L1_ffn_b2s': (0.0, 0.8),
     'L1_ffn_b1p': (0.0, 0.8),
     'L1_ffn_b2p': (0.0, 1.272)}
    factors = {'L0_gnn_gamma1': 7.468,
     'L0_gnn_beta1': 5.955,
     'L0_gnn_gamma2': 8.0,
     'L0_gnn_beta2': 8.0,
     'L0_gnn_W1': 3.08,
     'L0_gnn_b1': 8.0,
     'L0_gnn_W2': 3.005,
     'L0_gnn_b2': 8.0,
     'L0_ffn_W_x': 8.0,
     'L0_ffn_W_slice': 8.0,
     'L0_ffn_W_q': 8.0,
     'L0_ffn_W_k': 8.0,
     'L1_ffn_W1s': 3.114,
     'L1_ffn_W2s': 2.874,
     'L1_ffn_W1p': 4.44,
     'L1_ffn_W2p': 4.0}
    for name, (base, spread) in spreads.items():
        noise = np.random.default_rng([zlib.crc32(name.encode()), seed]).standard_normal(out[name].shape)
        drawn = base * np.exp(spread * noise) if base else spread * noise
        out[name] = jnp.asarray(drawn.astype(out[name].dtype))
    for name, factor in factors.items():
        out[name] = (out[name] * factor).astype(out[name].dtype)
    return out
```

```python
from contextlib import ExitStack, contextmanager

import concourse.bass as bass
from concourse import mybir

F32 = mybir.dt.float32
BF16 = mybir.dt.bfloat16
I32 = mybir.dt.int32
U32 = mybir.dt.uint32
ALU = mybir.AluOpType
ACT = mybir.ActivationFunctionType
AX = mybir.AxisListType

T = 128
D = 128
GB = 4
W = GB * T
EPS = 1e-5
HEADS = 8
HD = D // HEADS
HP = HEADS // 2
C = 64
HC = HEADS * C
FF = 512
FC = FF // 128
EXPERTS = 8
MASKED = -1e30


def run_steps(eng, step, count, lag, peel):
    for t in range(peel):
        step(t, t // 2, t % 2, t)
    with eng.Fori(0, (count - peel) // 2) as pair:
        for half in range(2):
            step(pair * 2 + (peel + half), pair + peel // 2, half, None)
    for t in range(count, count + lag):
        step(t, t // 2, t % 2, t)


def live(known, delay, count):
    return known is None or 0 <= known - delay < count


def since(known, n):
    return known is None or known >= n


@contextmanager
def semaphores(nc):
    held = []

    def sem(name):
        held.append(nc.alloc_semaphore(name))
        return held[-1]

    yield sem
    nc.clear_and_free_semaphores(held)
    nc.all_engine_barrier()


class Shared:
    pass


def setup_phase(nc, sem, sh, w):
    with ExitStack() as ctx:
        def sb(name, shape, dt=F32):
            return ctx.enter_context(nc.sbuf_tensor(name, shape, dt))

        wx = sb("wx", [128, HC])
        bxT = sb("bxT", [128, HP])
        wsl = sb("wslice_bd", [128, 128])
        wq = sb("wq_bd", [128, 128])
        wk = sb("wk_bd", [128, 128])
        wv = sb("wv_bd", [128, 128])
        wout = sb("wout", [128, HP, 128])
        temp = sb("temp", [128, HEADS])
        rtemp = sb("rtemp", [128, HEADS])
        bsl = sb("bslice_row", [1, C])
        wxT = sb("wxT", [128, HP, 128])
        wT = sb("wT", [128, 3, 128])
        rows = sb("bias_rows", [1, 4, HC])
        rest = sb("bias_rest", [1, 4, 2, HC])
        zero_one = sb("zero_one", [1, 1])
        ps_t = ctx.enter_context(nc.psum_tensor("ps_t", [128, HP, 128], F32))
        ps_u = ctx.enter_context(nc.psum_tensor("ps_u", [128, 3, 128], F32))
        ps_w = ctx.enter_context(nc.psum_tensor("ps_w", [128, HP, 128], F32))
        ps_b = ctx.enter_context(nc.psum_tensor("ps_b", [1, HC], F32))
        ps_m = ctx.enter_context(nc.psum_tensor("ps_m", [128, 128], F32))
        ps_v = ctx.enter_context(nc.psum_tensor("ps_v", [128, HP, 128], F32))

        zeroed = sem("setup_zeroed")
        loaded = sem("setup_loaded")
        selected = sem("setup_selected")
        turned = sem("setup_turned")
        copied = sem("setup_copied")
        multiplied = sem("setup_multiplied")
        step_done = sem("setup_step")
        loads = []

        block = ctx.enter_context(nc.Block())

        def load_list(sp):
            col = lambda a: a.rearrange("(a b) -> a b", b=1)
            row = lambda a: a.rearrange("(a b) -> a b", a=1)
            everywhere = lambda a: row(a).to_broadcast([128, a.shape[0]])
            pairs = [(wx[:, :], w["W_x"]), (bxT[:, :], w["b_x"].rearrange("(a p) -> p a", p=128)),
                     (wout[:, :, :], w["W_out"].rearrange("(a p) n -> p a n", p=128)),
                     (temp[:, :], everywhere(w["temperature"].rearrange("a h b c -> (a h b c)"))),
                     (bsl[:, :], row(w["b_slice"])),
                     (rows[:, 1, :], row(w["b_fx"])),
                     (rows[:, 2, 0:D], row(w["b_out"])),
                     (rows[:, 3, 0:D], row(w["conv2_b"])),
                     (sh.wfx[:, :], w["W_fx"]),
                     (sh.g1col[:, :], col(w["gamma1"])), (sh.b1col[:, :], col(w["beta1"])),
                     (sh.g2col[:, :], col(w["gamma2"])), (sh.b2col[:, :], col(w["beta2"])),
                     (sh.g1all[:, :], everywhere(w["gamma1"])), (sh.b1all[:, :], everywhere(w["beta1"]))]
            for tile, a in ((wsl, w["W_slice"]), (wq, w["W_q"]), (wk, w["W_k"]), (wv, w["W_v"])):
                pairs += [(tile[0:C, 0:C], a), (tile[C:128, C:128], a)]
            return pairs

        N_LOADS = 15 + 8

        @block.sync
        def _(sp):
            sp.wait_ge(zeroed, 1)
            pairs = load_list(sp)
            assert len(pairs) == N_LOADS
            for tile, a in pairs:
                sp.dma_start(tile, a, allow_slow_non_contiguous=True).then_inc(loaded, 16)

        @block.gpsimd
        def _(pool):
            nc.gpsimd.memset(sh.ident[:, :], 0.0)
            nc.gpsimd.memset(sh.headmask[:, :], 1.0).then_inc(selected, 1)
            pool.wait_ge(selected, 1)
            nc.gpsimd.affine_select(out=sh.ident[:, :], in_=sh.ident[:, :], compare_op=ALU.not_equal, fill=1.0,
                                    base=0, pattern=[[-1, 128]], channel_multiplier=1)
            nc.gpsimd.affine_select(out=sh.headmask[:, :], in_=sh.headmask[:, :], compare_op=ALU.is_ge, fill=0.0,
                                    base=0, pattern=[[-HD, HEADS]], channel_multiplier=1).then_inc(selected, 1)
            pool.wait_ge(selected, 2)
            nc.gpsimd.affine_select(out=sh.headmask[:, :], in_=sh.headmask[:, :], compare_op=ALU.is_ge, fill=0.0,
                                    base=HD - 1, pattern=[[HD, HEADS]], channel_multiplier=-1).then_inc(selected, 1)

        @block.tensor
        def _(pe):
            pe.wait_ge(loaded, 16 * N_LOADS)
            pe.wait_ge(selected, 3)
            for i in range(HP):
                nc.tensor.transpose(ps_t[:, i, :], wx[:, i * 128:(i + 1) * 128], sh.ident[:, :])
            for i, a in enumerate((wq, wk, wv)):
                last = nc.tensor.transpose(ps_u[:, i, :], a[:, :], sh.ident[:, :])
            last.then_inc(turned, 1)
            pe.wait_ge(copied, 2)
            for i in range(HP):
                nc.tensor.matmul(ps_w[:, i, :], wxT[:, i, :], wsl[:, :], start=True, stop=True)
                nc.tensor.matmul(ps_b[:, i * 128:(i + 1) * 128], bxT[:, i:i + 1], wsl[:, :], start=True, stop=True)
                nc.tensor.matmul(ps_v[:, i, :], wT[:, 2, :], wout[:, i, :], start=True, stop=True)
            nc.tensor.matmul(ps_m[:, :], wT[:, 1, :], wT[:, 0, :], start=True, stop=True).then_inc(multiplied, 1)

        @block.vector
        def _(dve):
            for tile in (wsl, wq, wk, wv):
                nc.vector.memset(tile[:, :], 0.0)
            nc.vector.memset(sh.eps[:, :], EPS)
            nc.vector.memset(sh.half_power[:, :], -0.5)
            nc.vector.memset(sh.ones_bf[:, :], 1.0)
            nc.vector.memset(rows[:, :, :], 0.0)
            for tile in (sh.logit_bias, sh.fx_bias, sh.out_bias, sh.conv2_bias):
                last = nc.vector.memset(tile[:, :], 0.0)
            last.then_inc(zeroed, 1)
            dve.wait_ge(selected, 3)
            nc.vector.tensor_copy(sh.ident_bf[:, :], sh.ident[:, :])
            dve.wait_ge(loaded, 16 * N_LOADS)
            done = 0
            nc.vector.tensor_scalar(temp[:, :], temp[:, :], 0.1, 5.0, ALU.max, ALU.min).then_inc(step_done, 1)
            dve.wait_ge(step_done, 1)
            nc.vector.reciprocal(rtemp[:, :], temp[:, :]).then_inc(step_done, 1)
            dve.wait_ge(turned, 1)
            nc.vector.tensor_copy(wxT[:, :, :], ps_t[:, :, :]).then_inc(copied, 1)
            nc.vector.tensor_copy(wT[:, :, :], ps_u[:, :, :]).then_inc(copied, 1)
            dve.wait_ge(step_done, 2)
            dve.wait_ge(multiplied, 1)
            per_head = lambda ap: ap.rearrange("p (h c) -> p h c", c=C)
            nc.vector.tensor_tensor(per_head(sh.wlogit[:, :]),
                                    ps_w[:, :, :].rearrange("p i (e c) -> p (i e) c", c=C),
                                    rtemp[:, :].unsqueeze(2).to_broadcast([128, HEADS, C]), ALU.mult)
            nc.vector.tensor_copy(sh.wscore[:, :], ps_m[:, :])
            nc.vector.tensor_copy(sh.wvalue[:, :, :], ps_v[:, :, :])
            row = per_head(rows[:, 0, :])
            nc.vector.tensor_tensor(row, per_head(ps_b[:, :]), bsl[:, :].unsqueeze(1).to_broadcast([1, HEADS, C]),
                                    ALU.add).then_inc(step_done, 1)
            dve.wait_ge(step_done, 3)
            nc.vector.tensor_tensor(row, row, rtemp[0:1, :].unsqueeze(2).to_broadcast([1, HEADS, C]),
                                    ALU.mult).then_inc(step_done, 1)
            dve.wait_ge(step_done, 4)
            n = 4
            for i, (tile, width) in enumerate(((sh.logit_bias, HC), (sh.fx_bias, HC), (sh.out_bias, D),
                                               (sh.conv2_bias, D))):
                left = rows[:, i, 0:width]
                for j in range(3):
                    part = tile[32 * j:32 * j + 1, 0:width]
                    nc.vector.tensor_copy(part, left).then_inc(step_done, 1)
                    n += 1
                    if j < 2:
                        dve.wait_ge(step_done, n)
                        nc.vector.tensor_copy(rest[:, i, j, 0:width], part).then_inc(step_done, 1)
                        n += 1
                        dve.wait_ge(step_done, n)
                        nc.vector.tensor_tensor(rest[:, i, j, 0:width], left, rest[:, i, j, 0:width],
                                                ALU.subtract).then_inc(step_done, 1)
                        n += 1
                        dve.wait_ge(step_done, n)
                        left = rest[:, i, j, 0:width]
            dve.wait_ge(step_done, n)


def attention_phase(nc, sem, sh, x_in, adj_in, n_graphs):
    groups = n_graphs // GB
    with ExitStack() as ctx:
        def sb(name, shape, dt=F32):
            return ctx.enter_context(nc.sbuf_tensor(name, shape, dt))

        X, X1 = sh.X, sh.X1
        adj = [sb(f"a_adj{i}", [T, GB, T], I32) for i in range(2)]
        edge_bias = [sb(f"a_edge_bias{i}", [T, GB, T], BF16) for i in range(2)]
        stats = sb("a_stats", [T, GB, 6])
        meanvar = [sb(f"a_meanvar{i}", [T, GB, 2]) for i in range(2)]
        rstd = [sb(f"a_rstd{i}", [T, 5, GB]) for i in range(2)]
        n0 = sb("a_n0", [T, GB, D])
        nT = [sb(f"a_nT{i}", [D, W]) for i in range(2)]
        headT = [sb(f"a_headT{i}", [D, HEADS, 2 * T]) for i in range(2)]
        scaled = sb("a_scaled", [T, GB, D])
        V = [sb(f"a_V{i}", [T, GB, HEADS, HD + 1]) for i in range(2)]
        top = [sb(f"a_top{i}", [T, HEADS]) for i in range(2)]
        diff = [sb(f"a_diff{i}", [T, HEADS, T]) for i in range(2)]
        prob = [sb(f"a_prob{i}", [T, HEADS, T]) for i in range(2)]
        probT = [sb(f"a_probT{i}", [T, HEADS, T]) for i in range(2)]
        rsum = [sb(f"a_rsum{i}", [T, HEADS]) for i in range(2)]
        attn = [sb(f"a_attn{i}", [T, HEADS, HD]) for i in range(2)]
        ps_s = [ctx.enter_context(nc.psum_tensor(f"a_ps_s{i}", [T, HEADS, T], F32)) for i in range(2)]
        ps_p = ctx.enter_context(nc.psum_tensor("a_ps_p", [T, HEADS, T], F32))
        ps_n = ctx.enter_context(nc.psum_tensor("a_ps_n", [D, W], F32))
        ps_o = ctx.enter_context(nc.psum_tensor("a_ps_o", [T, HEADS, HD + 1], F32))

        x_loaded = [sem(f"a_x_loaded{i}") for i in range(2)]
        adj_loaded = [sem(f"a_adj_loaded{i}") for i in range(2)]
        stats_done = sem("a_stats_done")
        meanvar_done = sem("a_meanvar_done")
        rstd_step = sem("a_rstd_step")
        rstd_done = sem("a_rstd_done")
        n0_done = sem("a_n0_done")
        bias_done = sem("a_edge_bias_done")
        n_turned = sem("a_n_turned")
        nT_done = sem("a_nT_done")
        headT_done = sem("a_headT_done")
        scaled_done = sem("a_scaled_done")
        V_done = sem("a_V_done")
        scores_done = sem("a_scores_done")
        top_done = sem("a_top_done")
        diff_done = sem("a_diff_done")
        prob_done = sem("a_prob_done")
        prob_turned = sem("a_prob_turned")
        probT_done = sem("a_probT_done")
        pv_done = sem("a_pv_done")
        rsum_done = sem("a_rsum_done")
        attn_done = sem("a_attn_done")
        added = sem("a_added")
        ones_set = sem("a_ones_set")

        block = ctx.enter_context(nc.Block())
        x_g = x_in.rearrange("(g b) n d -> g n b d", b=GB)
        adj_g = adj_in.rearrange("(g b) n d -> g n b d", b=GB)
        LAG, PEEL = 3, 4

        @block.sync
        def _(sp):
            def step(t, r, p, known):
                if live(known, 0, groups):
                    if since(known, 2):
                        sp.wait_ge(bias_done, t - 1)
                        sp.wait_ge(stats_done, t - 1)
                    sp.dma_start(X[:, bass.ds(t * GB, GB), :], x_g[t]).then_inc(x_loaded[p], 16)
                    sp.dma_start(adj[p][:, :, :], adj_g[t]).then_inc(adj_loaded[p], 16)
            run_steps(sp, step, groups, 0, PEEL)

        @block.gpsimd
        def _(pool):
            nc.gpsimd.memset(V[0][:, :, :, HD:HD + 1], 1.0)
            nc.gpsimd.memset(V[1][:, :, :, HD:HD + 1], 1.0).then_inc(ones_set, 1)

            def step(t, r, p, known):
                if live(known, 1, groups):
                    g = t - 1
                    pool.wait_ge(n0_done, t)
                    nc.gpsimd.tensor_tensor(scaled[:, :, :], n0[:, :, :],
                                            sh.g1all[:, :].unsqueeze(1).to_broadcast([T, GB, D]),
                                            ALU.mult).then_inc(scaled_done, 1)
                    pool.wait_ge(scaled_done, t)
                    if since(known, 3):
                        pool.wait_ge(pv_done, g * 4 - 4)
                    for b in range(GB):
                        last = nc.gpsimd.tensor_tensor(
                            V[1 - p][:, b, :, 0:HD], scaled[:, b, :].rearrange("p (h d) -> p h d", d=HD),
                            sh.b1all[:, :].rearrange("p (h d) -> p h d", d=HD), ALU.add)
                    last.then_inc(V_done, 1)
                for b in range(GB):
                    if live(None if known is None else (known - 2) * GB + b, 3, n_graphs):
                        k = (t - 2) * GB + b
                        pool.wait_ge(attn_done, k - 2)
                        at = X1[:, bass.ds(k - 3, 1), :].rearrange("p b (h d) -> p (b h) d", d=HD)
                        nc.gpsimd.tensor_tensor(at, at, attn[(b + 1) % 2][:, :, :], ALU.add).then_inc(added, 1)
                    if b % 2 == 1 and live(known, 1, groups):
                        half = b // 2
                        pool.wait_ge(nT_done, t)
                        if since(known, 2):
                            pool.wait_ge(scores_done, (t - 2) * GB + 2 * half + 2)
                        src = nT[1 - p][:, half * 2 * T:(half + 1) * 2 * T]
                        nc.gpsimd.tensor_tensor(headT[half][:, 0, :], src,
                                                sh.headmask[:, 0:1].to_broadcast([D, 2 * T]), ALU.mult)
                        for h in range(1, HEADS):
                            last = nc.gpsimd.tensor_scalar(headT[half][:, h, :], src, sh.headmask[:, h:h + 1], 1.0,
                                                           ALU.mult, ALU.mult)
                        last.then_inc(headT_done, 1)
                    if b == 2 and live(known, 0, groups):
                        q = rstd[p]
                        pool.wait_ge(meanvar_done, t + 1)
                        if since(known, 2):
                            pool.wait_ge(n0_done, t - 1)
                        var = meanvar[p][:, :, 1]
                        nc.gpsimd.tensor_tensor(q[:, 2, :], var, sh.eps[:, 0:GB], ALU.add).then_inc(rstd_step, 1)
                        pool.wait_ge(rstd_step, t * 6 + 1)
                        nc.gpsimd.tensor_tensor(q[:, 0, :], q[:, 2, :], sh.half_power[:, 0:GB], ALU.pow).then_inc(rstd_step, 1)
                        pool.wait_ge(rstd_step, t * 6 + 2)
                        nc.gpsimd.tensor_tensor(q[:, 3, :], var, q[:, 0, :], ALU.mult).then_inc(rstd_step, 1)
                        pool.wait_ge(rstd_step, t * 6 + 3)
                        nc.gpsimd.tensor_tensor(q[:, 4, :], q[:, 3, :], q[:, 0, :], ALU.mult).then_inc(rstd_step, 1)
                        pool.wait_ge(rstd_step, t * 6 + 4)
                        nc.gpsimd.tensor_tensor(q[:, 2, :], q[:, 4, :], sh.eps[:, 0:GB], ALU.add).then_inc(rstd_step, 1)
                        pool.wait_ge(rstd_step, t * 6 + 5)
                        nc.gpsimd.tensor_tensor(q[:, 3, :], q[:, 2, :], sh.half_power[:, 0:GB], ALU.pow).then_inc(rstd_step, 1)
                        pool.wait_ge(rstd_step, t * 6 + 6)
                        nc.gpsimd.tensor_tensor(q[:, 1, :], q[:, 3, :], q[:, 0, :], ALU.mult).then_inc(rstd_done, 1)
            run_steps(pool, step, groups, LAG, PEEL)

        @block.scalar
        def _(act):
            def step(t, r, p, known):
                for b in range(GB):
                    kk = None if known is None else (known - 2) * GB + b
                    k = (t - 2) * GB + b
                    if live(kk, 0, n_graphs):
                        act.wait_ge(diff_done, k + 1)
                        if since(kk, 2):
                            act.wait_ge(prob_turned, k - 1)
                        nc.scalar.activation(prob[b % 2][:, :, :], diff[b % 2][:, :, :], ACT.Exp,
                                             scale=float(HD) ** -0.5).then_inc(prob_done, 1)
                    if b == 0 and live(known, 1, groups):
                        act.wait_ge(n_turned, t)
                        if since(known, 3):
                            act.wait_ge(scores_done, (t - 3) * GB + GB)
                            act.wait_ge(headT_done, (t - 2) * 2)
                        nc.scalar.activation(nT[1 - p][:, :], ps_n[:, :], ACT.Identity, bias=sh.b1col[:, 0:1],
                                             scale=sh.g1col[:, 0:1]).then_inc(nT_done, 1)
                    if live(kk, 1, n_graphs):
                        act.wait_ge(prob_turned, k)
                        if since(kk, 3):
                            act.wait_ge(pv_done, k - 2)
                        for c in range(2):
                            last = nc.scalar.activation(probT[(b + 1) % 2][:, 4 * c:4 * c + 4, :],
                                                        ps_p[:, 4 * c:4 * c + 4, :], ACT.Copy)
                        last.then_inc(probT_done, 1)
            run_steps(act, step, groups, LAG, PEEL)

        @block.tensor
        def _(pe):
            pe.wait_ge(ones_set, 1)

            def step(t, r, p, known):
                for b in range(GB):
                    kk = None if known is None else (known - 2) * GB + b
                    k = (t - 2) * GB + b
                    half = b // 2
                    if live(kk, 0, n_graphs):
                        if b == 0:
                            pe.wait_ge(bias_done, t - 1)
                        if b % 2 == 0:
                            pe.wait_ge(headT_done, (t - 2) * 2 + half + 1)
                        if since(kk, 2):
                            pe.wait_ge(diff_done, k - 1)
                        S = ps_s[b % 2]
                        for c in range(2):
                            nc.tensor.matmul(S[:, 4 * c:4 * c + 4, :], sh.ident_bf[:, :],
                                             edge_bias[p][:, b:b + 1, :].to_broadcast([T, 4, T]),
                                             start=True, stop=False)
                            for h in range(4 * c, 4 * c + 4):
                                last = nc.tensor.matmul(S[:, h, :], nT[p][:, b * T:(b + 1) * T],
                                                        headT[half][:, h, (b % 2) * T:(b % 2 + 1) * T],
                                                        start=False, stop=(h == 4 * c + 3))
                        last.then_inc(scores_done, 1)
                    if b == 1 and live(known, 1, groups):
                        pe.wait_ge(n0_done, t)
                        if since(known, 2):
                            pe.wait_ge(nT_done, t - 1)
                        for i in range(GB):
                            last = nc.tensor.transpose(ps_n[:, i * T:(i + 1) * T], n0[:, i, :], sh.ident[:, :])
                        last.then_inc(n_turned, 1)
                    if live(kk, 1, n_graphs):
                        pe.wait_ge(prob_done, k)
                        if since(kk, 2):
                            pe.wait_ge(probT_done, k - 1)
                        for h in range(HEADS):
                            last = nc.tensor.transpose(ps_p[:, h, :], prob[(b + 1) % 2][:, h, :], sh.ident[:, :])
                        last.then_inc(prob_turned, 1)
                    if live(kk, 2, n_graphs):
                        pe.wait_ge(probT_done, k - 1)
                        pe.wait_ge(V_done, t - 1 if b >= 2 else t - 2)
                        if since(kk, 3):
                            pe.wait_ge(attn_done, k - 2)
                        own = V[p] if b >= 2 else V[1 - p]
                        for h in range(HEADS):
                            last = nc.tensor.matmul(ps_o[:, h, :], probT[b % 2][:, h, :],
                                                    own[:, (b + 2) % GB, h, :], start=True, stop=True)
                        last.then_inc(pv_done, 1)
            run_steps(pe, step, groups, LAG, PEEL)

        @block.vector
        def _(dve):
            def step(t, r, p, known):
                if live(known, 1, groups):
                    dve.wait_ge(rstd_done, t)
                    if since(known, 2):
                        dve.wait_ge(n_turned, t - 1)
                        dve.wait_ge(scaled_done, t - 1)
                    for b in range(GB):
                        at = X[:, bass.ds((t - 1) * GB + b, 1), :].squeeze(1)
                        nc.vector.tensor_scalar(n0[:, b, :], at, meanvar[1 - p][:, b, 0:1],
                                                rstd[1 - p][:, 1, b:b + 1], ALU.subtract, ALU.mult)
                        last = nc.vector.tensor_scalar(X1[:, bass.ds((t - 1) * GB + b, 1), :].squeeze(1), at,
                                                       meanvar[1 - p][:, b, 0:1], rstd[1 - p][:, 0, b:b + 1],
                                                       ALU.subtract, ALU.mult)
                    last.then_inc(n0_done, 1)
                for b in range(GB):
                    kk = None if known is None else (known - 2) * GB + b
                    k = (t - 2) * GB + b
                    if b == 2 and live(known, 0, groups):
                        dve.wait_ge(stats_done, t + 1)
                    if live(kk, 3, n_graphs):
                        q = (b + 1) % 2
                        dve.wait_ge(pv_done, k - 2)
                        nc.vector.reciprocal(rsum[q][:, :], ps_o[:, :, HD]).then_inc(rsum_done, 1)
                        dve.wait_ge(rsum_done, k - 2)
                        if since(kk, 5):
                            dve.wait_ge(added, k - 4)
                        nc.vector.tensor_tensor(attn[q][:, :, :], ps_o[:, :, 0:HD],
                                                rsum[q][:, :].unsqueeze(2).to_broadcast([T, HEADS, HD]),
                                                ALU.mult).then_inc(attn_done, 1)
                    if live(kk, 0, n_graphs):
                        dve.wait_ge(scores_done, k + 1)
                        nc.vector.reduce_max(top[b % 2][:, :], ps_s[b % 2][:, :, :], AX.X).then_inc(top_done, 1)
                        dve.wait_ge(top_done, k + 1)
                        if since(kk, 2):
                            dve.wait_ge(prob_done, k - 1)
                        nc.vector.tensor_tensor(diff[b % 2][:, :, :], ps_s[b % 2][:, :, :],
                                                top[b % 2][:, :].unsqueeze(2).to_broadcast([T, HEADS, T]),
                                                ALU.subtract).then_inc(diff_done, 1)
                    if b == 1 and live(known, 0, groups):
                        dve.wait_ge(x_loaded[p], (r + 1) * 16)
                        for i in range(GB):
                            last = nc.vector.bn_stats(stats[:, i, :], X[:, bass.ds(t * GB + i, 1), :].squeeze(1))
                        last.then_inc(stats_done, 1)
                    if b == 2 and live(known, 0, groups):
                        for i in range(GB):
                            last = nc.vector.bn_aggr(meanvar[p][:, i, :], stats[:, i, :])
                        last.then_inc(meanvar_done, 1)
                if live(known, 0, groups):
                    dve.wait_ge(adj_loaded[p], (r + 1) * 16)
                    if since(known, 2):
                        dve.wait_ge(scores_done, (t - 1) * GB)
                    nc.vector.tensor_scalar(edge_bias[p][:, :, :], adj[p][:, :, :], 0.0, MASKED,
                                            ALU.is_le, ALU.mult).then_inc(bias_done, 1)
            run_steps(dve, step, groups, LAG, PEEL)


def mlp_phase(nc, sem, sh, w, n_graphs):
    groups = n_graphs // GB
    with ExitStack() as ctx:
        def sb(name, shape, dt=F32):
            return ctx.enter_context(nc.sbuf_tensor(name, shape, dt))

        X, X1 = sh.X, sh.X1
        w1 = sb("m_w1", [D, FF])
        w2 = sb("m_w2", [128, FC, D])
        b1 = sb("m_b1", [128, FC])
        b2all = sb("m_b2all", [T, D])
        stats = sb("m_stats", [T, GB, 6])
        meanvar = [sb(f"m_meanvar{i}", [T, GB, 2]) for i in range(2)]
        rstd = [sb(f"m_rstd{i}", [T, 2, GB]) for i in range(2)]
        n1 = sb("m_n1", [T, GB, D])
        yT = [sb(f"m_yT{i}", [D, W]) for i in range(2)]
        hidden = [sb(f"m_hidden{i}", [128, FC, W]) for i in range(2)]
        total = sb("m_total", [T, GB, D])
        ps_n = ctx.enter_context(nc.psum_tensor("m_ps_n", [D, W], F32))
        ps_1 = [ctx.enter_context(nc.psum_tensor(f"m_ps_1{i}", [128, W], F32)) for i in range(2)]
        ps_2 = [ctx.enter_context(nc.psum_tensor(f"m_ps_2{i}", [T, GB, D], F32)) for i in range(2)]

        w_loaded = sem("m_w_loaded")
        stats_done = sem("m_stats_done")
        meanvar_done = sem("m_meanvar_done")
        eps_added = sem("m_eps_added")
        rstd_done = sem("m_rstd_done")
        n_done = sem("m_n_done")
        n_turned = sem("m_n_turned")
        yT_done = sem("m_yT_done")
        up_done = sem("m_up_done")
        hidden_done = sem("m_hidden_done")
        down_done = sem("m_down_done")
        bias_added = sem("m_bias_added")
        total_done = sem("m_total_done")
        x_done = sem("m_x_done")

        block = ctx.enter_context(nc.Block())
        LAG, PEEL = 3, 4

        @block.sync
        def _(sp):
            sp.dma_start(w1[:, :], w["W1"]).then_inc(w_loaded, 16)
            sp.dma_start(w2[:, :, :], w["W2"].rearrange("(c p) n -> p c n", p=128)).then_inc(w_loaded, 16)
            sp.dma_start(b1[:, :], w["b1"].rearrange("(c p) -> p c", p=128),
                         allow_slow_non_contiguous=True).then_inc(w_loaded, 16)
            sp.dma_start(b2all[:, :], w["b2"].rearrange("(a n) -> a n", a=1).to_broadcast([T, D]))\
              .then_inc(w_loaded, 16)

        @block.gpsimd
        def _(pool):
            pool.wait_ge(w_loaded, 64)

            def step(t, r, p, known):
                if live(known, 0, groups):
                    at = X[:, bass.ds(t * GB, GB), :]
                    nc.gpsimd.tensor_tensor(at, at, b2all[:, :].unsqueeze(1).to_broadcast([T, GB, D]),
                                            ALU.add).then_inc(bias_added, 1)
                    pool.wait_ge(meanvar_done, t + 1)
                    if since(known, 2):
                        pool.wait_ge(n_done, t - 1)
                    nc.gpsimd.tensor_tensor(rstd[p][:, 1, :], meanvar[p][:, :, 1], sh.eps[:, 0:GB],
                                            ALU.add).then_inc(eps_added, 1)
                    pool.wait_ge(eps_added, t + 1)
                    nc.gpsimd.tensor_tensor(rstd[p][:, 0, :], rstd[p][:, 1, :], sh.half_power[:, 0:GB],
                                            ALU.pow).then_inc(rstd_done, 1)
            run_steps(pool, step, groups, 0, PEEL)

        @block.scalar
        def _(act):
            act.wait_ge(w_loaded, 64)

            def step(t, r, p, known):
                for c in range(FC):
                    if c == 2 and live(known, 1, groups):
                        act.wait_ge(n_turned, t)
                        if since(known, 3):
                            act.wait_ge(up_done, (t - 2) * FC)
                        nc.scalar.activation(yT[1 - p][:, :], ps_n[:, :], ACT.Identity, bias=sh.b2col[:, 0:1],
                                             scale=sh.g2col[:, 0:1]).then_inc(yT_done, 1)
                    if live(known, 2, groups):
                        act.wait_ge(up_done, (t - 2) * FC + c + 1)
                        if c == 0 and since(known, 4):
                            act.wait_ge(down_done, t - 3)
                        nc.scalar.activation(hidden[p][:, c, :], ps_1[c % 2][:, :], ACT.Gelu,
                                             bias=b1[:, c:c + 1]).then_inc(hidden_done, 1)
            run_steps(act, step, groups, LAG, PEEL)

        @block.tensor
        def _(pe):
            pe.wait_ge(w_loaded, 64)

            def step(t, r, p, known):
                for c in range(FC):
                    if live(known, 2, groups):
                        if c == 0:
                            pe.wait_ge(yT_done, t - 1)
                        if c >= 2 or since(known, 3):
                            pe.wait_ge(hidden_done, (t - 2) * FC + c - 1)
                        nc.tensor.matmul(ps_1[c % 2][:, :], w1[:, c * 128:(c + 1) * 128], yT[p][:, :],
                                         start=True, stop=True).then_inc(up_done, 1)
                    if c == 1 and live(known, 1, groups):
                        pe.wait_ge(n_done, t)
                        if since(known, 2):
                            pe.wait_ge(yT_done, t - 1)
                        for b in range(GB):
                            last = nc.tensor.transpose(ps_n[:, b * T:(b + 1) * T], n1[:, b, :], sh.ident[:, :])
                        last.then_inc(n_turned, 1)
                    if c % 2 == 1 and live(known, 3, groups):
                        if c == 1:
                            pe.wait_ge(hidden_done, (t - 2) * FC)
                            if since(known, 5):
                                pe.wait_ge(total_done, t - 4)
                        for b in (c - 1, c):
                            for f in range(FC):
                                last = nc.tensor.matmul(ps_2[1 - p][:, b, :], hidden[1 - p][:, f, b * T:(b + 1) * T],
                                                        w2[:, f, :], start=(f == 0), stop=(f == FC - 1))
                        if c == 3:
                            last.then_inc(down_done, 1)
            run_steps(pe, step, groups, LAG, PEEL)

        @block.vector
        def _(dve):
            def step(t, r, p, known):
                if live(known, 1, groups):
                    dve.wait_ge(rstd_done, t)
                    if since(known, 2):
                        dve.wait_ge(n_turned, t - 1)
                    for b in range(GB):
                        last = nc.vector.tensor_scalar(n1[:, b, :], X1[:, bass.ds((t - 1) * GB + b, 1), :].squeeze(1),
                                                       meanvar[1 - p][:, b, 0:1], rstd[1 - p][:, 0, b:b + 1],
                                                       ALU.subtract, ALU.mult)
                    last.then_inc(n_done, 1)
                if live(known, 0, groups):
                    for b in range(GB):
                        last = nc.vector.bn_stats(stats[:, b, :], X1[:, bass.ds(t * GB + b, 1), :].squeeze(1))
                    last.then_inc(stats_done, 1)
                    dve.wait_ge(stats_done, t + 1)
                if live(known, 3, groups):
                    dve.wait_ge(down_done, t - 2)
                    if since(known, 4):
                        dve.wait_ge(x_done, t - 3)
                    nc.vector.tensor_tensor(total[:, :, :], ps_2[1 - p][:, :, :],
                                            X1[:, bass.ds((t - 3) * GB, GB), :], ALU.add).then_inc(total_done, 1)
                if live(known, 0, groups):
                    for b in range(GB):
                        last = nc.vector.bn_aggr(meanvar[p][:, b, :], stats[:, b, :])
                    last.then_inc(meanvar_done, 1)
                if live(known, 3, groups):
                    dve.wait_ge(total_done, t - 2)
                    dve.wait_ge(bias_added, t - 2)
                    at = X[:, bass.ds((t - 3) * GB, GB), :]
                    nc.vector.tensor_tensor(at, at, total[:, :, :], ALU.add).then_inc(x_done, 1)
            run_steps(dve, step, groups, LAG, PEEL)


def slice_phase(nc, sem, sh, n_graphs):
    with ExitStack() as ctx:
        def sb(name, shape, dt=F32):
            return ctx.enter_context(nc.sbuf_tensor(name, shape, dt))

        def two(name, shape, dt=F32):
            return [sb(f"{name}{i}", shape, dt) for i in range(2)]

        def ps(name, shape):
            return ctx.enter_context(nc.psum_tensor(name, shape, F32))

        X = sh.X
        stats = sb("s_stats", [T, 6])
        meanvar = two("s_meanvar", [T, 2])
        rstd = two("s_rstd", [T, 2])
        z = sb("s_z", [T, D])
        zT = two("s_zT", [D, T])
        top = sb("s_top", [T, HEADS])
        diff = two("s_diff", [T, HEADS, C])
        expo = two("s_expo", [T, HEADS, C])
        rsum = two("s_rsum", [T, 2, HEADS])
        sw = two("s_sw", [T, HEADS, C])
        fx = two("s_fx", [T, HEADS, C + 1])
        swT = two("s_swT", [128, HP, T])
        rnorm = sb("s_rnorm", [128, 2, HP])
        tok = sb("s_tok", [128, HP, 128])
        tokT = two("s_tokT", [128, HP, 128])
        tokTc = sb("s_tokTc", [128, HP, C])
        key = sb("s_key", [128, HP, C])
        top2 = sb("s_top2", [128, HP])
        diff2 = two("s_diff2", [128, HP, C])
        att = sb("s_att", [128, HP, 128])
        rsum2 = two("s_rsum2", [128, 2, HP])
        attT = two("s_attT", [128, HP, 128])
        val = two("s_val", [128, HP, D])
        mixed = sb("s_mixed", [128, HP, D])
        ps_l, ps_f, ps_w = ps("s_ps_l", [T, HEADS, C]), ps("s_ps_f", [T, HEADS, C]), ps("s_ps_w", [128, HP, T])
        ps_t, ps_v = ps("s_ps_t", [128, HP, 128]), ps("s_ps_v", [128, HP, D])
        ps_a, ps_b, ps_u = ps("s_ps_a", [128, HP, C]), ps("s_ps_b", [128, 128]), ps("s_ps_u", [128, HP, C + 1])

        names = ("constants stats_done meanvar_done eps_added rstd_done z_done z_turned zT_done logits_done fx_done "
                 "fx_copied top_done diff_done expo_done sum_done rsum_done sw_done u_done norm_step rnorm_done "
                 "tok_done sw_turned swT_done tok_turned tokT_done tokTc_done keys_done key_copied scores_done "
                 "top2_done diff2_done att_done sum2_done rsum2_done att_turned attT_done val_done val_copied "
                 "mixed_done mixed_scaled out_done x_done").split()
        s = {n: sem(f"s_{n}") for n in names}
        block = ctx.enter_context(nc.Block())
        LAG, PEEL = 4, 6
        lo, hi = slice(0, C), slice(C, 128)

        @block.gpsimd
        def _(pool):
            nc.gpsimd.memset(tok[:, :, :], 0.0)
            nc.gpsimd.memset(att[:, :, :], 0.0)
            nc.gpsimd.memset(fx[0][:, :, C:C + 1], 1.0)
            nc.gpsimd.memset(fx[1][:, :, C:C + 1], 1.0).then_inc(s["constants"], 1)

            def step(t, r, p, known):
                if live(known, 2, n_graphs):
                    pool.wait_ge(s["rsum_done"], t - 1)
                    if since(known, 4):
                        pool.wait_ge(s["sw_turned"], t - 3)
                        pool.wait_ge(s["u_done"], t - 3)
                    nc.gpsimd.tensor_tensor(sw[p][:, :, :], expo[p][:, :, :],
                                            rsum[p][:, 1, :].unsqueeze(2).to_broadcast([T, HEADS, C]),
                                            ALU.mult).then_inc(s["sw_done"], 1)
                if live(known, 0, n_graphs):
                    pool.wait_ge(s["meanvar_done"], t + 1)
                    if since(known, 2):
                        pool.wait_ge(s["z_done"], t - 1)
                    nc.gpsimd.tensor_tensor(rstd[p][:, 1:2], meanvar[p][:, 1:2], sh.eps[:, 0:1],
                                            ALU.add).then_inc(s["eps_added"], 1)
                    pool.wait_ge(s["eps_added"], t + 1)
                    nc.gpsimd.tensor_tensor(rstd[p][:, 0:1], rstd[p][:, 1:2], sh.half_power[:, 0:1],
                                            ALU.pow).then_inc(s["rstd_done"], 1)
            run_steps(pool, step, n_graphs, 2, PEEL)

        @block.tensor
        def _(pe):
            pe.wait_ge(s["constants"], 1)

            def step(t, r, p, known):
                q = 1 - p
                if live(known, 4, n_graphs):
                    pe.wait_ge(s["attT_done"], t - 3)
                    pe.wait_ge(s["val_copied"], t - 3)
                    if since(known, 5):
                        pe.wait_ge(s["mixed_scaled"], t - 4)
                    for i in range(HP):
                        last = nc.tensor.matmul(ps_v[:, i, :], attT[p][:, i, :], val[p][:, i, :], start=True, stop=True)
                    last.then_inc(s["mixed_done"], 1)
                if live(known, 3, n_graphs):
                    pe.wait_ge(s["tok_done"], t - 2)
                    if since(known, 4):
                        pe.wait_ge(s["attT_done"], t - 3)
                    for i in range(HP):
                        last = nc.tensor.transpose(ps_t[:, i, :], tok[:, i, :], sh.ident[:, :])
                    last.then_inc(s["tok_turned"], 1)
                if live(known, 2, n_graphs):
                    pe.wait_ge(s["zT_done"], t - 1)
                    if since(known, 3):
                        pe.wait_ge(s["diff_done"], t - 2)
                    nc.tensor.matmul(ps_l[:, :, :], sh.ones_bf[:, :], sh.logit_bias[:, :], start=True, stop=False)
                    nc.tensor.matmul(ps_l[:, :, :], zT[p][:, :], sh.wlogit[:, :], start=False,
                                     stop=True).then_inc(s["logits_done"], 1)
                if live(known, 3, n_graphs):
                    pe.wait_ge(s["tokTc_done"], t - 2)
                    if since(known, 4):
                        pe.wait_ge(s["diff2_done"], t - 3)
                    nc.tensor.matmul(ps_a[:, :, :], sh.wscore[:, :], tokTc[:, :, :], start=True,
                                     stop=True).then_inc(s["keys_done"], 1)
                if live(known, 2, n_graphs):
                    if since(known, 3):
                        pe.wait_ge(s["fx_copied"], t - 2)
                    nc.tensor.matmul(ps_f[:, :, :], sh.ones_bf[:, :], sh.fx_bias[:, :], start=True, stop=False)
                    nc.tensor.matmul(ps_f[:, :, :], zT[p][:, :], sh.wfx[:, :], start=False,
                                     stop=True).then_inc(s["fx_done"], 1)
                if live(known, 3, n_graphs):
                    pe.wait_ge(s["key_copied"], t - 2)
                    for i in range(HP):
                        last = nc.tensor.matmul(ps_a[:, i, :], tokT[q][:, i, :], key[:, i, :], start=True, stop=True)
                    last.then_inc(s["scores_done"], 1)
                if live(known, 4, n_graphs):
                    pe.wait_ge(s["mixed_scaled"], t - 3)
                    pe.wait_ge(s["swT_done"], t - 3)
                    nc.tensor.matmul(ps_b[:, :], sh.ones_bf[:, :], sh.out_bias[:, :], start=True, stop=False)
                    for i in range(HP):
                        last = nc.tensor.matmul(ps_b[:, :], swT[p][:, i, :], mixed[:, i, :], start=False,
                                                stop=(i == HP - 1))
                    last.then_inc(s["out_done"], 1)
                if live(known, 3, n_graphs):
                    if since(known, 4):
                        pe.wait_ge(s["mixed_scaled"], t - 3)
                    for i in range(HP):
                        last = nc.tensor.matmul(ps_v[:, i, :], tokT[q][:, i, :], sh.wvalue[:, i, :], start=True, stop=True)
                    last.then_inc(s["val_done"], 1)
                if live(known, 3, n_graphs):
                    pe.wait_ge(s["att_done"], t - 2)
                    for i in range(HP):
                        last = nc.tensor.transpose(ps_t[:, i, :], att[:, i, :], sh.ident[:, :])
                    last.then_inc(s["att_turned"], 1)
                if live(known, 2, n_graphs):
                    pe.wait_ge(s["sw_done"], t - 1)
                    pe.wait_ge(s["fx_copied"], t - 1)
                    if since(known, 3):
                        pe.wait_ge(s["tok_done"], t - 2)
                        pe.wait_ge(s["swT_done"], t - 2)
                    for h in range(HEADS):
                        last = nc.tensor.matmul(ps_u[(h % 2) * C:(h % 2 + 1) * C, h // 2, :], sw[p][:, h, :],
                                                fx[p][:, h, :], start=True, stop=True)
                    last.then_inc(s["u_done"], 1)
                    for i in range(HP):
                        last = nc.tensor.transpose(ps_w[:, i, :], sw[p][:, 2 * i:2 * i + 2, :], sh.ident[:, :])
                    last.then_inc(s["sw_turned"], 1)
                if live(known, 1, n_graphs):
                    pe.wait_ge(s["z_done"], t)
                    if since(known, 4):
                        pe.wait_ge(s["x_done"], t - 3)
                    nc.tensor.transpose(ps_b[:, :], z[:, :], sh.ident[:, :]).then_inc(s["z_turned"], 1)
            run_steps(pe, step, n_graphs, LAG, PEEL)

        @block.scalar
        def _(act):
            def step(t, r, p, known):
                q = 1 - p
                if live(known, 3, n_graphs):
                    act.wait_ge(s["tok_turned"], t - 2)
                    if since(known, 5):
                        act.wait_ge(s["val_done"], t - 4)
                    nc.scalar.activation(tokT[q][:, :, :], ps_t[:, :, :], ACT.Copy).then_inc(s["tokT_done"], 1)
                    act.wait_ge(s["keys_done"], t - 2)
                    if since(known, 4):
                        act.wait_ge(s["scores_done"], t - 3)
                    nc.scalar.activation(key[:, :, :], ps_a[:, :, :], ACT.Copy).then_inc(s["key_copied"], 1)
                if live(known, 2, n_graphs):
                    act.wait_ge(s["diff_done"], t - 1)
                    if since(known, 4):
                        act.wait_ge(s["sw_done"], t - 3)
                    nc.scalar.activation(expo[p][:, :, :], diff[p][:, :, :], ACT.Exp).then_inc(s["expo_done"], 1)
                    act.wait_ge(s["fx_done"], t - 1)
                    if since(known, 4):
                        act.wait_ge(s["u_done"], t - 3)
                    nc.scalar.activation(fx[p][:, :, 0:C], ps_f[:, :, :], ACT.Copy).then_inc(s["fx_copied"], 1)
                if live(known, 3, n_graphs):
                    act.wait_ge(s["diff2_done"], t - 2)
                    if since(known, 4):
                        act.wait_ge(s["att_turned"], t - 3)
                    scale = float(C) ** -0.5
                    nc.scalar.activation(att[lo, :, lo], diff2[q][lo, :, :], ACT.Exp, scale=scale)
                    nc.scalar.activation(att[hi, :, hi], diff2[q][hi, :, :], ACT.Exp,
                                         scale=scale).then_inc(s["att_done"], 1)
                    act.wait_ge(s["val_done"], t - 2)
                    if since(known, 5):
                        act.wait_ge(s["mixed_done"], t - 4)
                    nc.scalar.activation(val[q][:, :, :], ps_v[:, :, :], ACT.Copy).then_inc(s["val_copied"], 1)
                    act.wait_ge(s["att_turned"], t - 2)
                    nc.scalar.activation(attT[q][:, :, :], ps_t[:, :, :], ACT.Copy).then_inc(s["attT_done"], 1)
                if live(known, 2, n_graphs):
                    act.wait_ge(s["sw_turned"], t - 1)
                    if since(known, 4):
                        act.wait_ge(s["out_done"], t - 3)
                    nc.scalar.activation(swT[p][:, :, :], ps_w[:, :, :], ACT.Copy).then_inc(s["swT_done"], 1)
                if live(known, 1, n_graphs):
                    act.wait_ge(s["z_turned"], t)
                    if since(known, 3):
                        act.wait_ge(s["fx_done"], t - 2)
                    nc.scalar.activation(zT[q][:, :], ps_b[:, :], ACT.Copy).then_inc(s["zT_done"], 1)
            run_steps(act, step, n_graphs, LAG, PEEL)

        @block.vector
        def _(dve):
            def step(t, r, p, known):
                q = 1 - p
                if live(known, 4, n_graphs):
                    dve.wait_ge(s["mixed_done"], t - 3)
                    dve.wait_ge(s["rsum2_done"], t - 3)
                    if since(known, 5):
                        dve.wait_ge(s["out_done"], t - 4)
                    nc.vector.tensor_tensor(mixed[:, :, :], ps_v[:, :, :],
                                            rsum2[p][:, 1, :].unsqueeze(2).to_broadcast([128, HP, D]),
                                            ALU.mult).then_inc(s["mixed_scaled"], 1)
                if live(known, 3, n_graphs):
                    dve.wait_ge(s["tokT_done"], t - 2)
                    if since(known, 4):
                        dve.wait_ge(s["keys_done"], t - 3)
                    nc.vector.tensor_tensor(tokTc[:, :, :], tokT[q][:, :, lo], tokT[q][:, :, hi],
                                            ALU.add).then_inc(s["tokTc_done"], 1)
                if live(known, 2, n_graphs):
                    dve.wait_ge(s["logits_done"], t - 1)
                    nc.vector.reduce_max(top[:, :], ps_l[:, :, :], AX.X).then_inc(s["top_done"], 1)
                    dve.wait_ge(s["top_done"], t - 1)
                    if since(known, 4):
                        dve.wait_ge(s["expo_done"], t - 3)
                    nc.vector.tensor_tensor(diff[p][:, :, :], ps_l[:, :, :],
                                            top[:, :].unsqueeze(2).to_broadcast([T, HEADS, C]),
                                            ALU.subtract).then_inc(s["diff_done"], 1)
                if live(known, 3, n_graphs):
                    dve.wait_ge(s["scores_done"], t - 2)
                    nc.vector.reduce_max(top2[:, :], ps_a[:, :, :], AX.X).then_inc(s["top2_done"], 1)
                    dve.wait_ge(s["top2_done"], t - 2)
                    if since(known, 5):
                        dve.wait_ge(s["att_done"], t - 4)
                    nc.vector.tensor_tensor(diff2[q][:, :, :], ps_a[:, :, :],
                                            top2[:, :].unsqueeze(2).to_broadcast([128, HP, C]),
                                            ALU.subtract).then_inc(s["diff2_done"], 1)
                if live(known, 2, n_graphs):
                    dve.wait_ge(s["expo_done"], t - 1)
                    if since(known, 4):
                        dve.wait_ge(s["sw_done"], t - 3)
                    nc.vector.reduce_sum(rsum[p][:, 0, :], expo[p][:, :, :], AX.X).then_inc(s["sum_done"], 1)
                    dve.wait_ge(s["sum_done"], t - 1)
                    nc.vector.reciprocal(rsum[p][:, 1, :], rsum[p][:, 0, :]).then_inc(s["rsum_done"], 1)
                if live(known, 4, n_graphs):
                    dve.wait_ge(s["out_done"], t - 3)
                    at = X[:, bass.ds(t - 4, 1), :].squeeze(1)
                    nc.vector.tensor_tensor(at, at, ps_b[:, :], ALU.add).then_inc(s["x_done"], 1)
                if live(known, 1, n_graphs):
                    dve.wait_ge(s["rstd_done"], t)
                    if since(known, 2):
                        dve.wait_ge(s["z_turned"], t - 1)
                    nc.vector.tensor_scalar(z[:, :], X[:, bass.ds(t - 1, 1), :].squeeze(1), meanvar[q][:, 0:1],
                                            rstd[q][:, 0:1], ALU.subtract, ALU.mult).then_inc(s["z_done"], 1)
                if live(known, 0, n_graphs):
                    nc.vector.bn_stats(stats[:, :], X[:, bass.ds(t, 1), :].squeeze(1)).then_inc(s["stats_done"], 1)
                if live(known, 3, n_graphs):
                    dve.wait_ge(s["att_done"], t - 2)
                    if since(known, 5):
                        dve.wait_ge(s["mixed_scaled"], t - 4)
                    if live(known, 0, n_graphs):
                        dve.wait_ge(s["stats_done"], t + 1)
                    nc.vector.reduce_sum(rsum2[q][:, 0, :], att[:, :, :], AX.X).then_inc(s["sum2_done"], 1)
                elif live(known, 0, n_graphs):
                    dve.wait_ge(s["stats_done"], t + 1)
                if live(known, 0, n_graphs):
                    nc.vector.bn_aggr(meanvar[p][:, :], stats[:, :]).then_inc(s["meanvar_done"], 1)
                if live(known, 3, n_graphs):
                    dve.wait_ge(s["sum2_done"], t - 2)
                    nc.vector.reciprocal(rsum2[q][:, 1, :], rsum2[q][:, 0, :]).then_inc(s["rsum2_done"], 1)
                if live(known, 2, n_graphs):
                    dve.wait_ge(s["u_done"], t - 1)
                    nc.vector.tensor_scalar(rnorm[:, 0, :], ps_u[:, :, C], EPS, None,
                                            ALU.add).then_inc(s["norm_step"], 1)
                    dve.wait_ge(s["norm_step"], t - 1)
                    nc.vector.reciprocal(rnorm[:, 1, :], rnorm[:, 0, :]).then_inc(s["rnorm_done"], 1)
                    dve.wait_ge(s["rnorm_done"], t - 1)
                    if since(known, 3):
                        dve.wait_ge(s["tok_turned"], t - 2)
                    for half in (lo, hi):
                        last = nc.vector.tensor_tensor(tok[half, :, half], ps_u[half, :, 0:C],
                                                       rnorm[half, 1, :].unsqueeze(2).to_broadcast([C, HP, C]),
                                                       ALU.mult)
                    last.then_inc(s["tok_done"], 1)
            run_steps(dve, step, n_graphs, LAG, PEEL)


def graph_phase(nc, sem, sh, adj_in, w, n_graphs):
    groups = n_graphs // GB
    with ExitStack() as ctx:
        def sb(name, shape, dt=F32):
            return ctx.enter_context(nc.sbuf_tensor(name, shape, dt))

        def two(name, shape, dt=F32):
            return [sb(f"{name}{i}", shape, dt) for i in range(2)]

        def ps(name, shape):
            return ctx.enter_context(nc.psum_tensor(name, shape, F32))

        X = sh.X
        wroot1, wrel1, wroot2, wrel2 = (sb(f"g_{n}", [D, D]) for n in ("wroot1", "wrel1", "wroot2", "wrel2"))
        b1 = sb("g_b1", [D, 1])
        adj = two("g_adj", [T, GB, T], I32)
        edge = two("g_edge", [T, GB, T], BF16)
        deg = sb("g_deg", [T, GB, T])
        rdeg = two("g_rdeg", [T, GB, T])
        mean = two("g_mean", [T, GB, T])
        stats = sb("g_stats", [T, GB, 6])
        meanvar = two("g_meanvar", [T, GB, 2])
        rstd = two("g_rstd", [T, 2, GB])
        z = two("g_z", [T, GB, D])
        zT, aggT = two("g_zT", [D, W]), two("g_aggT", [D, W])
        neg1, exp1, pos1 = sb("g_neg1", [D, W]), sb("g_exp1", [D, W]), sb("g_pos1", [D, W])
        hT = two("g_hT", [D, W])
        h = sb("g_h", [T, GB, D])
        agg2T = sb("g_agg2T", [D, W])
        neg2, exp2, pos2 = (sb(n, [T, GB, D]) for n in ("g_neg2", "g_exp2", "g_pos2"))
        elu2 = two("g_elu2", [T, GB, D])
        ps_z, ps_g, ps_h, ps_g2 = ps("g_ps_z", [D, W]), ps("g_ps_g", [D, W]), ps("g_ps_h", [T, GB, D]), ps("g_ps_g2", [D, W])
        ps_c, ps_d, ps_o = ps("g_ps_c", [D, W]), ps("g_ps_d", [T, GB, T]), ps("g_ps_o", [T, GB, D])

        names = ("w_loaded edge_done degree_summed deg_done rdeg_done mean_done stats_done meanvar_done eps_added "
                 "rstd_done z_done z_turned zT_done agg_done aggT_done conv1_done neg1_done exp1_done pos1_done "
                 "hT_done h_turned h_done agg2_done agg2T_done conv2_done neg2_done exp2_done pos2_done elu2_done "
                 "x_done").split()
        s = {n: sem(f"g_{n}") for n in names}
        adj_loaded = [sem(f"g_adj_loaded{i}") for i in range(2)]
        block = ctx.enter_context(nc.Block())
        adj_g = adj_in.rearrange("(g b) n d -> g n b d", b=GB)
        LAG, PEEL = 3, 4

        @block.sync
        def _(sp):
            for tile, a in ((wroot1, w["w_root1"]), (wrel1, w["w_rel1"][1]), (wroot2, w["w_root2"]),
                            (wrel2, w["w_rel2"][1]), (b1, w["b1"].rearrange("(p a) -> p a", a=1))):
                sp.dma_start(tile[:, :], a, allow_slow_non_contiguous=True).then_inc(s["w_loaded"], 16)

            def step(t, r, p, known):
                if since(known, 2):
                    sp.wait_ge(s["edge_done"], t - 1)
                sp.dma_start(adj[p][:, :, :], adj_g[t]).then_inc(adj_loaded[p], 16)
            run_steps(sp, step, groups, 0, PEEL)

        @block.gpsimd
        def _(pool):
            def step(t, r, p, known):
                if live(known, 0, groups):
                    pool.wait_ge(s["meanvar_done"], t + 1)
                    if since(known, 2):
                        pool.wait_ge(s["z_done"], t - 1)
                    nc.gpsimd.tensor_tensor(rstd[p][:, 1, :], meanvar[p][:, :, 1], sh.eps[:, 0:GB],
                                            ALU.add).then_inc(s["eps_added"], 1)
                    pool.wait_ge(s["eps_added"], t + 1)
                    nc.gpsimd.tensor_tensor(rstd[p][:, 0, :], rstd[p][:, 1, :], sh.half_power[:, 0:GB],
                                            ALU.pow).then_inc(s["rstd_done"], 1)
                    pool.wait_ge(s["rdeg_done"], t + 1)
                    if since(known, 2):
                        pool.wait_ge(s["agg2_done"], t - 1)
                    nc.gpsimd.tensor_tensor(mean[p][:, :, :], edge[p][:, :, :], rdeg[p][:, :, :],
                                            ALU.mult).then_inc(s["mean_done"], 1)
                if live(known, 3, groups):
                    pool.wait_ge(s["elu2_done"], t - 2)
                    at = X[:, bass.ds((t - 3) * GB, GB), :]
                    nc.gpsimd.tensor_tensor(at, at, elu2[1 - p][:, :, :], ALU.add).then_inc(s["x_done"], 1)
            run_steps(pool, step, groups, LAG, PEEL)

        @block.tensor
        def _(pe):
            pe.wait_ge(s["w_loaded"], 80)

            def step(t, r, p, known):
                q = 1 - p
                if live(known, 2, groups):
                    pe.wait_ge(s["hT_done"], t - 1)
                    if since(known, 3):
                        pe.wait_ge(s["h_done"], t - 2)
                    for b in range(GB):
                        last = nc.tensor.transpose(ps_h[:, b, :], hT[p][:, b * T:(b + 1) * T], sh.ident[:, :])
                    last.then_inc(s["h_turned"], 1)
                if live(known, 1, groups):
                    pe.wait_ge(s["z_done"], t)
                    if since(known, 2):
                        pe.wait_ge(s["zT_done"], t - 1)
                    for b in range(GB):
                        last = nc.tensor.transpose(ps_z[:, b * T:(b + 1) * T], z[q][:, b, :], sh.ident[:, :])
                    last.then_inc(s["z_turned"], 1)
                    pe.wait_ge(s["mean_done"], t)
                    if since(known, 2):
                        pe.wait_ge(s["aggT_done"], t - 1)
                    for b in range(GB):
                        last = nc.tensor.matmul(ps_g[:, b * T:(b + 1) * T], z[q][:, b, :], mean[q][:, b, :],
                                                start=True, stop=True)
                    last.then_inc(s["agg_done"], 1)
                if live(known, 2, groups):
                    pe.wait_ge(s["h_done"], t - 1)
                    if since(known, 3):
                        pe.wait_ge(s["agg2T_done"], t - 2)
                    for b in range(GB):
                        last = nc.tensor.matmul(ps_g2[:, b * T:(b + 1) * T], h[:, b, :], mean[p][:, b, :],
                                                start=True, stop=True)
                    last.then_inc(s["agg2_done"], 1)
                if live(known, 1, groups):
                    pe.wait_ge(s["zT_done"], t)
                    if since(known, 2):
                        pe.wait_ge(s["neg1_done"], t - 1)
                        pe.wait_ge(s["pos1_done"], t - 1)
                    nc.tensor.matmul(ps_c[:, :], wroot1[:, :], zT[q][:, :], start=True, stop=False)
                    pe.wait_ge(s["aggT_done"], t)
                    nc.tensor.matmul(ps_c[:, :], wrel1[:, :], aggT[q][:, :], start=False,
                                     stop=True).then_inc(s["conv1_done"], 1)
                if live(known, 0, groups):
                    pe.wait_ge(s["edge_done"], t + 1)
                    if since(known, 1):
                        pe.wait_ge(s["deg_done"], t)
                    nc.tensor.matmul(ps_d[:, :, :], sh.ones_bf[:, :], edge[p][:, :, :], start=True,
                                     stop=True).then_inc(s["degree_summed"], 1)
                if live(known, 2, groups):
                    pe.wait_ge(s["agg2T_done"], t - 1)
                    if since(known, 3):
                        pe.wait_ge(s["neg2_done"], t - 2)
                        pe.wait_ge(s["pos2_done"], t - 2)
                    nc.tensor.matmul(ps_o[:, :, :], sh.ones_bf[:, :],
                                     sh.conv2_bias[:, :].unsqueeze(1).to_broadcast([128, GB, D]), start=True,
                                     stop=False)
                    for b in range(GB):
                        nc.tensor.matmul(ps_o[:, b, :], hT[p][:, b * T:(b + 1) * T], wroot2[:, :], start=False,
                                         stop=False)
                        last = nc.tensor.matmul(ps_o[:, b, :], agg2T[:, b * T:(b + 1) * T], wrel2[:, :],
                                                start=False, stop=(b == GB - 1))
                    last.then_inc(s["conv2_done"], 1)
            run_steps(pe, step, groups, LAG, PEEL)

        @block.scalar
        def _(act):
            act.wait_ge(s["w_loaded"], 80)

            def step(t, r, p, known):
                q = 1 - p
                if live(known, 2, groups):
                    act.wait_ge(s["h_turned"], t - 1)
                    if since(known, 3):
                        act.wait_ge(s["agg2_done"], t - 2)
                    nc.scalar.activation(h[:, :, :], ps_h[:, :, :], ACT.Copy).then_inc(s["h_done"], 1)
                if live(known, 1, groups):
                    act.wait_ge(s["z_turned"], t)
                    if since(known, 3):
                        act.wait_ge(s["conv1_done"], t - 2)
                    nc.scalar.activation(zT[q][:, :], ps_z[:, :], ACT.Copy).then_inc(s["zT_done"], 1)
                    act.wait_ge(s["agg_done"], t)
                    nc.scalar.activation(aggT[q][:, :], ps_g[:, :], ACT.Copy).then_inc(s["aggT_done"], 1)
                if live(known, 2, groups):
                    act.wait_ge(s["agg2_done"], t - 1)
                    if since(known, 3):
                        act.wait_ge(s["conv2_done"], t - 2)
                    nc.scalar.activation(agg2T[:, :], ps_g2[:, :], ACT.Copy).then_inc(s["agg2T_done"], 1)
                if live(known, 1, groups):
                    act.wait_ge(s["neg1_done"], t)
                    if since(known, 2):
                        act.wait_ge(s["hT_done"], t - 1)
                    nc.scalar.activation(pos1[:, :], ps_c[:, :], ACT.Relu, bias=b1[:, 0:1]).then_inc(s["pos1_done"], 1)
                    nc.scalar.activation(exp1[:, :], neg1[:, :], ACT.Exp).then_inc(s["exp1_done"], 1)
                if live(known, 2, groups):
                    act.wait_ge(s["neg2_done"], t - 1)
                    if since(known, 3):
                        act.wait_ge(s["elu2_done"], t - 2)
                    nc.scalar.activation(pos2[:, :, :], ps_o[:, :, :], ACT.Relu).then_inc(s["pos2_done"], 1)
                    nc.scalar.activation(exp2[:, :, :], neg2[:, :, :], ACT.Exp).then_inc(s["exp2_done"], 1)
            run_steps(act, step, groups, LAG, PEEL)

        @block.vector
        def _(dve):
            dve.wait_ge(s["w_loaded"], 80)

            def step(t, r, p, known):
                q = 1 - p
                if live(known, 1, groups):
                    dve.wait_ge(s["rstd_done"], t)
                    if since(known, 3):
                        dve.wait_ge(s["agg_done"], t - 2)
                        dve.wait_ge(s["z_turned"], t - 2)
                    for b in range(GB):
                        last = nc.vector.tensor_scalar(z[q][:, b, :], X[:, bass.ds((t - 1) * GB + b, 1), :].squeeze(1),
                                                       meanvar[q][:, b, 0:1], rstd[q][:, 0, b:b + 1],
                                                       ALU.subtract, ALU.mult)
                    last.then_inc(s["z_done"], 1)
                if live(known, 3, groups):
                    dve.wait_ge(s["exp2_done"], t - 2)
                    dve.wait_ge(s["pos2_done"], t - 2)
                    if since(known, 5):
                        dve.wait_ge(s["x_done"], t - 4)
                    nc.vector.scalar_tensor_tensor(out=elu2[q][:, :, :], in0=exp2[:, :, :], scalar=-1.0,
                                                   in1=pos2[:, :, :], op0=ALU.add, op1=ALU.add)\
                      .then_inc(s["elu2_done"], 1)
                if live(known, 0, groups):
                    dve.wait_ge(adj_loaded[p], (r + 1) * 16)
                    if since(known, 2):
                        dve.wait_ge(s["mean_done"], t - 1)
                        dve.wait_ge(s["degree_summed"], t - 1)
                    nc.vector.tensor_scalar(edge[p][:, :, :], adj[p][:, :, :], 1.0, None,
                                            ALU.is_equal).then_inc(s["edge_done"], 1)
                    for b in range(GB):
                        last = nc.vector.bn_stats(stats[:, b, :], X[:, bass.ds(t * GB + b, 1), :].squeeze(1))
                    last.then_inc(s["stats_done"], 1)
                if live(known, 1, groups):
                    dve.wait_ge(s["conv1_done"], t)
                    if since(known, 2):
                        dve.wait_ge(s["exp1_done"], t - 1)
                    if live(known, 0, groups):
                        dve.wait_ge(s["stats_done"], t + 1)
                    nc.vector.tensor_scalar(neg1[:, :], ps_c[:, :], b1[:, 0:1], 0.0, ALU.add,
                                            ALU.min).then_inc(s["neg1_done"], 1)
                elif live(known, 0, groups):
                    dve.wait_ge(s["stats_done"], t + 1)
                if live(known, 0, groups):
                    for b in range(GB):
                        last = nc.vector.bn_aggr(meanvar[p][:, b, :], stats[:, b, :])
                    last.then_inc(s["meanvar_done"], 1)
                    dve.wait_ge(s["degree_summed"], t + 1)
                    nc.vector.tensor_scalar(deg[:, :, :], ps_d[:, :, :], 1.0, None,
                                            ALU.max).then_inc(s["deg_done"], 1)
                    dve.wait_ge(s["deg_done"], t + 1)
                    nc.vector.reciprocal(rdeg[p][:, :, :], deg[:, :, :]).then_inc(s["rdeg_done"], 1)
                if live(known, 1, groups):
                    dve.wait_ge(s["exp1_done"], t)
                    dve.wait_ge(s["pos1_done"], t)
                    if since(known, 3):
                        dve.wait_ge(s["conv2_done"], t - 2)
                        dve.wait_ge(s["h_turned"], t - 2)
                    nc.vector.scalar_tensor_tensor(out=hT[q][:, :], in0=exp1[:, :], scalar=-1.0, in1=pos1[:, :],
                                                   op0=ALU.add, op1=ALU.add).then_inc(s["hT_done"], 1)
                if live(known, 2, groups):
                    dve.wait_ge(s["conv2_done"], t - 1)
                    if since(known, 3):
                        dve.wait_ge(s["exp2_done"], t - 2)
                    nc.vector.tensor_scalar(neg2[:, :, :], ps_o[:, :, :], 0.0, None,
                                            ALU.min).then_inc(s["neg2_done"], 1)
            run_steps(dve, step, groups, LAG, PEEL)


def routing_sizes(n_tokens):
    capacity = n_tokens + W
    most = (2 * n_tokens + EXPERTS * (W - 1)) // W
    return capacity, most + most % 2


def router_phase(nc, sem, sh, w, n_graphs):
    groups = n_graphs // GB
    capacity, _ = routing_sizes(n_graphs * T)
    with ExitStack() as ctx:
        def sb(name, shape, dt=F32):
            return ctx.enter_context(nc.sbuf_tensor(name, shape, dt))

        def two(name, shape, dt=F32):
            return [sb(f"{name}{i}", shape, dt) for i in range(2)]

        def ps(name, shape):
            return ctx.enter_context(nc.psum_tensor(name, shape, F32))

        X = sh.X
        wr = sb("r_wr", [D, EXPERTS])
        before = sb("r_before", [T, T], BF16)
        number = sb("r_number", [T, EXPERTS])
        number_i = sb("r_number_i", [T, 2, EXPERTS], I32)
        region = sb("r_region", [T, EXPERTS])
        stats = sb("r_stats", [T, GB, 6])
        meanvar = two("r_meanvar", [T, GB, 2])
        rstd = two("r_rstd", [T, 2, GB])
        z = two("r_z", [T, GB, D])
        zT = sb("r_zT", [D, W])
        logits = sb("r_logits", [T, GB, EXPERTS])
        best = sb("r_best", [T, GB, EXPERTS])
        which = sb("r_which", [T, GB, EXPERTS], U32)
        which_f = sb("r_which_f", [T, 2, GB])
        chosen = sb("r_chosen", [T, 2, GB, EXPERTS])
        either = sb("r_either", [T, GB, EXPERTS], BF16)
        taken = sb("r_taken", [T, GB + 1, EXPERTS])
        place = sb("r_place", [T, 3, GB, EXPERTS])
        place_of = sb("r_place_of", [T, 2, GB, EXPERTS])
        rows_f = sb("r_rows_f", [T, 2, GB])
        rows = two("r_rows", [T, 2 * GB], U32)
        ps_z, ps_l, ps_k = ps("r_ps_z", [D, W]), ps("r_ps_l", [T, GB, EXPERTS]), ps("r_ps_k", [T, 2, GB, EXPERTS])

        names = ("w_loaded numbered before_set setup stats_done meanvar_done eps_added rstd_done z_done z_turned "
                 "zT_done logits_done copied carried best_done gap_done which_done whichf_done chosen_done "
                 "either_done ranked taken_step place_step placed_done rowsf_done rows_done kept").split()
        s = {n: sem(f"r_{n}") for n in names}
        scattered = [sem(f"r_scattered{i}") for i in range(2)]
        block = ctx.enter_context(nc.Block())
        LAG, PEEL = 2, 4

        @block.sync
        def _(sp):
            sp.dma_start(wr[:, :], w["Wr"]).then_inc(s["w_loaded"], 16)

        @block.gpsimd
        def _(pool):
            nc.gpsimd.iota(number_i[:, 0, :], pattern=[[1, EXPERTS]], base=0, channel_multiplier=0)
            nc.gpsimd.iota(number_i[:, 1, :], pattern=[[capacity // 8, EXPERTS]], base=0, channel_multiplier=0)\
              .then_inc(s["numbered"], 1)
            nc.gpsimd.memset(before[:, :], 1.0).then_inc(s["before_set"], 1)
            pool.wait_ge(s["before_set"], 1)
            nc.gpsimd.affine_select(out=before[:, :], in_=before[:, :], compare_op=ALU.is_ge, fill=0.0, base=-1,
                                    pattern=[[1, T]], channel_multiplier=-1).then_inc(s["before_set"], 1)

            def step(t, r, p, known):
                if live(known, 2, groups):
                    pool.wait_ge(s["rows_done"], t - 1)
                if live(known, 0, groups):
                    pool.wait_ge(s["meanvar_done"], t + 1)
                    if since(known, 2):
                        pool.wait_ge(s["z_done"], t - 1)
                    nc.gpsimd.tensor_tensor(rstd[p][:, 1, :], meanvar[p][:, :, 1], sh.eps[:, 0:GB],
                                            ALU.add).then_inc(s["eps_added"], 1)
                    pool.wait_ge(s["eps_added"], t + 1)
                    nc.gpsimd.tensor_tensor(rstd[p][:, 0, :], rstd[p][:, 1, :], sh.half_power[:, 0:GB],
                                            ALU.pow).then_inc(s["rstd_done"], 1)
                if live(known, 2, groups):
                    for e in range(2):
                        for b in range(GB):
                            nc.gpsimd.indirect_dma_start(
                                sh.sorted_z, bass.IndirectOffsetOnAxis(ap=rows[p][:, e * GB + b:e * GB + b + 1], axis=0),
                                z[p][:, b, :], None).then_inc(scattered[p], 16)
            run_steps(pool, step, groups, LAG, PEEL)
            for p in range(2):
                pool.wait_ge(scattered[p], groups // 2 * 2 * GB * 16)

        @block.scalar
        def _(act):
            def step(t, r, p, known):
                if live(known, 1, groups):
                    act.wait_ge(s["z_turned"], t)
                    if since(known, 2):
                        act.wait_ge(s["logits_done"], t - 1)
                    nc.scalar.activation(zT[:, :], ps_z[:, :], ACT.Copy).then_inc(s["zT_done"], 1)
            run_steps(act, step, groups, LAG, PEEL)

        @block.tensor
        def _(pe):
            pe.wait_ge(s["w_loaded"], 16)
            pe.wait_ge(s["before_set"], 2)

            def step(t, r, p, known):
                q = 1 - p
                if live(known, 1, groups):
                    pe.wait_ge(s["z_done"], t)
                    if since(known, 2):
                        pe.wait_ge(s["zT_done"], t - 1)
                    for b in range(GB):
                        last = nc.tensor.transpose(ps_z[:, b * T:(b + 1) * T], z[q][:, b, :], sh.ident[:, :])
                    last.then_inc(s["z_turned"], 1)
                    pe.wait_ge(s["zT_done"], t)
                    if since(known, 2):
                        pe.wait_ge(s["copied"], t - 1)
                    for b in range(GB):
                        last = nc.tensor.matmul(ps_l[:, b, :], zT[:, b * T:(b + 1) * T], wr[:, :],
                                                start=True, stop=True)
                    last.then_inc(s["logits_done"], 1)
                    pe.wait_ge(s["either_done"], t)
                    if since(known, 2):
                        pe.wait_ge(s["taken_step"], (t - 1) * GB)
                        pe.wait_ge(s["place_step"], (t - 1) * 2)
                    nc.tensor.matmul(ps_k[:, 0, :, :], before[:, :], either[:, :, :], start=True, stop=True)
                    nc.tensor.matmul(ps_k[:, 1, :, :], sh.ones_bf[:, :], either[:, :, :], start=True,
                                     stop=True).then_inc(s["ranked"], 1)
            run_steps(pe, step, groups, LAG, PEEL)

        @block.vector
        def _(dve):
            dve.wait_ge(s["numbered"], 1)
            nc.vector.tensor_copy(number[:, :], number_i[:, 0, :])
            nc.vector.tensor_scalar(region[:, :], number_i[:, 1, :], 8.0, None, ALU.mult)
            nc.vector.memset(taken[:, :, :], 0.0).then_inc(s["setup"], 1)
            dve.wait_ge(s["setup"], 1)

            def step(t, r, p, known):
                q = 1 - p
                g = t - 1
                if live(known, 0, groups):
                    if since(known, 1):
                        dve.wait_ge(s["meanvar_done"], t)
                    for b in range(GB):
                        last = nc.vector.bn_stats(stats[:, b, :], X[:, bass.ds(t * GB + b, 1), :].squeeze(1))
                    last.then_inc(s["stats_done"], 1)
                    dve.wait_ge(s["stats_done"], t + 1)
                if live(known, 1, groups):
                    dve.wait_ge(s["rstd_done"], t)
                    if since(known, 3):
                        dve.wait_ge(scattered[q], (r + p - 1) * 2 * GB * 16)
                    for b in range(GB):
                        last = nc.vector.tensor_scalar(z[q][:, b, :], X[:, bass.ds(g * GB + b, 1), :].squeeze(1),
                                                       meanvar[q][:, b, 0:1], rstd[q][:, 0, b:b + 1],
                                                       ALU.subtract, ALU.mult)
                    last.then_inc(s["z_done"], 1)
                if live(known, 0, groups):
                    for b in range(GB):
                        last = nc.vector.bn_aggr(meanvar[p][:, b, :], stats[:, b, :])
                    last.then_inc(s["meanvar_done"], 1)
                if live(known, 1, groups):
                    dve.wait_ge(s["logits_done"], t)
                    nc.vector.tensor_copy(logits[:, :, :], ps_l[:, :, :]).then_inc(s["copied"], 1)
                    dve.wait_ge(s["copied"], t)
                    nc.vector.tensor_copy(taken[:, 0, :], taken[:, GB, :]).then_inc(s["carried"], 1)
                    for b in range(GB):
                        last = nc.vector.max(best[:, b, :], logits[:, b, :])
                    last.then_inc(s["best_done"], 1)
                    dve.wait_ge(s["best_done"], t)
                    nc.vector.tensor_tensor(sh.gap[:, bass.ds(g * GB, GB)], best[:, :, 1], best[:, :, 0],
                                            ALU.subtract).then_inc(s["gap_done"], 1)
                    for b in range(GB):
                        last = nc.vector.max_index(which[:, b, :], best[:, b, :], logits[:, b, :])
                    last.then_inc(s["which_done"], 1)
                    dve.wait_ge(s["which_done"], t)
                    nc.vector.tensor_copy(which_f[:, :, :], which[:, :, 0:2].rearrange("p b e -> p e b"))\
                      .then_inc(s["whichf_done"], 1)
                    dve.wait_ge(s["whichf_done"], t)
                    nc.vector.tensor_copy(sh.expert_of[:, bass.ds(g, 1), :].squeeze(1),
                                          which_f[:, :, :].rearrange("p e b -> p (e b)"))
                    nc.vector.tensor_tensor(
                        chosen[:, :, :, :].rearrange("p e b x -> p (e b) x"),
                        which_f[:, :, :].rearrange("p e b -> p (e b)").unsqueeze(2).to_broadcast([T, 2 * GB, EXPERTS]),
                        number[:, :].unsqueeze(1).to_broadcast([T, 2 * GB, EXPERTS]),
                        ALU.is_equal).then_inc(s["chosen_done"], 1)
                    dve.wait_ge(s["chosen_done"], t)
                    nc.vector.tensor_tensor(either[:, :, :], chosen[:, 0, :, :], chosen[:, 1, :, :],
                                            ALU.add).then_inc(s["either_done"], 1)
                    dve.wait_ge(s["ranked"], t)
                    dve.wait_ge(s["carried"], t)
                    for b in range(GB):
                        if b:
                            dve.wait_ge(s["taken_step"], g * GB + b)
                        nc.vector.tensor_tensor(taken[:, b + 1, :], taken[:, b, :], ps_k[:, 1, b, :],
                                                ALU.add).then_inc(s["taken_step"], 1)
                    dve.wait_ge(s["taken_step"], t * GB)
                    nc.vector.tensor_tensor(place[:, 0, :, :], ps_k[:, 0, :, :], taken[:, 0:GB, :],
                                            ALU.add).then_inc(s["place_step"], 1)
                    dve.wait_ge(s["place_step"], g * 2 + 1)
                    nc.vector.tensor_tensor(place[:, 1, :, :], place[:, 0, :, :],
                                            region[:, :].unsqueeze(1).to_broadcast([T, GB, EXPERTS]),
                                            ALU.add).then_inc(s["place_step"], 1)
                    dve.wait_ge(s["place_step"], g * 2 + 2)
                    nc.vector.tensor_tensor(place_of[:, 0, :, :], chosen[:, 0, :, :], place[:, 1, :, :], ALU.mult)
                    nc.vector.tensor_tensor(place_of[:, 1, :, :], chosen[:, 1, :, :], place[:, 1, :, :],
                                            ALU.mult).then_inc(s["placed_done"], 1)
                    dve.wait_ge(s["placed_done"], t)
                    nc.vector.reduce_sum(rows_f[:, :, :].rearrange("p e b -> p (e b)"),
                                         place_of[:, :, :, :].rearrange("p e b x -> p (e b) x"),
                                         AX.X).then_inc(s["rowsf_done"], 1)
                    dve.wait_ge(s["rowsf_done"], t)
                    nc.vector.tensor_copy(sh.row_of[:, bass.ds(g, 1), :].squeeze(1),
                                          rows_f[:, :, :].rearrange("p e b -> p (e b)")).then_inc(s["kept"], 1)
                    nc.vector.tensor_copy(rows[q][:, :],
                                          rows_f[:, :, :].rearrange("p e b -> p (e b)")).then_inc(s["rows_done"], 1)
            run_steps(dve, step, groups, LAG, PEEL)
            dve.wait_ge(s["kept"], groups)
            nc.vector.tensor_copy(sh.counts[:, :], taken[:, GB, :]).then_inc(s["setup"], 1)
            dve.wait_ge(s["setup"], 2)


def schedule_phase(nc, sem, sh, n_graphs):
    capacity, n_groups = routing_sizes(n_graphs * T)
    spans = capacity // W
    E = EXPERTS
    with ExitStack() as ctx:
        def sb(name, shape, dt=F32):
            return ctx.enter_context(nc.sbuf_tensor(name, shape, dt))

        edges_i = sb("p_edges_i", [T, spans], I32)
        groups_i = sb("p_groups_i", [1, n_groups], I32)
        region_i = sb("p_region_i", [T, E], I32)
        edges, group = sb("p_edges", [T, spans]), sb("p_group", [1, n_groups])
        region = sb("p_region", [T, E])
        full = sb("p_full", [T, E, spans])
        size = sb("p_size", [T, E])
        end = sb("p_end", [T, E + 1])
        past = sb("p_past", [1, n_groups, E])
        mine = sb("p_mine", [1, n_groups, E])
        shift = sb("p_shift", [T, E])
        expert = sb("p_expert", [1, 2, n_groups])
        unused = sb("p_unused", [1, n_groups])
        base = sb("p_base", [1, 5, n_groups])
        back = sb("p_back", [T, 2, n_graphs // GB * 2 * GB])
        tail = sb("p_tail", [T, E])
        tail_i = sb("p_tail_i", [T, E], I32)
        zeros = sb("p_zeros", [T, GB * D])
        odds = sb("p_odds", [T, 2, n_graphs])

        numbered = sem("p_numbered")
        done = sem("p_done")
        tails_ready = sem("p_tails_ready")
        zero_set = sem("p_zero_set")
        odds_done = sem("p_odds_done")
        filled = sem("p_filled")
        block = ctx.enter_context(nc.Block())

        @block.gpsimd
        def _(pool):
            nc.gpsimd.iota(edges_i[:, :], pattern=[[W, spans]], base=0, channel_multiplier=0)
            nc.gpsimd.iota(groups_i[:, :], pattern=[[1, n_groups]], base=0, channel_multiplier=0)
            nc.gpsimd.iota(region_i[:, :], pattern=[[capacity // 8, E]], base=0, channel_multiplier=0)\
              .then_inc(numbered, 1)

        @block.scalar
        def _(act):
            nc.scalar.activation(odds[:, 0, :], sh.gap[:, :], ACT.Exp).then_inc(odds_done, 1)

        @block.vector
        def _(dve):
            n = [0]

            def after(ins):
                n[0] += 1
                ins.then_inc(done, 1)
                dve.wait_ge(done, n[0])

            nc.vector.memset(zeros[:, :], 0.0).then_inc(zero_set, 1)
            dve.wait_ge(numbered, 1)
            nc.vector.tensor_copy(edges[:, :], edges_i[:, :])
            nc.vector.tensor_copy(group[:, :], groups_i[:, :])
            after(nc.vector.tensor_scalar(region[:, :], region_i[:, :], 8.0, None, ALU.mult))
            after(nc.vector.tensor_tensor(tail[:, :], region[:, :], sh.counts[:, :], ALU.add))
            nc.vector.tensor_copy(tail_i[:, :], tail[:, :]).then_inc(tails_ready, 1)
            after(nc.vector.tensor_tensor(full[:, :, :], edges[:, :].unsqueeze(1).to_broadcast([T, E, spans]),
                                          sh.counts[:, :].unsqueeze(2).to_broadcast([T, E, spans]), ALU.is_lt))
            nc.vector.memset(end[:, :], 0.0)
            after(nc.vector.reduce_sum(size[:, :], full[:, :, :], AX.X))
            for e in range(E):
                after(nc.vector.tensor_tensor(end[:, e + 1:e + 2], end[:, e:e + 1], size[:, e:e + 1], ALU.add))
            groups_by = group[:, :].unsqueeze(2).to_broadcast([1, n_groups, E])
            after(nc.vector.tensor_tensor(past[:, :, :], end[0:1, 1:E + 1].unsqueeze(1).to_broadcast([1, n_groups, E]),
                                          groups_by, ALU.is_le))
            after(nc.vector.reduce_sum(expert[:, 0, :], past[:, :, :], AX.X))
            nc.vector.tensor_scalar(unused[:, :], expert[:, 0, :], float(E), None, ALU.is_ge)
            after(nc.vector.tensor_scalar(shift[:, :], end[:, 0:E], -float(W), None, ALU.mult))
            after(nc.vector.tensor_tensor(shift[:, :], shift[:, :], region[:, :], ALU.add))
            after(nc.vector.tensor_tensor(mine[:, :, :], end[0:1, 0:E].unsqueeze(1).to_broadcast([1, n_groups, E]),
                                          groups_by, ALU.is_le))
            after(nc.vector.tensor_tensor(mine[:, :, :], mine[:, :, :], past[:, :, :], ALU.subtract))
            after(nc.vector.tensor_tensor(mine[:, :, :], mine[:, :, :],
                                          shift[0:1, :].unsqueeze(1).to_broadcast([1, n_groups, E]), ALU.mult))
            after(nc.vector.reduce_sum(base[:, 0, :], mine[:, :, :], AX.X))
            after(nc.vector.tensor_scalar(base[:, 1, :], group[:, :], float(W), None, ALU.mult))
            after(nc.vector.tensor_tensor(base[:, 2, :], base[:, 0, :], base[:, 1, :], ALU.add))
            after(nc.vector.tensor_scalar(base[:, 3, :], unused[:, :], -1.0, 1.0, ALU.mult, ALU.add))
            after(nc.vector.tensor_tensor(base[:, 2, :], base[:, 2, :], base[:, 3, :], ALU.mult))
            after(nc.vector.scalar_tensor_tensor(out=base[:, 4, :], in0=unused[:, :], scalar=float(E * capacity),
                                                 in1=base[:, 2, :], op0=ALU.mult, op1=ALU.add))
            after(nc.vector.tensor_scalar(expert[:, 1, :], expert[:, 0, :], float(E - 1), None, ALU.min))
            nc.vector.tensor_copy(sh.plan[:, 0, :], expert[:, 1, :])
            after(nc.vector.tensor_copy(sh.plan[:, 1, :], base[:, 4, :]))
            experts_of = sh.expert_of[:, :, :].rearrange("p g i -> p (g i)")
            rows_of = sh.row_of[:, :, :].rearrange("p g i -> p (g i)")
            for e in range(E):
                after(nc.vector.tensor_scalar(back[:, e % 2, :], experts_of, float(e), shift[:, e:e + 1],
                                              ALU.is_equal, ALU.mult))
                after(nc.vector.tensor_tensor(rows_of, rows_of, back[:, e % 2, :], ALU.subtract))
            dve.wait_ge(odds_done, 1)
            after(nc.vector.tensor_scalar(odds[:, 1, :], odds[:, 0, :], 1.0, None, ALU.add))
            after(nc.vector.reciprocal(sh.gate[:, 0, :], odds[:, 1, :]))
            after(nc.vector.tensor_tensor(sh.gate[:, 1, :], odds[:, 0, :], sh.gate[:, 0, :], ALU.mult))

        @block.sync
        def _(sp):
            sp.wait_ge(zero_set, 1)
            rows = lambda start: sh.sorted_z[bass.ds(start, W), :].rearrange("(p b) d -> p (b d)", b=GB)
            sp.dma_start(rows(E * capacity), zeros[:, :]).then_inc(filled, 16)
            sp.wait_ge(tails_ready, 1)
            for e in range(E):
                start = nc.sync.value_load(tail_i[0:1, e:e + 1], min_val=0, max_val=E * capacity - W)
                sp.dma_start(rows(start), zeros[:, :]).then_inc(filled, 16)
            sp.wait_ge(filled, 16 * (E + 1))


def expert_phase(nc, sem, sh, w, n_graphs):
    capacity, n_groups = routing_sizes(n_graphs * T)
    with ExitStack() as ctx:
        def sb(name, shape, dt=F32):
            return ctx.enter_context(nc.sbuf_tensor(name, shape, dt))

        def two(name, shape, dt=F32):
            return [sb(f"{name}{i}", shape, dt) for i in range(2)]

        def ps(name, shape):
            return ctx.enter_context(nc.psum_tensor(name, shape, F32))

        w1 = sb("e_w1", [D, EXPERTS, FF])
        w2 = sb("e_w2", [128, EXPERTS, FC * D])
        b1 = sb("e_b1", [128, EXPERTS, FC])
        w1g, w2g, b1g = two("e_w1g", [D, FF]), two("e_w2g", [128, FC, D]), two("e_b1g", [128, FC])
        z = two("e_z", [T, GB, D])
        zT = two("e_zT", [D, W])
        hidden = two("e_hidden", [128, FC, W])
        y = two("e_y", [T, GB, D])
        ps_z = ps("e_ps_z", [D, W])
        ps_1 = [ps(f"e_ps_1{i}", [128, W]) for i in range(2)]
        ps_2 = [ps(f"e_ps_2{i}", [T, GB, D]) for i in range(2)]

        names = ("w_loaded w_picked w2_picked z_turned zT_done up_done hidden_done down_done y_done").split()
        s = {n: sem(f"e_{n}") for n in names}
        z_loaded = [sem(f"e_z_loaded{i}") for i in range(2)]
        y_stored = [sem(f"e_y_stored{i}") for i in range(2)]
        block = ctx.enter_context(nc.Block())
        LAG, PEEL = 4, 6

        def rows(tensor, start):
            return tensor[bass.ds(start, W), :].rearrange("(b p) d -> p b d", p=T)

        @block.sync
        def _(sp):
            for tile, a in ((w1[:, :, :], w["W1p"].rearrange("e d f -> d e f")),
                            (b1[:, :, :], w["b1p"].rearrange("e (c p) -> p e c", p=128))):
                sp.dma_start(tile, a, allow_slow_non_contiguous=True).then_inc(s["w_loaded"], 16)
            for c in range(FC):
                sp.dma_start(w2[:, :, c * D:(c + 1) * D], w["W2p"][:, c * 128:(c + 1) * 128, :]
                             .rearrange("e p d -> p e d")).then_inc(s["w_loaded"], 16)

            def step(t, r, p, known):
                if live(known, 0, n_groups):
                    start = nc.sync.value_load(sh.plan[0:1, 1, bass.ds(t, 1)], min_val=0, max_val=EXPERTS * capacity)
                    if since(known, 2):
                        sp.wait_ge(s["z_turned"], t - 1)
                    sp.dma_start(z[p][:, :, :], rows(sh.sorted_z, start)).then_inc(z_loaded[p], 16)
                if live(known, 4, n_groups):
                    sp.wait_ge(s["y_done"], t - 3)
                    sp.dma_start(rows(sh.sorted_y, (t - 4) * W), y[p][:, :, :]).then_inc(y_stored[p], 16)
            run_steps(sp, step, n_groups, LAG, PEEL)
            for p in range(2):
                sp.wait_ge(y_stored[p], n_groups // 2 * 16)

        @block.gpsimd
        def _(pool):
            pool.wait_ge(s["w_loaded"], 96)

            def step(t, r, p, known):
                q = 1 - p
                if live(known, 1, n_groups):
                    e = nc.gpsimd.value_load(sh.plan[0:1, 0, bass.ds(t - 1, 1)], min_val=0, max_val=EXPERTS - 1)
                    if since(known, 3):
                        pool.wait_ge(s["up_done"], (t - 2) * FC)
                        pool.wait_ge(s["hidden_done"], (t - 2) * FC)
                    nc.gpsimd.tensor_copy(w1g[q][:, :], w1[:, bass.ds(e, 1), :].squeeze(1))
                    nc.gpsimd.tensor_copy(b1g[q][:, :], b1[:, bass.ds(e, 1), :].squeeze(1)).then_inc(s["w_picked"], 1)
                if live(known, 2, n_groups):
                    e = nc.gpsimd.value_load(sh.plan[0:1, 0, bass.ds(t - 2, 1)], min_val=0, max_val=EXPERTS - 1)
                    if since(known, 4):
                        pool.wait_ge(s["down_done"], t - 3)
                    nc.gpsimd.tensor_copy(w2g[p][:, :, :].rearrange("p c d -> p (c d)"),
                                          w2[:, bass.ds(e, 1), :].squeeze(1)).then_inc(s["w2_picked"], 1)
            run_steps(pool, step, n_groups, LAG, PEEL)

        @block.scalar
        def _(act):
            def step(t, r, p, known):
                for c in range(FC):
                    if c == 2 and live(known, 1, n_groups):
                        act.wait_ge(s["z_turned"], t)
                        if since(known, 3):
                            act.wait_ge(s["up_done"], (t - 2) * FC)
                        nc.scalar.activation(zT[1 - p][:, :], ps_z[:, :], ACT.Copy).then_inc(s["zT_done"], 1)
                    if live(known, 2, n_groups):
                        act.wait_ge(s["up_done"], (t - 2) * FC + c + 1)
                        if c == 0 and since(known, 4):
                            act.wait_ge(s["down_done"], t - 3)
                        nc.scalar.activation(hidden[p][:, c, :], ps_1[c % 2][:, :], ACT.Gelu,
                                             bias=b1g[p][:, c:c + 1]).then_inc(s["hidden_done"], 1)
            run_steps(act, step, n_groups, LAG, PEEL)

        @block.tensor
        def _(pe):
            def step(t, r, p, known):
                q = 1 - p
                for c in range(FC):
                    if live(known, 2, n_groups):
                        if c == 0:
                            pe.wait_ge(s["zT_done"], t - 1)
                            pe.wait_ge(s["w_picked"], t - 1)
                        if c >= 2 or since(known, 3):
                            pe.wait_ge(s["hidden_done"], (t - 2) * FC + c - 1)
                        nc.tensor.matmul(ps_1[c % 2][:, :], w1g[p][:, c * 128:(c + 1) * 128], zT[p][:, :],
                                         start=True, stop=True).then_inc(s["up_done"], 1)
                    if c == 1 and live(known, 1, n_groups):
                        pe.wait_ge(z_loaded[q], (r + p) * 16)
                        if since(known, 2):
                            pe.wait_ge(s["zT_done"], t - 1)
                        for b in range(GB):
                            last = nc.tensor.transpose(ps_z[:, b * T:(b + 1) * T], z[q][:, b, :], sh.ident[:, :])
                        last.then_inc(s["z_turned"], 1)
                    if c % 2 == 1 and live(known, 3, n_groups):
                        if c == 1:
                            pe.wait_ge(s["hidden_done"], (t - 2) * FC)
                            pe.wait_ge(s["w2_picked"], t - 2)
                            if since(known, 5):
                                pe.wait_ge(s["y_done"], t - 4)
                        for b in (c - 1, c):
                            for f in range(FC):
                                last = nc.tensor.matmul(ps_2[q][:, b, :], hidden[q][:, f, b * T:(b + 1) * T],
                                                        w2g[q][:, f, :], start=(f == 0), stop=(f == FC - 1))
                        if c == 3:
                            last.then_inc(s["down_done"], 1)
            run_steps(pe, step, n_groups, LAG, PEEL)

        @block.vector
        def _(dve):
            def step(t, r, p, known):
                q = 1 - p
                if live(known, 3, n_groups):
                    dve.wait_ge(s["down_done"], t - 2)
                    if since(known, 5):
                        dve.wait_ge(y_stored[q], (r + p - 2) * 16)
                    nc.vector.tensor_copy(y[q][:, :, :], ps_2[q][:, :, :]).then_inc(s["y_done"], 1)
            run_steps(dve, step, n_groups, LAG, PEEL)


def combine_phase(nc, sem, sh, w, out, n_graphs):
    groups = n_graphs // GB
    with ExitStack() as ctx:
        def sb(name, shape, dt=F32):
            return ctx.enter_context(nc.sbuf_tensor(name, shape, dt))

        def two(name, shape, dt=F32):
            return [sb(f"{name}{i}", shape, dt) for i in range(2)]

        def ps(name, shape):
            return ctx.enter_context(nc.psum_tensor(name, shape, F32))

        X = sh.X
        NB2 = EXPERTS + 1
        w1 = sb("c_w1", [D, FF])
        w2 = sb("c_w2", [128, FC, D])
        b1 = sb("c_b1", [128, FC])
        b2 = sb("c_b2", [NB2, D])
        number_i = sb("c_number_i", [T, EXPERTS], I32)
        number = sb("c_number", [T, EXPERTS])
        stats = sb("c_stats", [T, GB, 6])
        meanvar = two("c_meanvar", [T, GB, 2])
        rstd = two("c_rstd", [T, 2, GB])
        z = sb("c_z", [T, GB, D])
        zT = two("c_zT", [D, W])
        chosen = sb("c_chosen", [T, 2 * GB, EXPERTS])
        gated = sb("c_gated", [T, 2 * GB, EXPERTS])
        gates = sb("c_gates", [T, GB, NB2])
        gatesT = two("c_gatesT", [NB2, GB, T])
        hidden = two("c_hidden", [128, FC, W])
        rows = two("c_rows", [T, 2 * GB], U32)
        y = two("c_y", [T, 2 * GB, D])
        ps_z = ps("c_ps_z", [D, W])
        ps_g = ps("c_ps_g", [NB2, GB, T])
        ps_1 = [ps(f"c_ps_1{i}", [128, W]) for i in range(2)]
        ps_2 = [ps(f"c_ps_2{i}", [T, GB, D]) for i in range(2)]

        names = ("w_loaded numbered number_set stats_done meanvar_done eps_added rstd_done z_done z_turned zT_done "
                 "chosen_done gated_done gates_done gates_turned gatesT_done up_done hidden_done down_done rows_done "
                 "shared_added weighted").split()
        s = {n: sem(f"c_{n}") for n in names}
        y_gathered = [sem(f"c_y_gathered{i}") for i in range(2)]
        stored = sem("c_stored")
        block = ctx.enter_context(nc.Block())
        out_g = out.rearrange("(g b) n d -> g n b d", b=GB)
        LAG, PEEL = 4, 6

        @block.sync
        def _(sp):
            for tile, a in ((w1[:, :], w["W1s"]), (w2[:, :, :], w["W2s"].rearrange("(c p) n -> p c n", p=128)),
                            (b1[:, :], w["b1s"].rearrange("(c p) -> p c", p=128)), (b2[0:EXPERTS, :], w["b2p"]),
                            (b2[EXPERTS:NB2, :], w["b2s"].rearrange("(a n) -> a n", a=1))):
                sp.dma_start(tile, a, allow_slow_non_contiguous=True).then_inc(s["w_loaded"], 16)

            def step(t, r, p, known):
                if live(known, 3, groups):
                    sp.wait_ge(s["weighted"], (t - 2) * 2 * GB)
                    sp.dma_start(out_g[t - 3], X[:, bass.ds((t - 3) * GB, GB), :]).then_inc(stored, 16)
            run_steps(sp, step, groups, LAG, PEEL)
            sp.wait_ge(stored, 16 * groups)

        @block.gpsimd
        def _(pool):
            nc.gpsimd.iota(number_i[:, :], pattern=[[1, EXPERTS]], base=0, channel_multiplier=0)\
              .then_inc(s["numbered"], 1)

            def step(t, r, p, known):
                if live(known, 1, groups):
                    pool.wait_ge(s["rows_done"], t)
                    if since(known, 3):
                        pool.wait_ge(s["weighted"], (t - 2) * 2 * GB)
                if live(known, 0, groups):
                    pool.wait_ge(s["meanvar_done"], t + 1)
                    if since(known, 2):
                        pool.wait_ge(s["z_done"], t - 1)
                    nc.gpsimd.tensor_tensor(rstd[p][:, 1, :], meanvar[p][:, :, 1], sh.eps[:, 0:GB],
                                            ALU.add).then_inc(s["eps_added"], 1)
                    pool.wait_ge(s["eps_added"], t + 1)
                    nc.gpsimd.tensor_tensor(rstd[p][:, 0, :], rstd[p][:, 1, :], sh.half_power[:, 0:GB],
                                            ALU.pow).then_inc(s["rstd_done"], 1)
                if live(known, 1, groups):
                    q = 1 - p
                    for i in range(2 * GB):
                        nc.gpsimd.indirect_dma_start(
                            y[q][:, i, :], None, sh.sorted_y,
                            bass.IndirectOffsetOnAxis(ap=rows[q][:, i:i + 1], axis=0)).then_inc(y_gathered[q], 16)
            run_steps(pool, step, groups, LAG, PEEL)

        @block.scalar
        def _(act):
            act.wait_ge(s["w_loaded"], 80)

            def step(t, r, p, known):
                for c in range(FC):
                    if c == 2 and live(known, 1, groups):
                        act.wait_ge(s["z_turned"], t)
                        if since(known, 3):
                            act.wait_ge(s["up_done"], (t - 2) * FC)
                        nc.scalar.activation(zT[1 - p][:, :], ps_z[:, :], ACT.Copy).then_inc(s["zT_done"], 1)
                    if live(known, 2, groups):
                        act.wait_ge(s["up_done"], (t - 2) * FC + c + 1)
                        if c == 0 and since(known, 4):
                            act.wait_ge(s["down_done"], t - 3)
                        nc.scalar.activation(hidden[p][:, c, :], ps_1[c % 2][:, :], ACT.Gelu,
                                             bias=b1[:, c:c + 1]).then_inc(s["hidden_done"], 1)
                if live(known, 2, groups):
                    act.wait_ge(s["gates_turned"], t - 1)
                    nc.scalar.activation(gatesT[p][:, :, :], ps_g[:, :, :], ACT.Copy).then_inc(s["gatesT_done"], 1)
            run_steps(act, step, groups, LAG, PEEL)

        @block.tensor
        def _(pe):
            pe.wait_ge(s["w_loaded"], 80)

            def step(t, r, p, known):
                q = 1 - p
                for c in range(FC):
                    if live(known, 2, groups):
                        if c == 0:
                            pe.wait_ge(s["zT_done"], t - 1)
                        if c >= 2 or since(known, 3):
                            pe.wait_ge(s["hidden_done"], (t - 2) * FC + c - 1)
                        nc.tensor.matmul(ps_1[c % 2][:, :], w1[:, c * 128:(c + 1) * 128], zT[p][:, :],
                                         start=True, stop=True).then_inc(s["up_done"], 1)
                    if c == 1 and live(known, 1, groups):
                        pe.wait_ge(s["z_done"], t)
                        if since(known, 2):
                            pe.wait_ge(s["zT_done"], t - 1)
                        for b in range(GB):
                            last = nc.tensor.transpose(ps_z[:, b * T:(b + 1) * T], z[:, b, :], sh.ident[:, :])
                        last.then_inc(s["z_turned"], 1)
                    if c == 1 and live(known, 2, groups):
                        pe.wait_ge(s["gates_done"], t - 1)
                        if since(known, 3):
                            pe.wait_ge(s["gatesT_done"], t - 2)
                        for b in range(GB):
                            last = nc.tensor.transpose(ps_g[:, b, :], gates[:, b, :], sh.ident[:, :])
                        last.then_inc(s["gates_turned"], 1)
                    if c % 2 == 1 and live(known, 3, groups):
                        if c == 1:
                            pe.wait_ge(s["hidden_done"], (t - 2) * FC)
                            pe.wait_ge(s["gatesT_done"], t - 2)
                            if since(known, 5):
                                pe.wait_ge(s["shared_added"], t - 4)
                        for b in (c - 1, c):
                            nc.tensor.matmul(ps_2[q][:, b, :], gatesT[q][:, b, :], b2[:, :], start=True, stop=False)
                            for f in range(FC):
                                last = nc.tensor.matmul(ps_2[q][:, b, :], hidden[q][:, f, b * T:(b + 1) * T],
                                                        w2[:, f, :], start=False, stop=(f == FC - 1))
                        if c == 3:
                            last.then_inc(s["down_done"], 1)
            run_steps(pe, step, groups, LAG, PEEL)

        @block.vector
        def _(dve):
            dve.wait_ge(s["numbered"], 1)
            nc.vector.memset(gates[:, :, EXPERTS:NB2], 1.0)
            nc.vector.tensor_copy(number[:, :], number_i[:, :]).then_inc(s["number_set"], 1)
            dve.wait_ge(s["number_set"], 1)

            def step(t, r, p, known):
                q = 1 - p
                g = t - 1
                if live(known, 0, groups):
                    if since(known, 1):
                        dve.wait_ge(s["meanvar_done"], t)
                    for b in range(GB):
                        last = nc.vector.bn_stats(stats[:, b, :], X[:, bass.ds(t * GB + b, 1), :].squeeze(1))
                    last.then_inc(s["stats_done"], 1)
                    dve.wait_ge(s["stats_done"], t + 1)
                    if since(known, 2):
                        dve.wait_ge(y_gathered[p], r * 2 * GB * 16)
                    nc.vector.tensor_copy(rows[p][:, :], sh.row_of[:, bass.ds(t, 1), :].squeeze(1))\
                      .then_inc(s["rows_done"], 1)
                    for b in range(GB):
                        last = nc.vector.bn_aggr(meanvar[p][:, b, :], stats[:, b, :])
                    last.then_inc(s["meanvar_done"], 1)
                if live(known, 1, groups):
                    dve.wait_ge(s["rstd_done"], t)
                    if since(known, 2):
                        dve.wait_ge(s["z_turned"], t - 1)
                    for b in range(GB):
                        last = nc.vector.tensor_scalar(z[:, b, :], X[:, bass.ds(g * GB + b, 1), :].squeeze(1),
                                                       meanvar[q][:, b, 0:1], rstd[q][:, 0, b:b + 1],
                                                       ALU.subtract, ALU.mult)
                    last.then_inc(s["z_done"], 1)
                if live(known, 2, groups):
                    nc.vector.tensor_tensor(
                        chosen[:, :, :],
                        sh.expert_of[:, bass.ds(t - 2, 1), :].squeeze(1).unsqueeze(2).to_broadcast([T, 2 * GB, EXPERTS]),
                        number[:, :].unsqueeze(1).to_broadcast([T, 2 * GB, EXPERTS]),
                        ALU.is_equal).then_inc(s["chosen_done"], 1)
                    dve.wait_ge(s["chosen_done"], t - 1)
                    for e in range(2):
                        last = nc.vector.tensor_tensor(
                            gated[:, e * GB:(e + 1) * GB, :], chosen[:, e * GB:(e + 1) * GB, :],
                            sh.gate[:, e, bass.ds((t - 2) * GB, GB)].unsqueeze(2).to_broadcast([T, GB, EXPERTS]), ALU.mult)
                    last.then_inc(s["gated_done"], 1)
                    dve.wait_ge(s["gated_done"], t - 1)
                    if since(known, 3):
                        dve.wait_ge(s["gates_turned"], t - 2)
                    nc.vector.tensor_tensor(gates[:, :, 0:EXPERTS], gated[:, 0:GB, :], gated[:, GB:2 * GB, :],
                                            ALU.add).then_inc(s["gates_done"], 1)
                if live(known, 3, groups):
                    dve.wait_ge(s["down_done"], t - 2)
                    at = X[:, bass.ds((t - 3) * GB, GB), :]
                    nc.vector.tensor_tensor(at, at, ps_2[q][:, :, :], ALU.add).then_inc(s["shared_added"], 1)
                    dve.wait_ge(s["shared_added"], t - 2)
                    dve.wait_ge(y_gathered[q], (r + p - 1) * 2 * GB * 16)
                    for e in range(2):
                        if e:
                            dve.wait_ge(s["weighted"], (t - 3) * 2 * GB + GB)
                        for b in range(GB):
                            at = X[:, bass.ds((t - 3) * GB + b, 1), :].squeeze(1)
                            nc.vector.scalar_tensor_tensor(
                                out=at, in0=y[q][:, e * GB + b, :],
                                scalar=sh.gate[:, e, bass.ds((t - 3) * GB + b, 1)], in1=at, op0=ALU.mult,
                                op1=ALU.add).then_inc(s["weighted"], 1)
            run_steps(dve, step, groups, LAG, PEEL)


def program(nc, stages, x, adj, wts, out):
    n_graphs = x.shape[0]
    with ExitStack() as ctx:
        def sb(name, shape, dt=F32):
            return ctx.enter_context(nc.sbuf_tensor(name, shape, dt))

        sh = Shared()
        sh.X = sb("X", [T, n_graphs, D])
        sh.ident = sb("ident", [128, 128])
        sh.ident_bf = sb("ident_bf", [128, 128], BF16)
        sh.ones_bf = sb("ones_bf", [128, 128], BF16)
        sh.headmask = sb("headmask", [128, HEADS])
        sh.eps = sb("eps", [128, 8])
        sh.half_power = sb("half_power", [128, 8])
        sh.g1col, sh.b1col, sh.g2col, sh.b2col = (sb(n, [128, 1]) for n in ("g1col", "b1col", "g2col", "b2col"))
        sh.g1all, sh.b1all = sb("g1all", [128, D]), sb("b1all", [128, D])
        sh.wlogit = sb("wlogit", [D, HC])
        sh.wfx = sb("wfx", [D, HC])
        sh.wscore = sb("wscore", [128, 128])
        sh.wvalue = sb("wvalue", [128, HP, 128])
        sh.logit_bias = sb("logit_bias", [128, HC], BF16)
        sh.fx_bias = sb("fx_bias", [128, HC], BF16)
        sh.out_bias = sb("out_bias", [128, D], BF16)
        sh.conv2_bias = sb("conv2_bias", [128, D], BF16)
        ffn0 = {k[len("L0_ffn_"):]: v for k, v in wts.items() if k.startswith("L0_ffn_")}
        gnn0 = {k[len("L0_gnn_"):]: v for k, v in wts.items() if k.startswith("L0_gnn_")}
        gnn1 = {k[len("L1_gnn_"):]: v for k, v in wts.items() if k.startswith("L1_gnn_")}
        ffn1 = {k[len("L1_ffn_"):]: v for k, v in wts.items() if k.startswith("L1_ffn_")}
        with semaphores(nc) as sem:
            setup_phase(nc, sem, sh, {**ffn0, **{k: gnn0[k] for k in ("gamma1", "beta1", "gamma2", "beta2")},
                                      "conv2_b": gnn1["b2"]})
        with ExitStack() as early:
            sh.X1 = early.enter_context(nc.sbuf_tensor("X1", [T, n_graphs, D], F32))
            with semaphores(nc) as sem:
                attention_phase(nc, sem, sh, x, adj, n_graphs)
            if stages == 1:
                with semaphores(nc) as sem:
                    store_phase(nc, sem, sh.X1, out)
                return
            with semaphores(nc) as sem:
                mlp_phase(nc, sem, sh, gnn0, n_graphs)
        if stages >= 3:
            with semaphores(nc) as sem:
                slice_phase(nc, sem, sh, n_graphs)
        if stages >= 4:
            with semaphores(nc) as sem:
                graph_phase(nc, sem, sh, adj, gnn1, n_graphs)
        if stages >= 5:
            capacity, n_groups = routing_sizes(n_graphs * T)
            sh.sorted_z = nc.dram_tensor("sorted_z", [EXPERTS * capacity + W, D], F32, kind="Internal").ap()
            sh.sorted_y = nc.dram_tensor("sorted_y", [n_groups * W, D], F32, kind="Internal").ap()
            sh.gap = sb("gap", [T, n_graphs])
            sh.gate = sb("gate", [T, 2, n_graphs])
            sh.expert_of = sb("expert_of", [T, n_graphs // GB, 2 * GB])
            sh.row_of = sb("row_of", [T, n_graphs // GB, 2 * GB])
            sh.counts = sb("counts", [T, EXPERTS])
            sh.plan = sb("plan", [1, 2, n_groups], I32)
            with semaphores(nc) as sem:
                router_phase(nc, sem, sh, ffn1, n_graphs)
            with semaphores(nc) as sem:
                schedule_phase(nc, sem, sh, n_graphs)
            with semaphores(nc) as sem:
                expert_phase(nc, sem, sh, ffn1, n_graphs)
            with semaphores(nc) as sem:
                combine_phase(nc, sem, sh, ffn1, out, n_graphs)
        else:
            with semaphores(nc) as sem:
                store_phase(nc, sem, sh.X, out)


def store_phase(nc, sem, X, out):
    stored = sem("stored")
    with nc.Block() as block:
        @block.sync
        def _(sp):
            sp.dma_start(out.rearrange("b n d -> n b d"), X[:, :, :]).then_inc(stored, 16)
            sp.wait_ge(stored, 16)


STAGES = 5
_INS = ['x', 'adj', 'L0_gnn_gamma1', 'L0_gnn_beta1', 'L0_gnn_gamma2', 'L0_gnn_beta2', 'L0_gnn_W1', 'L0_gnn_b1',
        'L0_gnn_W2', 'L0_gnn_b2', 'L0_ffn_W_fx', 'L0_ffn_b_fx', 'L0_ffn_W_x', 'L0_ffn_b_x', 'L0_ffn_W_slice',
        'L0_ffn_b_slice', 'L0_ffn_W_q', 'L0_ffn_W_k', 'L0_ffn_W_v', 'L0_ffn_W_out', 'L0_ffn_b_out',
        'L0_ffn_temperature', 'L1_gnn_w_rel1', 'L1_gnn_w_root1', 'L1_gnn_b1', 'L1_gnn_w_rel2', 'L1_gnn_w_root2',
        'L1_gnn_b2', 'L1_ffn_Wr', 'L1_ffn_W1s', 'L1_ffn_b1s', 'L1_ffn_W2s', 'L1_ffn_b2s', 'L1_ffn_W1p',
        'L1_ffn_b1p', 'L1_ffn_W2p', 'L1_ffn_b2p']


def kernel(**inputs):
    import numpy as _np
    import concourse.bacc as _bacc
    from concourse import mybir as _mybir
    from concourse.bass_utils import run_bass_kernel_spmd as _run

    nc = _bacc.Bacc("TRN2", target_bir_lowering=False, num_devices=1)
    arrays, aps = {}, {}
    for name in _INS:
        a = _np.ascontiguousarray(inputs[name])
        arrays[f"in_{name}_dram"] = a
        aps[name] = nc.dram_tensor(f"in_{name}_dram", a.shape, _mybir.dt.from_np(a.dtype), kind="ExternalInput").ap()
    out = nc.dram_tensor("out_0_dram", inputs["x"].shape, _mybir.dt.float32, kind="ExternalOutput").ap()
    program(nc, STAGES, aps["x"], aps["adj"], {n: aps[n] for n in _INS[2:]}, out)
    r = _run(nc, [arrays], core_ids=[0])
    return r.results[0]["out_0_dram"]
```

```python
from contextlib import ExitStack, contextmanager

import concourse.bass as bass
from concourse import mybir

F32 = mybir.dt.float32
F32R = mybir.dt.float32r
BF16 = mybir.dt.bfloat16
I32 = mybir.dt.int32
U32 = mybir.dt.uint32
ALU = mybir.AluOpType
ACT = mybir.ActivationFunctionType
AX = mybir.AxisListType

T = 128
D = 128
GB = 4
W = GB * T
EPS = 1e-5
HEADS = 8
HD = D // HEADS
HP = HEADS // 2
C = 64
HC = HEADS * C
FF = 512
FC = FF // 128
EXPERTS = 8
MASKED = -1e30


def run_steps(eng, step, count, lag, peel):
    for t in range(peel):
        step(t, t // 2, t % 2, t)
    with eng.Fori(0, (count - peel) // 2) as pair:
        for half in range(2):
            step(pair * 2 + (peel + half), pair + peel // 2, half, None)
    for t in range(count, count + lag):
        step(t, t // 2, t % 2, t)


def live(known, delay, count):
    return known is None or 0 <= known - delay < count


def since(known, n):
    return known is None or known >= n


def split_matmul(nc, out, weights, moving, start, stop):
    nc.tensor.matmul(out, weights[0], moving[0], start=start, stop=False)
    nc.tensor.matmul(out, weights[0], moving[1], start=False, stop=False)
    return nc.tensor.matmul(out, weights[1], moving[0], start=False, stop=stop)


@contextmanager
def semaphores(nc):
    held = []

    def sem(name):
        held.append(nc.alloc_semaphore(name))
        return held[-1]

    yield sem
    nc.clear_and_free_semaphores(held)
    nc.all_engine_barrier()


class Shared:
    pass


def setup_phase(nc, sem, sh, w):
    with ExitStack() as ctx:
        def sb(name, shape, dt=F32):
            return ctx.enter_context(nc.sbuf_tensor(name, shape, dt))

        wx = sb("wx", [128, HC])
        bxT = sb("bxT", [128, HP])
        wsl = sb("wslice_bd", [128, 128])
        wq = sb("wq_bd", [128, 128])
        wk = sb("wk_bd", [128, 128])
        wv = sb("wv_bd", [128, 128])
        wout = sb("wout", [128, HP, 128])
        temp = sb("temp", [128, HEADS])
        rtemp = sb("rtemp", [128, HEADS])
        bsl = sb("bslice_row", [1, C])
        wxT = sb("wxT", [128, HP, 128])
        wT = sb("wT", [128, 3, 128])
        rows = sb("bias_rows", [1, 5, HC])
        rest = sb("bias_rest", [1, 5, 2, HC])
        ps_t = ctx.enter_context(nc.psum_tensor("ps_t", [128, HP, 128], F32))
        ps_u = ctx.enter_context(nc.psum_tensor("ps_u", [128, 3, 128], F32))
        ps_w = ctx.enter_context(nc.psum_tensor("ps_w", [128, HP, 128], F32))
        ps_b = ctx.enter_context(nc.psum_tensor("ps_b", [1, HC], F32))
        ps_m = ctx.enter_context(nc.psum_tensor("ps_m", [128, 128], F32))
        ps_v = ctx.enter_context(nc.psum_tensor("ps_v", [128, HP, 128], F32))

        zeroed = sem("setup_zeroed")
        loaded = sem("setup_loaded")
        selected = sem("setup_selected")
        turned = sem("setup_turned")
        copied = sem("setup_copied")
        multiplied = sem("setup_multiplied")
        step_done = sem("setup_step")
        loads = []

        block = ctx.enter_context(nc.Block())

        def load_list(sp):
            col = lambda a: a.rearrange("(a b) -> a b", b=1)
            row = lambda a: a.rearrange("(a b) -> a b", a=1)
            everywhere = lambda a: row(a).to_broadcast([128, a.shape[0]])
            pairs = [(wx[:, :], w["W_x"]), (bxT[:, :], w["b_x"].rearrange("(a p) -> p a", p=128)),
                     (wout[:, :, :], w["W_out"].rearrange("(a p) n -> p a n", p=128)),
                     (temp[:, :], everywhere(w["temperature"].rearrange("a h b c -> (a h b c)"))),
                     (bsl[:, :], row(w["b_slice"])),
                     (rows[:, 1, :], row(w["b_fx"])),
                     (rows[:, 2, 0:D], row(w["b_out"])),
                     (rows[:, 3, 0:D], row(w["conv1_b"])),
                     (rows[:, 4, 0:D], row(w["conv2_b"])),
                     (sh.wfx[:, :], w["W_fx"]),
                     (sh.g1col[:, :], col(w["gamma1"])), (sh.b1col[:, :], col(w["beta1"])),
                     (sh.g2col[:, :], col(w["gamma2"])), (sh.b2col[:, :], col(w["beta2"])),
                     (sh.g1all[:, :], everywhere(w["gamma1"])), (sh.b1all[:, :], everywhere(w["beta1"]))]
            for tile, a in ((wsl, w["W_slice"]), (wq, w["W_q"]), (wk, w["W_k"]), (wv, w["W_v"])):
                pairs += [(tile[0:C, 0:C], a), (tile[C:128, C:128], a)]
            return pairs

        N_LOADS = 16 + 8

        @block.sync
        def _(sp):
            sp.wait_ge(zeroed, 1)
            pairs = load_list(sp)
            assert len(pairs) == N_LOADS
            for tile, a in pairs:
                sp.dma_start(tile, a, allow_slow_non_contiguous=True).then_inc(loaded, 16)

        @block.gpsimd
        def _(pool):
            nc.gpsimd.memset(sh.ident[:, :], 0.0).then_inc(selected, 1)
            pool.wait_ge(selected, 1)
            nc.gpsimd.affine_select(out=sh.ident[:, :], in_=sh.ident[:, :], compare_op=ALU.not_equal, fill=1.0,
                                    base=0, pattern=[[-1, 128]], channel_multiplier=1).then_inc(selected, 1)

        @block.tensor
        def _(pe):
            pe.wait_ge(loaded, 16 * N_LOADS)
            pe.wait_ge(selected, 2)
            for i in range(HP):
                nc.tensor.transpose(ps_t[:, i, :], wx[:, i * 128:(i + 1) * 128], sh.ident[:, :])
            for i, a in enumerate((wq, wk, wv)):
                last = nc.tensor.transpose(ps_u[:, i, :], a[:, :], sh.ident[:, :])
            last.then_inc(turned, 1)
            pe.wait_ge(copied, 2)
            for i in range(HP):
                nc.tensor.matmul(ps_w[:, i, :], wxT[:, i, :], wsl[:, :], start=True, stop=True)
                nc.tensor.matmul(ps_b[:, i * 128:(i + 1) * 128], bxT[:, i:i + 1], wsl[:, :], start=True, stop=True)
                nc.tensor.matmul(ps_v[:, i, :], wT[:, 2, :], wout[:, i, :], start=True, stop=True)
            nc.tensor.matmul(ps_m[:, :], wT[:, 1, :], wT[:, 0, :], start=True, stop=True).then_inc(multiplied, 1)

        @block.vector
        def _(dve):
            for tile in (wsl, wq, wk, wv):
                nc.vector.memset(tile[:, :], 0.0)
            nc.vector.memset(sh.eps[:, :], EPS)
            nc.vector.memset(sh.half_power[:, :], -0.5)
            nc.vector.memset(sh.ones_bf[:, :], 1.0)
            nc.vector.memset(rows[:, :, :], 0.0)
            for tile in (sh.logit_bias, sh.fx_bias, sh.out_bias, sh.conv1_bias, sh.conv2_bias):
                last = nc.vector.memset(tile[:, :], 0.0)
            last.then_inc(zeroed, 1)
            dve.wait_ge(selected, 2)
            nc.vector.tensor_copy(sh.ident_bf[:, :], sh.ident[:, :])
            dve.wait_ge(loaded, 16 * N_LOADS)
            done = 0
            nc.vector.tensor_scalar(temp[:, :], temp[:, :], 0.1, 5.0, ALU.max, ALU.min).then_inc(step_done, 1)
            dve.wait_ge(step_done, 1)
            nc.vector.reciprocal(rtemp[:, :], temp[:, :]).then_inc(step_done, 1)
            dve.wait_ge(turned, 1)
            nc.vector.tensor_copy(wxT[:, :, :], ps_t[:, :, :]).then_inc(copied, 1)
            nc.vector.tensor_copy(wT[:, :, :], ps_u[:, :, :]).then_inc(copied, 1)
            dve.wait_ge(step_done, 2)
            dve.wait_ge(multiplied, 1)
            per_head = lambda ap: ap.rearrange("p (h c) -> p h c", c=C)
            nc.vector.tensor_tensor(per_head(sh.wlogit[:, :]),
                                    ps_w[:, :, :].rearrange("p i (e c) -> p (i e) c", c=C),
                                    rtemp[:, :].unsqueeze(2).to_broadcast([128, HEADS, C]), ALU.mult)
            nc.vector.tensor_copy(sh.wscore[:, :], ps_m[:, :])
            nc.vector.tensor_copy(sh.wvalue[:, :, :], ps_v[:, :, :])
            row = per_head(rows[:, 0, :])
            nc.vector.tensor_tensor(row, per_head(ps_b[:, :]), bsl[:, :].unsqueeze(1).to_broadcast([1, HEADS, C]),
                                    ALU.add).then_inc(step_done, 1)
            dve.wait_ge(step_done, 3)
            nc.vector.tensor_tensor(row, row, rtemp[0:1, :].unsqueeze(2).to_broadcast([1, HEADS, C]),
                                    ALU.mult).then_inc(step_done, 1)
            dve.wait_ge(step_done, 4)
            n = 4
            biases = ((sh.logit_bias, HC), (sh.fx_bias, HC), (sh.out_bias, D), (sh.conv1_bias, D), (sh.conv2_bias, D))
            left = [rows[:, i, 0:width] for i, (_, width) in enumerate(biases)]
            for j in range(3):
                for i, (tile, width) in enumerate(biases):
                    last = nc.vector.tensor_copy(tile[32 * j:32 * j + 1, 0:width], left[i])
                last.then_inc(step_done, 1)
                n += 1
                if j < 2:
                    dve.wait_ge(step_done, n)
                    for i, (tile, width) in enumerate(biases):
                        last = nc.vector.tensor_copy(rest[:, i, j, 0:width], tile[32 * j:32 * j + 1, 0:width])
                    last.then_inc(step_done, 1)
                    n += 1
                    dve.wait_ge(step_done, n)
                    for i, (tile, width) in enumerate(biases):
                        last = nc.vector.tensor_tensor(rest[:, i, j, 0:width], left[i], rest[:, i, j, 0:width],
                                                       ALU.subtract)
                        left[i] = rest[:, i, j, 0:width]
                    last.then_inc(step_done, 1)
                    n += 1
                    dve.wait_ge(step_done, n)
            dve.wait_ge(step_done, n)


def attention_phase(nc, sem, sh, x_in, adj_in, n_graphs):
    groups = n_graphs // GB
    with ExitStack() as ctx:
        def sb(name, shape, dt=F32):
            return ctx.enter_context(nc.sbuf_tensor(name, shape, dt))

        X, X1 = sh.X, sh.X1
        adj = [sb(f"a_adj{i}", [T, GB, T], I32) for i in range(2)]
        edge_bias = [sb(f"a_edge_bias{i}", [T, GB, T], BF16) for i in range(2)]
        stats = sb("a_stats", [T, GB, 6])
        meanvar = [sb(f"a_meanvar{i}", [T, GB, 2]) for i in range(2)]
        rstd = [sb(f"a_rstd{i}", [T, 5, GB]) for i in range(2)]
        n0 = sb("a_n0", [T, GB, D])
        nT = [sb(f"a_nT{i}", [D, W]) for i in range(2)]
        headT = [sb(f"a_headT{i}", [D, HEADS, W]) for i in range(2)]
        scaled = sb("a_scaled", [T, GB, D])
        V = [sb(f"a_V{i}", [T, GB, HEADS, HD + 1]) for i in range(2)]
        top = [sb(f"a_top{i}", [T, HEADS]) for i in range(2)]
        prob = [sb(f"a_prob{i}", [T, HEADS, T]) for i in range(2)]
        probT = [sb(f"a_probT{i}", [T, HEADS, T]) for i in range(2)]
        rsum = [sb(f"a_rsum{i}", [T, HEADS]) for i in range(2)]
        attn = [sb(f"a_attn{i}", [T, HEADS, HD]) for i in range(2)]
        ps_s = [ctx.enter_context(nc.psum_tensor(f"a_ps_s{i}", [T, HEADS, T], F32)) for i in range(2)]
        ps_p = ctx.enter_context(nc.psum_tensor("a_ps_p", [T, HEADS, T], F32))
        ps_n = ctx.enter_context(nc.psum_tensor("a_ps_n", [D, W], F32))
        ps_o = ctx.enter_context(nc.psum_tensor("a_ps_o", [T, HEADS, HD + 1], F32))

        x_loaded = [sem(f"a_x_loaded{i}") for i in range(2)]
        adj_loaded = [sem(f"a_adj_loaded{i}") for i in range(2)]
        stats_done = sem("a_stats_done")
        meanvar_done = sem("a_meanvar_done")
        rstd_step = sem("a_rstd_step")
        rstd_done = sem("a_rstd_done")
        n0_done = sem("a_n0_done")
        z_done = sem("a_z_done")
        bias_done = sem("a_edge_bias_done")
        n_turned = sem("a_n_turned")
        nT_done = sem("a_nT_done")
        headT_loaded = [sem(f"a_headT_loaded{i}") for i in range(2)]
        zeros_set = sem("a_zeros_set")
        scaled_done = sem("a_scaled_done")
        V_done = sem("a_V_done")
        scores_done = sem("a_scores_done")
        top_done = sem("a_top_done")
        diff_done = sem("a_diff_done")
        prob_done = sem("a_prob_done")
        prob_turned = sem("a_prob_turned")
        probT_done = sem("a_probT_done")
        pv_done = sem("a_pv_done")
        rsum_done = sem("a_rsum_done")
        attn_done = sem("a_attn_done")
        added = sem("a_added")
        ones_set = sem("a_ones_set")

        block = ctx.enter_context(nc.Block())
        x_g = x_in.rearrange("(g b) n d -> g n b d", b=GB)
        adj_g = adj_in.rearrange("(g b) n d -> g n b d", b=GB)
        LAG, PEEL = 3, 4

        @block.sync
        def _(sp):
            def load(t, p):
                sp.dma_start(X[:, bass.ds(t * GB, GB), :], x_g[t]).then_inc(x_loaded[p], 16)
                sp.dma_start(adj[p][:, :, :], adj_g[t]).then_inc(adj_loaded[p], 16)

            load(0, 0)
            sp.wait_ge(zeros_set, 1)

            def step(t, p, known):
                if live(known, 0, groups):
                    if since(known, 2):
                        sp.wait_ge(bias_done, t - 1)
                        sp.wait_ge(stats_done, t - 1)
                    load(t, p)
                if since(known, 3):
                    sp.wait_ge(scores_done, (t - 2) * GB)
                sp.wait_ge(nT_done, t)
                for h in range(HEADS):
                    rows = slice(h * HD, (h + 1) * HD)
                    sp.dma_start(headT[1 - p][rows, h, :], nT[1 - p][rows, :]).then_inc(headT_loaded[1 - p], 16)
            for t in range(1, 3):
                step(t, t % 2, t)
            with sp.Fori(0, groups // 2 - 2) as pair:
                for odd in range(2):
                    step(pair * 2 + (3 + odd), 1 - odd, None)
            for t in range(groups - 1, groups + 1):
                step(t, t % 2, t)

        @block.gpsimd
        def _(pool):
            nc.gpsimd.memset(headT[0][:, :, :], 0.0)
            nc.gpsimd.memset(headT[1][:, :, :], 0.0).then_inc(zeros_set, 1)
            nc.gpsimd.memset(V[0][:, :, :, HD:HD + 1], 1.0)
            nc.gpsimd.memset(V[1][:, :, :, HD:HD + 1], 1.0).then_inc(ones_set, 1)

            def step(t, r, p, known):
                if live(known, 1, groups):
                    g = t - 1
                    pool.wait_ge(n0_done, t)
                    nc.gpsimd.tensor_tensor(scaled[:, :, :], n0[:, :, :],
                                            sh.g1all[:, :].unsqueeze(1).to_broadcast([T, GB, D]),
                                            ALU.mult).then_inc(scaled_done, 1)
                    pool.wait_ge(scaled_done, t)
                    if since(known, 3):
                        pool.wait_ge(pv_done, g * 4 - 4)
                    for b in range(GB):
                        last = nc.gpsimd.tensor_tensor(
                            V[1 - p][:, b, :, 0:HD], scaled[:, b, :].rearrange("p (h d) -> p h d", d=HD),
                            sh.b1all[:, :].rearrange("p (h d) -> p h d", d=HD), ALU.add)
                    last.then_inc(V_done, 1)
                for b in range(GB):
                    if live(None if known is None else (known - 2) * GB + b, 3, n_graphs):
                        k = (t - 2) * GB + b
                        pool.wait_ge(attn_done, k - 2)
                        at = X1[:, bass.ds(k - 3, 1), :].rearrange("p b (h d) -> p (b h) d", d=HD)
                        nc.gpsimd.tensor_tensor(at, at, attn[(b + 1) % 2][:, :, :], ALU.add).then_inc(added, 1)
                    if b == 2 and live(known, 0, groups):
                        q = rstd[p]
                        pool.wait_ge(meanvar_done, t + 1)
                        if since(known, 2):
                            pool.wait_ge(z_done, t - 1)
                        var = meanvar[p][:, :, 1]
                        nc.gpsimd.tensor_tensor(q[:, 2, :], var, sh.eps[:, 0:GB], ALU.add).then_inc(rstd_step, 1)
                        pool.wait_ge(rstd_step, t * 6 + 1)
                        nc.gpsimd.tensor_tensor(q[:, 0, :], q[:, 2, :], sh.half_power[:, 0:GB], ALU.pow).then_inc(rstd_step, 1)
                        pool.wait_ge(rstd_step, t * 6 + 2)
                        nc.gpsimd.tensor_tensor(q[:, 3, :], var, q[:, 0, :], ALU.mult).then_inc(rstd_step, 1)
                        pool.wait_ge(rstd_step, t * 6 + 3)
                        nc.gpsimd.tensor_tensor(q[:, 4, :], q[:, 3, :], q[:, 0, :], ALU.mult).then_inc(rstd_step, 1)
                        pool.wait_ge(rstd_step, t * 6 + 4)
                        nc.gpsimd.tensor_tensor(q[:, 2, :], q[:, 4, :], sh.eps[:, 0:GB], ALU.add).then_inc(rstd_step, 1)
                        pool.wait_ge(rstd_step, t * 6 + 5)
                        nc.gpsimd.tensor_tensor(q[:, 3, :], q[:, 2, :], sh.half_power[:, 0:GB], ALU.pow).then_inc(rstd_step, 1)
                        pool.wait_ge(rstd_step, t * 6 + 6)
                        nc.gpsimd.tensor_tensor(q[:, 1, :], q[:, 3, :], q[:, 0, :], ALU.mult).then_inc(rstd_done, 1)
            run_steps(pool, step, groups, LAG, PEEL)

        @block.scalar
        def _(act):
            def step(t, r, p, known):
                for b in range(GB):
                    kk = None if known is None else (known - 2) * GB + b
                    k = (t - 2) * GB + b
                    if live(kk, 0, n_graphs):
                        act.wait_ge(diff_done, k + 1)
                        nc.scalar.activation(prob[b % 2][:, :, :], prob[b % 2][:, :, :], ACT.Exp,
                                             scale=float(HD) ** -0.5).then_inc(prob_done, 1)
                    if live(kk, 1, n_graphs):
                        act.wait_ge(prob_turned, k)
                        if since(kk, 3):
                            act.wait_ge(pv_done, k - 2)
                        for c in range(2):
                            last = nc.scalar.activation(probT[(b + 1) % 2][:, 4 * c:4 * c + 4, :],
                                                        ps_p[:, 4 * c:4 * c + 4, :], ACT.Copy)
                        last.then_inc(probT_done, 1)
                    if b == 1 and live(known, 1, groups):
                        act.wait_ge(n_turned, t)
                        if since(known, 3):
                            act.wait_ge(scores_done, (t - 3) * GB + GB)
                            act.wait_ge(headT_loaded[1 - p], (r - 1 + p) * 16 * HEADS)
                        nc.scalar.activation(nT[1 - p][:, :], ps_n[:, :], ACT.Identity, bias=sh.b1col[:, 0:1],
                                             scale=sh.g1col[:, 0:1]).then_inc(nT_done, 1)
            run_steps(act, step, groups, LAG, PEEL)

        @block.tensor
        def _(pe):
            pe.wait_ge(ones_set, 1)

            def step(t, r, p, known):
                for b in range(GB):
                    kk = None if known is None else (known - 2) * GB + b
                    k = (t - 2) * GB + b
                    if live(kk, 0, n_graphs):
                        if b == 0:
                            pe.wait_ge(bias_done, t - 1)
                            pe.wait_ge(headT_loaded[p], r * 16 * HEADS)
                        if since(kk, 2):
                            pe.wait_ge(diff_done, k - 1)
                        S = ps_s[b % 2]
                        for c in range(2):
                            nc.tensor.matmul(S[:, 4 * c:4 * c + 4, :], sh.ident_bf[:, :],
                                             edge_bias[p][:, b:b + 1, :].to_broadcast([T, 4, T]),
                                             start=True, stop=False)
                            for h in range(4 * c, 4 * c + 4):
                                last = nc.tensor.matmul(S[:, h, :], nT[p][:, b * T:(b + 1) * T],
                                                        headT[p][:, h, b * T:(b + 1) * T],
                                                        start=False, stop=(h == 4 * c + 3))
                        last.then_inc(scores_done, 1)
                    if b == 1 and live(known, 1, groups):
                        pe.wait_ge(n0_done, t)
                        if since(known, 2):
                            pe.wait_ge(nT_done, t - 1)
                        for i in range(GB):
                            last = nc.tensor.transpose(ps_n[:, i * T:(i + 1) * T], n0[:, i, :], sh.ident[:, :])
                        last.then_inc(n_turned, 1)
                    if live(kk, 1, n_graphs):
                        pe.wait_ge(prob_done, k)
                        if since(kk, 2):
                            pe.wait_ge(probT_done, k - 1)
                        for h in range(HEADS):
                            last = nc.tensor.transpose(ps_p[:, h, :], prob[(b + 1) % 2][:, h, :], sh.ident[:, :])
                        last.then_inc(prob_turned, 1)
                    if live(kk, 2, n_graphs):
                        pe.wait_ge(probT_done, k - 1)
                        pe.wait_ge(V_done, t - 1 if b >= 2 else t - 2)
                        if since(kk, 3):
                            pe.wait_ge(attn_done, k - 2)
                        own = V[p] if b >= 2 else V[1 - p]
                        for h in range(HEADS):
                            last = nc.tensor.matmul(ps_o[:, h, :], probT[b % 2][:, h, :],
                                                    own[:, (b + 2) % GB, h, :], start=True, stop=True)
                        last.then_inc(pv_done, 1)
            run_steps(pe, step, groups, LAG, PEEL)

        @block.vector
        def _(dve):
            def step(t, r, p, known):
                for b in range(GB):
                    kk = None if known is None else (known - 2) * GB + b
                    k = (t - 2) * GB + b
                    if b == 2 and live(known, 0, groups):
                        dve.wait_ge(stats_done, t + 1)
                    if live(kk, 3, n_graphs):
                        q = (b + 1) % 2
                        dve.wait_ge(pv_done, k - 2)
                        nc.vector.reciprocal(rsum[q][:, :], ps_o[:, :, HD]).then_inc(rsum_done, 1)
                        dve.wait_ge(rsum_done, k - 2)
                        if since(kk, 5):
                            dve.wait_ge(added, k - 4)
                        nc.vector.tensor_tensor(attn[q][:, :, :], ps_o[:, :, 0:HD],
                                                rsum[q][:, :].unsqueeze(2).to_broadcast([T, HEADS, HD]),
                                                ALU.mult).then_inc(attn_done, 1)
                    if live(kk, 0, n_graphs):
                        dve.wait_ge(scores_done, k + 1)
                        nc.vector.reduce_max(top[b % 2][:, :], ps_s[b % 2][:, :, :], AX.X).then_inc(top_done, 1)
                        dve.wait_ge(top_done, k + 1)
                        if since(kk, 2):
                            dve.wait_ge(prob_turned, k - 1)
                        nc.vector.tensor_tensor(prob[b % 2][:, :, :], ps_s[b % 2][:, :, :],
                                                top[b % 2][:, :].unsqueeze(2).to_broadcast([T, HEADS, T]),
                                                ALU.subtract).then_inc(diff_done, 1)
                    if b == 0 and live(known, 1, groups):
                        dve.wait_ge(rstd_done, t)
                        if since(known, 2):
                            dve.wait_ge(n_turned, t - 1)
                            dve.wait_ge(scaled_done, t - 1)
                        for i in range(GB):
                            last = nc.vector.tensor_scalar(
                                n0[:, i, :], X[:, bass.ds((t - 1) * GB + i, 1), :].squeeze(1),
                                meanvar[1 - p][:, i, 0:1], rstd[1 - p][:, 1, i:i + 1], ALU.subtract, ALU.mult)
                        last.then_inc(n0_done, 1)
                    if b == 2 and live(known, 1, groups):
                        for i in range(GB):
                            last = nc.vector.tensor_scalar(
                                X1[:, bass.ds((t - 1) * GB + i, 1), :].squeeze(1),
                                X[:, bass.ds((t - 1) * GB + i, 1), :].squeeze(1),
                                meanvar[1 - p][:, i, 0:1], rstd[1 - p][:, 0, i:i + 1], ALU.subtract, ALU.mult)
                        last.then_inc(z_done, 1)
                    if b == 1 and live(known, 0, groups):
                        dve.wait_ge(x_loaded[p], (r + 1) * 16)
                        for i in range(GB):
                            last = nc.vector.bn_stats(stats[:, i, :], X[:, bass.ds(t * GB + i, 1), :].squeeze(1))
                        last.then_inc(stats_done, 1)
                    if b == 2 and live(known, 0, groups):
                        for i in range(GB):
                            last = nc.vector.bn_aggr(meanvar[p][:, i, :], stats[:, i, :])
                        last.then_inc(meanvar_done, 1)
                if live(known, 0, groups):
                    dve.wait_ge(adj_loaded[p], (r + 1) * 16)
                    if since(known, 2):
                        dve.wait_ge(scores_done, (t - 1) * GB)
                    nc.vector.tensor_scalar(edge_bias[p][:, :, :], adj[p][:, :, :], 0.0, MASKED,
                                            ALU.is_le, ALU.mult).then_inc(bias_done, 1)
            run_steps(dve, step, groups, LAG, PEEL)


def mlp_phase(nc, sem, sh, w, n_graphs):
    groups = n_graphs // GB
    with ExitStack() as ctx:
        def sb(name, shape, dt=F32):
            return ctx.enter_context(nc.sbuf_tensor(name, shape, dt))

        X, X1 = sh.X, sh.X1
        w1 = sb("m_w1", [D, FF])
        w2 = sb("m_w2", [128, FC, D])
        b1 = sb("m_b1", [128, FC])
        b2all = sb("m_b2all", [T, D])
        stats = sb("m_stats", [T, GB, 6])
        meanvar = [sb(f"m_meanvar{i}", [T, GB, 2]) for i in range(2)]
        rstd = [sb(f"m_rstd{i}", [T, 2, GB]) for i in range(2)]
        n1 = sb("m_n1", [T, GB, D])
        spare = sb("m_spare", [T, 1])
        yT = sb("m_yT", [D, W])
        yTh = [sb(f"m_yTh{i}", [D, W], F32R) for i in range(2)]
        yTl = [sb(f"m_yTl{i}", [D, W], F32R) for i in range(2)]
        w1h, w1l = sb("m_w1h", [D, FF], F32R), sb("m_w1l", [D, FF], F32R)
        hidden = [sb(f"m_hidden{i}", [128, FC, W]) for i in range(2)]
        total = sb("m_total", [T, GB, D])
        ps_n = ctx.enter_context(nc.psum_tensor("m_ps_n", [D, W], F32))
        ps_1 = [ctx.enter_context(nc.psum_tensor(f"m_ps_1{i}", [128, W], F32)) for i in range(2)]
        ps_2 = [ctx.enter_context(nc.psum_tensor(f"m_ps_2{i}", [T, GB, D], F32)) for i in range(2)]

        w_loaded = sem("m_w_loaded")
        stats_done = sem("m_stats_done")
        meanvar_done = sem("m_meanvar_done")
        eps_added = sem("m_eps_added")
        rstd_done = sem("m_rstd_done")
        n_done = sem("m_n_done")
        n_turned = sem("m_n_turned")
        yT_done = sem("m_yT_done")
        yTh_done = sem("m_yTh_done")
        yT_split = sem("m_yT_split")
        w1h_done = sem("m_w1h_done")
        w1_split = sem("m_w1_split")
        up_done = sem("m_up_done")
        hidden_done = sem("m_hidden_done")
        down_done = sem("m_down_done")
        bias_added = sem("m_bias_added")
        total_done = sem("m_total_done")
        x_done = sem("m_x_done")

        block = ctx.enter_context(nc.Block())
        LAG, PEEL = 3, 4

        @block.sync
        def _(sp):
            sp.dma_start(w1[:, :], w["W1"]).then_inc(w_loaded, 16)
            sp.dma_start(w2[:, :, :], w["W2"].rearrange("(c p) n -> p c n", p=128)).then_inc(w_loaded, 16)
            sp.dma_start(b1[:, :], w["b1"].rearrange("(c p) -> p c", p=128),
                         allow_slow_non_contiguous=True).then_inc(w_loaded, 16)
            sp.dma_start(b2all[:, :], w["b2"].rearrange("(a n) -> a n", a=1).to_broadcast([T, D]))\
              .then_inc(w_loaded, 16)

        @block.gpsimd
        def _(pool):
            pool.wait_ge(w_loaded, 64)

            def step(t, r, p, known):
                if live(known, 0, groups):
                    pool.wait_ge(meanvar_done, t + 1)
                    if since(known, 2):
                        pool.wait_ge(n_done, t - 1)
                    nc.gpsimd.tensor_tensor(rstd[p][:, 1, :], meanvar[p][:, :, 1], sh.eps[:, 0:GB],
                                            ALU.add).then_inc(eps_added, 1)
                    pool.wait_ge(eps_added, t + 1)
                    nc.gpsimd.tensor_tensor(rstd[p][:, 0, :], rstd[p][:, 1, :], sh.half_power[:, 0:GB],
                                            ALU.pow).then_inc(rstd_done, 1)
                    at = X[:, bass.ds(t * GB, GB), :]
                    nc.gpsimd.tensor_tensor(at, at, b2all[:, :].unsqueeze(1).to_broadcast([T, GB, D]),
                                            ALU.add).then_inc(bias_added, 1)
            run_steps(pool, step, groups, 0, PEEL)

        @block.scalar
        def _(act):
            act.wait_ge(w_loaded, 64)

            def step(t, r, p, known):
                for c in range(FC):
                    if c == 2 and live(known, 1, groups):
                        act.wait_ge(n_turned, t)
                        if since(known, 2):
                            act.wait_ge(yT_split, t - 1)
                        nc.scalar.activation(yT[:, :], ps_n[:, :], ACT.Identity, bias=sh.b2col[:, 0:1],
                                             scale=sh.g2col[:, 0:1]).then_inc(yT_done, 1)
                        act.wait_ge(yT_done, t)
                        if since(known, 3):
                            act.wait_ge(up_done, (t - 2) * FC)
                        nc.scalar.activation(yTh[1 - p][:, :], yT[:, :], ACT.Copy).then_inc(yTh_done, 1)
                    if live(known, 2, groups):
                        act.wait_ge(up_done, (t - 2) * FC + c + 1)
                        if c == 0 and since(known, 4):
                            act.wait_ge(down_done, t - 3)
                        nc.scalar.activation(hidden[p][:, c, :], ps_1[c % 2][:, :], ACT.Gelu,
                                             bias=b1[:, c:c + 1]).then_inc(hidden_done, 1)
            run_steps(act, step, groups, LAG, PEEL)

        @block.tensor
        def _(pe):
            pe.wait_ge(w1_split, 1)

            def step(t, r, p, known):
                for c in range(FC):
                    if live(known, 2, groups):
                        if c == 0:
                            pe.wait_ge(yT_split, t - 1)
                        if c >= 2 or since(known, 3):
                            pe.wait_ge(hidden_done, (t - 2) * FC + c - 1)
                        ch = slice(c * 128, (c + 1) * 128)
                        split_matmul(nc, ps_1[c % 2][:, :], (w1h[:, ch], w1l[:, ch]), (yTh[p][:, :], yTl[p][:, :]),
                                     True, True).then_inc(up_done, 1)
                    if c == 1 and live(known, 1, groups):
                        pe.wait_ge(n_done, t)
                        if since(known, 2):
                            pe.wait_ge(yT_done, t - 1)
                        for b in range(GB):
                            last = nc.tensor.transpose(ps_n[:, b * T:(b + 1) * T], n1[:, b, :], sh.ident[:, :])
                        last.then_inc(n_turned, 1)
                    if c % 2 == 1 and live(known, 3, groups):
                        if c == 1:
                            pe.wait_ge(hidden_done, (t - 2) * FC)
                            if since(known, 5):
                                pe.wait_ge(total_done, t - 4)
                        for b in (c - 1, c):
                            for f in range(FC):
                                last = nc.tensor.matmul(ps_2[1 - p][:, b, :], hidden[1 - p][:, f, b * T:(b + 1) * T],
                                                        w2[:, f, :], start=(f == 0), stop=(f == FC - 1))
                        if c == 3:
                            last.then_inc(down_done, 1)
            run_steps(pe, step, groups, LAG, PEEL)

        @block.vector
        def _(dve):
            dve.wait_ge(w_loaded, 64)
            nc.vector.tensor_copy(w1h[:, :], w1[:, :]).then_inc(w1h_done, 1)
            dve.wait_ge(w1h_done, 1)
            nc.vector.tensor_tensor(w1l[:, :], w1[:, :], w1h[:, :], ALU.subtract).then_inc(w1_split, 1)

            def step(t, r, p, known):
                if live(known, 0, groups):
                    for b in range(GB):
                        last = nc.vector.bn_stats(stats[:, b, :], X1[:, bass.ds(t * GB + b, 1), :].squeeze(1))
                    last.then_inc(stats_done, 1)
                if live(known, 0, groups):
                    dve.wait_ge(stats_done, t + 1)
                    nc.vector.tensor_copy(spare[:, :], sh.eps[:, 0:1])
                    for b in range(GB):
                        last = nc.vector.bn_aggr(meanvar[p][:, b, :], stats[:, b, :])
                    last.then_inc(meanvar_done, 1)
                if live(known, 1, groups):
                    dve.wait_ge(yTh_done, t)
                    nc.vector.tensor_tensor(yTl[1 - p][:, :], yT[:, :], yTh[1 - p][:, :], ALU.subtract)\
                      .then_inc(yT_split, 1)
                if live(known, 0, groups):
                    dve.wait_ge(rstd_done, t + 1)
                    if since(known, 1):
                        dve.wait_ge(n_turned, t)
                    for b in range(GB):
                        last = nc.vector.tensor_scalar(n1[:, b, :], X1[:, bass.ds(t * GB + b, 1), :].squeeze(1),
                                                       meanvar[p][:, b, 0:1], rstd[p][:, 0, b:b + 1],
                                                       ALU.subtract, ALU.mult)
                    last.then_inc(n_done, 1)
                if live(known, 3, groups):
                    dve.wait_ge(down_done, t - 2)
                    if since(known, 4):
                        dve.wait_ge(x_done, t - 3)
                    nc.vector.tensor_tensor(total[:, :, :], ps_2[1 - p][:, :, :],
                                            X1[:, bass.ds((t - 3) * GB, GB), :], ALU.add).then_inc(total_done, 1)
                if live(known, 3, groups):
                    dve.wait_ge(total_done, t - 2)
                    dve.wait_ge(bias_added, t - 2)
                    at = X[:, bass.ds((t - 3) * GB, GB), :]
                    nc.vector.tensor_tensor(at, at, total[:, :, :], ALU.add).then_inc(x_done, 1)
            run_steps(dve, step, groups, LAG, PEEL)


def slice_phase(nc, sem, sh, n_graphs):
    with ExitStack() as ctx:
        def sb(name, shape, dt=F32):
            return ctx.enter_context(nc.sbuf_tensor(name, shape, dt))

        def two(name, shape, dt=F32):
            return [sb(f"{name}{i}", shape, dt) for i in range(2)]

        def ps(name, shape):
            return ctx.enter_context(nc.psum_tensor(name, shape, F32))

        X = sh.X
        stats = sb("s_stats", [T, 6])
        meanvar = two("s_meanvar", [T, 2])
        rstd = two("s_rstd", [T, 2])
        z = sb("s_z", [T, D])
        spare = sb("s_spare", [T, 1])
        wlogit = [sb(f"s_wlogit_{n}", [D, HC], F32R) for n in ("high", "low")]
        wfx = [sb(f"s_wfx_{n}", [D, HC], F32R) for n in ("high", "low")]
        zTh, zTl = two("s_zTh", [D, T], F32R), two("s_zTl", [D, T], F32R)
        top = sb("s_top", [T, HEADS])
        diff = two("s_diff", [T, HEADS, C])
        expo = two("s_expo", [T, HEADS, C])
        rsum = two("s_rsum", [T, 2, HEADS])
        sw = two("s_sw", [T, HEADS, C])
        fx = two("s_fx", [T, HEADS, C + 1])
        swT = two("s_swT", [128, HP, T])
        rnorm = sb("s_rnorm", [128, 2, HP])
        tok = sb("s_tok", [128, HP, 128])
        tokT = two("s_tokT", [128, HP, 128])
        tokTc = sb("s_tokTc", [128, HP, C])
        key = sb("s_key", [128, HP, C])
        top2 = sb("s_top2", [128, HP])
        diff2 = two("s_diff2", [128, HP, C])
        att = sb("s_att", [128, HP, 128])
        rsum2 = two("s_rsum2", [128, 2, HP])
        attT = two("s_attT", [128, HP, 128])
        val = two("s_val", [128, HP, D])
        mixed = sb("s_mixed", [128, HP, D])
        ps_l, ps_f, ps_w = ps("s_ps_l", [T, HEADS, C]), ps("s_ps_f", [T, HEADS, C]), ps("s_ps_w", [128, HP, T])
        ps_t, ps_v = ps("s_ps_t", [128, HP, 128]), ps("s_ps_v", [128, HP, D])
        ps_a, ps_b, ps_u = ps("s_ps_a", [128, HP, C]), ps("s_ps_b", [128, 128]), ps("s_ps_u", [128, HP, C + 1])

        names = ("constants weights_split stats_done meanvar_done eps_added rstd_done z_done z_turned zTh_done zT_done logits_done fx_done "
                 "fx_copied top_done diff_done expo_done sum_done rsum_done sw_done u_done norm_step rnorm_done "
                 "tok_done sw_turned swT_done tok_turned tokT_done tokTc_done keys_done key_copied scores_done "
                 "top2_done diff2_done att_done sum2_done rsum2_done att_turned attT_done val_done val_copied "
                 "mixed_done mixed_scaled out_done x_done").split()
        s = {n: sem(f"s_{n}") for n in names}
        block = ctx.enter_context(nc.Block())
        LAG, PEEL = 5, 6
        lo, hi = slice(0, C), slice(C, 128)

        @block.gpsimd
        def _(pool):
            nc.gpsimd.memset(tok[:, :, :], 0.0)
            nc.gpsimd.memset(att[:, :, :], 0.0)
            nc.gpsimd.memset(fx[0][:, :, C:C + 1], 1.0)
            nc.gpsimd.memset(fx[1][:, :, C:C + 1], 1.0).then_inc(s["constants"], 1)

            def step(t, r, p, known):
                if live(known, 2, n_graphs):
                    pool.wait_ge(s["rsum_done"], t - 1)
                    if since(known, 4):
                        pool.wait_ge(s["sw_turned"], t - 3)
                        pool.wait_ge(s["u_done"], t - 3)
                    nc.gpsimd.tensor_tensor(sw[p][:, :, :], expo[p][:, :, :],
                                            rsum[p][:, 1, :].unsqueeze(2).to_broadcast([T, HEADS, C]),
                                            ALU.mult).then_inc(s["sw_done"], 1)
                if live(known, 0, n_graphs):
                    pool.wait_ge(s["meanvar_done"], t + 1)
                    if since(known, 2):
                        pool.wait_ge(s["z_done"], t - 1)
                    nc.gpsimd.tensor_tensor(rstd[p][:, 1:2], meanvar[p][:, 1:2], sh.eps[:, 0:1],
                                            ALU.add).then_inc(s["eps_added"], 1)
                    pool.wait_ge(s["eps_added"], t + 1)
                    nc.gpsimd.tensor_tensor(rstd[p][:, 0:1], rstd[p][:, 1:2], sh.half_power[:, 0:1],
                                            ALU.pow).then_inc(s["rstd_done"], 1)
            run_steps(pool, step, n_graphs, 2, PEEL)

        @block.tensor
        def _(pe):
            pe.wait_ge(s["constants"], 1)
            pe.wait_ge(s["weights_split"], 2)

            def step(t, r, p, known):
                q = 1 - p
                if live(known, 2, n_graphs):
                    pe.wait_ge(s["zT_done"], t - 1)
                    if since(known, 3):
                        pe.wait_ge(s["diff_done"], t - 2)
                    nc.tensor.matmul(ps_l[:, :, :], sh.ones_bf[:, :], sh.logit_bias[:, :], start=True, stop=False)
                    split_matmul(nc, ps_l[:, :, :], (zTh[p][:, :], zTl[p][:, :]), [a[:, :] for a in wlogit],
                                 False, True).then_inc(s["logits_done"], 1)
                if live(known, 4, n_graphs):
                    pe.wait_ge(s["tok_done"], t - 3)
                    if since(known, 5):
                        pe.wait_ge(s["attT_done"], t - 4)
                    for i in range(HP):
                        last = nc.tensor.transpose(ps_t[:, i, :], tok[:, i, :], sh.ident[:, :])
                    last.then_inc(s["tok_turned"], 1)
                if live(known, 5, n_graphs):
                    pe.wait_ge(s["attT_done"], t - 4)
                    pe.wait_ge(s["val_copied"], t - 4)
                    if since(known, 6):
                        pe.wait_ge(s["mixed_scaled"], t - 5)
                    for i in range(HP):
                        last = nc.tensor.matmul(ps_v[:, i, :], attT[q][:, i, :], val[q][:, i, :], start=True, stop=True)
                    last.then_inc(s["mixed_done"], 1)
                if live(known, 2, n_graphs):
                    if since(known, 3):
                        pe.wait_ge(s["fx_copied"], t - 2)
                    nc.tensor.matmul(ps_f[:, :, :], sh.ones_bf[:, :], sh.fx_bias[:, :], start=True, stop=False)
                    split_matmul(nc, ps_f[:, :, :], (zTh[p][:, :], zTl[p][:, :]), [a[:, :] for a in wfx],
                                 False, True).then_inc(s["fx_done"], 1)
                if live(known, 4, n_graphs):
                    pe.wait_ge(s["tokTc_done"], t - 3)
                    if since(known, 5):
                        pe.wait_ge(s["diff2_done"], t - 4)
                    nc.tensor.matmul(ps_a[:, :, :], sh.wscore[:, :], tokTc[:, :, :], start=True,
                                     stop=True).then_inc(s["keys_done"], 1)
                if live(known, 5, n_graphs):
                    pe.wait_ge(s["mixed_scaled"], t - 4)
                    pe.wait_ge(s["swT_done"], t - 4)
                    nc.tensor.matmul(ps_b[:, :], sh.ones_bf[:, :], sh.out_bias[:, :], start=True, stop=False)
                    for i in range(HP):
                        last = nc.tensor.matmul(ps_b[:, :], swT[q][:, i, :], mixed[:, i, :], start=False,
                                                stop=(i == HP - 1))
                    last.then_inc(s["out_done"], 1)
                if live(known, 4, n_graphs):
                    pe.wait_ge(s["key_copied"], t - 3)
                    for i in range(HP):
                        last = nc.tensor.matmul(ps_a[:, i, :], tokT[p][:, i, :], key[:, i, :], start=True, stop=True)
                    last.then_inc(s["scores_done"], 1)
                if live(known, 1, n_graphs):
                    pe.wait_ge(s["z_done"], t)
                    if since(known, 5):
                        pe.wait_ge(s["x_done"], t - 4)
                    nc.tensor.transpose(ps_b[:, :], z[:, :], sh.ident[:, :]).then_inc(s["z_turned"], 1)
                if live(known, 3, n_graphs):
                    pe.wait_ge(s["sw_done"], t - 2)
                    pe.wait_ge(s["fx_copied"], t - 2)
                    if since(known, 4):
                        pe.wait_ge(s["tok_done"], t - 3)
                    for h in range(HEADS):
                        last = nc.tensor.matmul(ps_u[(h % 2) * C:(h % 2 + 1) * C, h // 2, :], sw[q][:, h, :],
                                                fx[q][:, h, :], start=True, stop=True)
                    last.then_inc(s["u_done"], 1)
                if live(known, 3, n_graphs):
                    if since(known, 4):
                        pe.wait_ge(s["swT_done"], t - 3)
                    for i in range(HP):
                        last = nc.tensor.transpose(ps_w[:, i, :], sw[q][:, 2 * i:2 * i + 2, :], sh.ident[:, :])
                    last.then_inc(s["sw_turned"], 1)
                if live(known, 4, n_graphs):
                    if since(known, 5):
                        pe.wait_ge(s["mixed_scaled"], t - 4)
                    for i in range(HP):
                        last = nc.tensor.matmul(ps_v[:, i, :], tokT[p][:, i, :], sh.wvalue[:, i, :], start=True, stop=True)
                    last.then_inc(s["val_done"], 1)
                if live(known, 4, n_graphs):
                    pe.wait_ge(s["att_done"], t - 3)
                    for i in range(HP):
                        last = nc.tensor.transpose(ps_t[:, i, :], att[:, i, :], sh.ident[:, :])
                    last.then_inc(s["att_turned"], 1)
            run_steps(pe, step, n_graphs, LAG, PEEL)

        @block.scalar
        def _(act):
            def step(t, r, p, known):
                q = 1 - p
                if live(known, 4, n_graphs):
                    act.wait_ge(s["tok_turned"], t - 3)
                    if since(known, 6):
                        act.wait_ge(s["val_done"], t - 5)
                    nc.scalar.activation(tokT[p][:, :, :], ps_t[:, :, :], ACT.Copy).then_inc(s["tokT_done"], 1)
                if live(known, 2, n_graphs):
                    act.wait_ge(s["diff_done"], t - 1)
                    if since(known, 4):
                        act.wait_ge(s["sw_done"], t - 3)
                    nc.scalar.activation(expo[p][:, :, :], diff[p][:, :, :], ACT.Exp).then_inc(s["expo_done"], 1)
                if live(known, 2, n_graphs):
                    act.wait_ge(s["fx_done"], t - 1)
                    if since(known, 4):
                        act.wait_ge(s["u_done"], t - 3)
                    nc.scalar.activation(fx[p][:, :, 0:C], ps_f[:, :, :], ACT.Copy).then_inc(s["fx_copied"], 1)
                if live(known, 4, n_graphs):
                    act.wait_ge(s["keys_done"], t - 3)
                    if since(known, 5):
                        act.wait_ge(s["scores_done"], t - 4)
                    nc.scalar.activation(key[:, :, :], ps_a[:, :, :], ACT.Copy).then_inc(s["key_copied"], 1)
                if live(known, 1, n_graphs):
                    act.wait_ge(s["z_turned"], t)
                    if since(known, 3):
                        act.wait_ge(s["fx_done"], t - 2)
                    nc.scalar.activation(zTh[q][:, :], ps_b[:, :], ACT.Copy).then_inc(s["zTh_done"], 1)
                if live(known, 4, n_graphs):
                    act.wait_ge(s["diff2_done"], t - 3)
                    if since(known, 5):
                        act.wait_ge(s["att_turned"], t - 4)
                    scale = float(C) ** -0.5
                    nc.scalar.activation(att[lo, :, lo], diff2[p][lo, :, :], ACT.Exp, scale=scale)
                    nc.scalar.activation(att[hi, :, hi], diff2[p][hi, :, :], ACT.Exp,
                                         scale=scale).then_inc(s["att_done"], 1)
                if live(known, 3, n_graphs):
                    act.wait_ge(s["sw_turned"], t - 2)
                    if since(known, 5):
                        act.wait_ge(s["out_done"], t - 4)
                    nc.scalar.activation(swT[q][:, :, :], ps_w[:, :, :], ACT.Copy).then_inc(s["swT_done"], 1)
                if live(known, 4, n_graphs):
                    act.wait_ge(s["val_done"], t - 3)
                    if since(known, 6):
                        act.wait_ge(s["mixed_done"], t - 5)
                    nc.scalar.activation(val[p][:, :, :], ps_v[:, :, :], ACT.Copy).then_inc(s["val_copied"], 1)
                if live(known, 4, n_graphs):
                    act.wait_ge(s["att_turned"], t - 3)
                    nc.scalar.activation(attT[p][:, :, :], ps_t[:, :, :], ACT.Copy).then_inc(s["attT_done"], 1)
            run_steps(act, step, n_graphs, LAG, PEEL)

        @block.vector
        def _(dve):
            for (high, low), whole in ((wlogit, sh.wlogit), (wfx, sh.wfx)):
                last = nc.vector.tensor_copy(high[:, :], whole[:, :])
            last.then_inc(s["weights_split"], 1)
            dve.wait_ge(s["weights_split"], 1)
            for (high, low), whole in ((wlogit, sh.wlogit), (wfx, sh.wfx)):
                last = nc.vector.tensor_tensor(low[:, :], whole[:, :], high[:, :], ALU.subtract)
            last.then_inc(s["weights_split"], 1)

            def step(t, r, p, known):
                q = 1 - p
                if live(known, 2, n_graphs):
                    dve.wait_ge(s["logits_done"], t - 1)
                    nc.vector.reduce_max(top[:, :], ps_l[:, :, :], AX.X).then_inc(s["top_done"], 1)
                    dve.wait_ge(s["top_done"], t - 1)
                    if since(known, 4):
                        dve.wait_ge(s["expo_done"], t - 3)
                    nc.vector.tensor_tensor(diff[p][:, :, :], ps_l[:, :, :],
                                            top[:, :].unsqueeze(2).to_broadcast([T, HEADS, C]),
                                            ALU.subtract).then_inc(s["diff_done"], 1)
                if live(known, 4, n_graphs):
                    dve.wait_ge(s["tokT_done"], t - 3)
                    if since(known, 5):
                        dve.wait_ge(s["keys_done"], t - 4)
                    nc.vector.tensor_tensor(tokTc[:, :, :], tokT[p][:, :, lo], tokT[p][:, :, hi],
                                            ALU.add).then_inc(s["tokTc_done"], 1)
                if live(known, 5, n_graphs):
                    dve.wait_ge(s["mixed_done"], t - 4)
                    dve.wait_ge(s["rsum2_done"], t - 4)
                    if since(known, 6):
                        dve.wait_ge(s["out_done"], t - 5)
                    nc.vector.tensor_tensor(mixed[:, :, :], ps_v[:, :, :],
                                            rsum2[q][:, 1, :].unsqueeze(2).to_broadcast([128, HP, D]),
                                            ALU.mult).then_inc(s["mixed_scaled"], 1)
                if live(known, 2, n_graphs):
                    dve.wait_ge(s["expo_done"], t - 1)
                    if since(known, 4):
                        dve.wait_ge(s["sw_done"], t - 3)
                    nc.vector.reduce_sum(rsum[p][:, 0, :], expo[p][:, :, :], AX.X).then_inc(s["sum_done"], 1)
                    dve.wait_ge(s["sum_done"], t - 1)
                    nc.vector.reciprocal(rsum[p][:, 1, :], rsum[p][:, 0, :]).then_inc(s["rsum_done"], 1)
                if live(known, 1, n_graphs):
                    dve.wait_ge(s["rstd_done"], t)
                    if since(known, 2):
                        dve.wait_ge(s["z_turned"], t - 1)
                    nc.vector.tensor_scalar(z[:, :], X[:, bass.ds(t - 1, 1), :].squeeze(1), meanvar[q][:, 0:1],
                                            rstd[q][:, 0:1], ALU.subtract, ALU.mult).then_inc(s["z_done"], 1)
                if live(known, 5, n_graphs):
                    dve.wait_ge(s["out_done"], t - 4)
                    at = X[:, bass.ds(t - 5, 1), :].squeeze(1)
                    nc.vector.tensor_tensor(at, at, ps_b[:, :], ALU.add).then_inc(s["x_done"], 1)
                if live(known, 0, n_graphs):
                    nc.vector.bn_stats(stats[:, :], X[:, bass.ds(t, 1), :].squeeze(1)).then_inc(s["stats_done"], 1)
                if live(known, 4, n_graphs):
                    dve.wait_ge(s["scores_done"], t - 3)
                    nc.vector.reduce_max(top2[:, :], ps_a[:, :, :], AX.X).then_inc(s["top2_done"], 1)
                    dve.wait_ge(s["top2_done"], t - 3)
                    if since(known, 6):
                        dve.wait_ge(s["att_done"], t - 5)
                    nc.vector.tensor_tensor(diff2[p][:, :, :], ps_a[:, :, :],
                                            top2[:, :].unsqueeze(2).to_broadcast([128, HP, C]),
                                            ALU.subtract).then_inc(s["diff2_done"], 1)
                if live(known, 1, n_graphs):
                    dve.wait_ge(s["zTh_done"], t)
                    nc.vector.tensor_tensor(zTl[q][:, :], ps_b[:, :], zTh[q][:, :], ALU.subtract)\
                      .then_inc(s["zT_done"], 1)
                if live(known, 3, n_graphs):
                    dve.wait_ge(s["u_done"], t - 2)
                    nc.vector.tensor_scalar(rnorm[:, 0, :], ps_u[:, :, C], EPS, None,
                                            ALU.add).then_inc(s["norm_step"], 1)
                    dve.wait_ge(s["norm_step"], t - 2)
                    nc.vector.reciprocal(rnorm[:, 1, :], rnorm[:, 0, :]).then_inc(s["rnorm_done"], 1)
                    dve.wait_ge(s["rnorm_done"], t - 2)
                    if since(known, 4):
                        dve.wait_ge(s["tok_turned"], t - 3)
                    for half in (lo, hi):
                        last = nc.vector.tensor_tensor(tok[half, :, half], ps_u[half, :, 0:C],
                                                       rnorm[half, 1, :].unsqueeze(2).to_broadcast([C, HP, C]),
                                                       ALU.mult)
                    last.then_inc(s["tok_done"], 1)
                if live(known, 0, n_graphs):
                    dve.wait_ge(s["stats_done"], t + 1)
                    nc.vector.tensor_copy(spare[:, :], sh.eps[:, 0:1])
                    nc.vector.bn_aggr(meanvar[p][:, :], stats[:, :]).then_inc(s["meanvar_done"], 1)
                if live(known, 4, n_graphs):
                    dve.wait_ge(s["att_done"], t - 3)
                    if since(known, 6):
                        dve.wait_ge(s["mixed_scaled"], t - 5)
                    nc.vector.reduce_sum(rsum2[p][:, 0, :], att[:, :, :], AX.X).then_inc(s["sum2_done"], 1)
                if live(known, 4, n_graphs):
                    dve.wait_ge(s["sum2_done"], t - 3)
                    nc.vector.reciprocal(rsum2[p][:, 1, :], rsum2[p][:, 0, :]).then_inc(s["rsum2_done"], 1)
            run_steps(dve, step, n_graphs, LAG, PEEL)


def routing_sizes(n_tokens):
    capacity = n_tokens + W
    most = (2 * n_tokens + EXPERTS * (W - 1)) // W
    return capacity, most + most % 2


def graph_phase(nc, sem, sh, adj_in, w, experts, n_graphs):
    groups = n_graphs // GB
    capacity, _ = routing_sizes(n_graphs * T)
    with ExitStack() as ctx:
        def sb(name, shape, dt=F32):
            return ctx.enter_context(nc.sbuf_tensor(name, shape, dt))

        def two(name, shape, dt=F32):
            return [sb(f"{name}{i}", shape, dt) for i in range(2)]

        def ps(name, shape):
            return ctx.enter_context(nc.psum_tensor(name, shape, F32))

        X = sh.X
        wroot1, wrel1, wroot2, wrel2 = (sb(f"g_{n}", [D, D]) for n in ("wroot1", "wrel1", "wroot2", "wrel2"))
        adj = two("g_adj", [T, GB, T], I32)
        edge = two("g_edge", [T, GB, T])
        ones = sb("g_ones", [T, 1])
        carrier, spare = sb("g_carrier", [T, 1]), sb("g_spare", [T, 2])
        rdeg = two("g_rdeg", [T, 2, GB])
        stats = sb("g_stats", [T, 2 * GB, 6])
        meanvar = two("g_meanvar", [T, 2 * GB, 2])
        rstd = two("g_rstd", [T, 2, 2 * GB])
        z = two("g_z", [T, GB, D])
        zT, hT = sb("g_zT", [D, W]), sb("g_hT", [D, W])
        y1, sum1, below1, exp1, above1 = (sb(f"g_{n}1", [T, GB, D]) for n in ("y", "sum", "below", "exp", "above"))
        y2, sum2, below2, exp2, above2 = (sb(f"g_{n}2", [T, GB, D]) for n in ("y", "sum", "below", "exp", "above"))
        h = sb("g_h", [T, GB, D])
        elu2 = two("g_elu2", [T, GB, D])
        wr = sb("r_wr", [D, EXPERTS])
        before = sb("r_before", [T, T], BF16)
        number = sb("r_number", [T, EXPERTS])
        number_i = sb("r_number_i", [T, 2, EXPERTS], I32)
        region = sb("r_region", [T, EXPERTS])
        zr = two("r_z", [T, GB, D])
        zrT = sb("r_zT", [D, W])
        logits = sb("r_logits", [T, GB, EXPERTS])
        best = sb("r_best", [T, GB, EXPERTS])
        which = sb("r_which", [T, GB, EXPERTS], U32)
        which_f = sb("r_which_f", [T, 2, GB])
        chosen = sb("r_chosen", [T, 2, GB, EXPERTS])
        either = sb("r_either", [T, GB, EXPERTS], BF16)
        taken = sb("r_taken", [T, GB + 1, EXPERTS])
        place = sb("r_place", [T, 3, GB, EXPERTS])
        place_of = sb("r_place_of", [T, 2, GB, EXPERTS])
        rows_f = sb("r_rows_f", [T, 2, GB])
        rows = two("r_rows", [T, 2 * GB], U32)
        ps_z, ps_h = ps("g_ps_z", [D, W]), ps("g_ps_h", [D, W])
        ps_y, ps_r1, ps_g1, ps_r2, ps_g2 = (ps(f"g_ps_{n}", [T, GB, D]) for n in ("y", "r1", "g1", "r2", "g2"))
        ps_r = ps("r_ps_r", [T, 4, GB, EXPERTS])
        ps_deg = ps_r[:, 3, :, 0]
        names = ("w_loaded experts_loaded ones_set edge_done degree_summed degree_done rdeg_done stats_done meanvar_done eps_added "
                 "rstd_done z_done z_turned zT_done y1_made y1_done root1_done gathered1 sum1_done below1_done exp1_done "
                 "above1_done h_done h_turned hT_done y2_made y2_done root2_done root2_copied root1_copied gathered2 sum2_done below2_done "
                 "exp2_done above2_done elu2_done x_done numbered before_set setup zr_done zr_turned zrT_done "
                 "logits_done copied carried spare_done best_done which_done whichf_done chosen_done either_done "
                 "ranked taken_step place_step placed_done rowsf_done rows_done kept").split()
        s = {n: sem(f"g_{n}") for n in names}
        adj_loaded = [sem(f"g_adj_loaded{i}") for i in range(2)]
        scattered = [sem(f"g_scattered{i}") for i in range(2)]
        block = ctx.enter_context(nc.Block())
        adj_g = adj_in.rearrange("(g b) n d -> g n b d", b=GB)
        LAG, PEEL = 6, 8

        @block.sync
        def _(sp):
            for tile, a in ((wroot1, w["w_root1"]), (wrel1, w["w_rel1"][1]), (wroot2, w["w_root2"]),
                            (wrel2, w["w_rel2"][1]), (wr, experts["Wr"])):
                sp.dma_start(tile[:, :], a, allow_slow_non_contiguous=True).then_inc(s["w_loaded"], 16)

            def step(t, r, p, known):
                if since(known, 2):
                    sp.wait_ge(s["edge_done"], t - 1)
                sp.dma_start(adj[p][:, :, :], adj_g[t]).then_inc(adj_loaded[p], 16)
            run_steps(sp, step, groups, 0, PEEL)
            sp.dma_start(sh.expert_w1[:, :, :], experts["W1p"].rearrange("e d f -> d e f")).then_inc(s["experts_loaded"], 16)
            sp.dma_start(sh.expert_b1[:, :, :], experts["b1p"].rearrange("e (c p) -> p e c", p=128),
                         allow_slow_non_contiguous=True).then_inc(s["experts_loaded"], 16)
            for c in range(FC):
                sp.dma_start(sh.expert_w2[:, :, c * D:(c + 1) * D], experts["W2p"][:, c * 128:(c + 1) * 128, :]
                             .rearrange("e p d -> p e d")).then_inc(s["experts_loaded"], 16)
            sp.wait_ge(s["experts_loaded"], 16 * (2 + FC))

        @block.gpsimd
        def _(pool):
            nc.gpsimd.memset(meanvar[0][:, :, :], 1.0)
            nc.gpsimd.memset(meanvar[1][:, :, :], 1.0)
            nc.gpsimd.memset(ones[:, :], 1.0).then_inc(s["ones_set"], 1)
            nc.gpsimd.iota(number_i[:, 0, :], pattern=[[1, EXPERTS]], base=0, channel_multiplier=0)
            nc.gpsimd.iota(number_i[:, 1, :], pattern=[[capacity // 8, EXPERTS]], base=0, channel_multiplier=0)\
              .then_inc(s["numbered"], 1)
            nc.gpsimd.memset(before[:, :], 1.0).then_inc(s["before_set"], 1)
            pool.wait_ge(s["before_set"], 1)
            nc.gpsimd.affine_select(out=before[:, :], in_=before[:, :], compare_op=ALU.is_ge, fill=0.0, base=-1,
                                    pattern=[[1, T]], channel_multiplier=-1).then_inc(s["before_set"], 1)

            def step(t, r, p, known):
                if live(known, 3, groups):
                    pool.wait_ge(s["elu2_done"], t - 2)
                    at = X[:, bass.ds((t - 3) * GB, GB), :]
                    nc.gpsimd.tensor_tensor(at, at, elu2[1 - p][:, :, :], ALU.add).then_inc(s["x_done"], 1)
                measured = live(known, 0, groups) or live(known, 4, groups)
                if measured:
                    pool.wait_ge(s["meanvar_done"], t + 1)
                    if since(known, 2):
                        pool.wait_ge(s["z_done"], t - 1 if known is None else min(known - 1, groups))
                    if since(known, 6):
                        pool.wait_ge(s["zr_done"], t - 5)
                    nc.gpsimd.tensor_tensor(rstd[p][:, 1, :], meanvar[p][:, :, 1], sh.eps[:, :],
                                            ALU.add).then_inc(s["eps_added"], 1)
                    pool.wait_ge(s["eps_added"], t + 1)
                    nc.gpsimd.tensor_tensor(rstd[p][:, 0, :], rstd[p][:, 1, :], sh.half_power[:, :],
                                            ALU.pow).then_inc(s["rstd_done"], 1)
                if live(known, 6, groups):
                    if since(known, 8):
                        pool.wait_ge(s["spare_done"], t - 7)
                    pool.wait_ge(s["rows_done"], t - 5)
                    nc.gpsimd.tensor_tensor(spare[:, p:p + 1], ones[:, :], ones[:, :], ALU.add)\
                      .then_inc(s["spare_done"], 1)
                    for e in range(2):
                        for b in range(GB):
                            nc.gpsimd.indirect_dma_start(
                                sh.sorted_z, bass.IndirectOffsetOnAxis(ap=rows[p][:, e * GB + b:e * GB + b + 1], axis=0),
                                zr[p][:, b, :], None).then_inc(scattered[p], 16)
            run_steps(pool, step, groups, LAG, PEEL)
            for p in range(2):
                pool.wait_ge(scattered[p], groups // 2 * 2 * GB * 16)

        @block.tensor
        def _(pe):
            pe.wait_ge(s["w_loaded"], 80)
            pe.wait_ge(s["before_set"], 2)
            pe.wait_ge(s["ones_set"], 1)

            def step(t, r, p, known):
                q = 1 - p
                if live(known, 1, groups):
                    pe.wait_ge(s["z_done"], t)
                    if since(known, 2):
                        pe.wait_ge(s["zT_done"], t - 1)
                    if since(known, 6):
                        pe.wait_ge(s["zrT_done"], t - 5)
                    for b in range(GB):
                        last = nc.tensor.transpose(ps_z[:, b * T:(b + 1) * T], z[q][:, b, :], sh.ident[:, :])
                    last.then_inc(s["z_turned"], 1)
                if live(known, 1, groups):
                    pe.wait_ge(s["zT_done"], t)
                    if since(known, 3):
                        pe.wait_ge(s["y2_done"], t - 2)
                    for b in range(GB):
                        last = nc.tensor.matmul(ps_y[:, b, :], zT[:, b * T:(b + 1) * T], wrel1[:, :],
                                                start=True, stop=True)
                    last.then_inc(s["y1_made"], 1)
                if live(known, 6, groups):
                    pe.wait_ge(s["either_done"], t - 5)
                    if live(known, 1, groups):
                        pe.wait_ge(s["degree_done"], t)
                    nc.tensor.matmul(ps_r[:, 1, :, :], before[:, :], either[:, :, :], start=True, stop=True)
                    nc.tensor.matmul(ps_r[:, 2, :, :], sh.ones_bf[:, :], either[:, :, :], start=True,
                                     stop=True).then_inc(s["ranked"], 1)
                if live(known, 1, groups):
                    if since(known, 2):
                        pe.wait_ge(s["root1_copied"], t - 1)
                    nc.tensor.matmul(ps_r1[:, :, :], sh.ones_bf[:, :],
                                     sh.conv1_bias[:, :].unsqueeze(1).to_broadcast([128, GB, D]), start=True,
                                     stop=False)
                    for b in range(GB):
                        last = nc.tensor.matmul(ps_r1[:, b, :], zT[:, b * T:(b + 1) * T], wroot1[:, :], start=False,
                                                stop=(b == GB - 1))
                    last.then_inc(s["root1_done"], 1)
                if live(known, 2, groups):
                    pe.wait_ge(s["h_done"], t - 1)
                    if since(known, 3):
                        pe.wait_ge(s["hT_done"], t - 2)
                    for b in range(GB):
                        last = nc.tensor.transpose(ps_h[:, b * T:(b + 1) * T], h[:, b, :], sh.ident[:, :])
                    last.then_inc(s["h_turned"], 1)
                if live(known, 1, groups):
                    pe.wait_ge(s["y1_done"], t)
                    if since(known, 2):
                        pe.wait_ge(s["sum1_done"], t - 1)
                    for b in range(GB):
                        last = nc.tensor.matmul(ps_g1[:, b, :], edge[q][:, b, :], y1[:, b, :], start=True, stop=True)
                    last.then_inc(s["gathered1"], 1)
                if live(known, 2, groups):
                    pe.wait_ge(s["hT_done"], t - 1)
                    pe.wait_ge(s["y1_done"], t if known is None else min(known, groups))
                    for b in range(GB):
                        last = nc.tensor.matmul(ps_y[:, b, :], hT[:, b * T:(b + 1) * T], wrel2[:, :],
                                                start=True, stop=True)
                    last.then_inc(s["y2_made"], 1)
                if live(known, 2, groups):
                    if since(known, 3):
                        pe.wait_ge(s["root2_copied"], t - 2)
                    nc.tensor.matmul(ps_r2[:, :, :], sh.ones_bf[:, :],
                                     sh.conv2_bias[:, :].unsqueeze(1).to_broadcast([128, GB, D]), start=True,
                                     stop=False)
                    for b in range(GB):
                        last = nc.tensor.matmul(ps_r2[:, b, :], hT[:, b * T:(b + 1) * T], wroot2[:, :], start=False,
                                                stop=(b == GB - 1))
                    last.then_inc(s["root2_done"], 1)
                if live(known, 5, groups):
                    pe.wait_ge(s["zr_done"], t - 4)
                    if live(known, 1, groups):
                        pe.wait_ge(s["zT_done"], t)
                    elif known is not None:
                        pe.wait_ge(s["zT_done"], groups)
                        pe.wait_ge(s["zrT_done"], t - 5)
                    for b in range(GB):
                        last = nc.tensor.transpose(ps_z[:, b * T:(b + 1) * T], zr[q][:, b, :], sh.ident[:, :])
                    last.then_inc(s["zr_turned"], 1)
                if live(known, 2, groups):
                    pe.wait_ge(s["y2_done"], t - 1)
                    if since(known, 3):
                        pe.wait_ge(s["sum2_done"], t - 2)
                    for b in range(GB):
                        last = nc.tensor.matmul(ps_g2[:, b, :], edge[p][:, b, :], y2[:, b, :], start=True, stop=True)
                    last.then_inc(s["gathered2"], 1)
                if live(known, 5, groups):
                    pe.wait_ge(s["zrT_done"], t - 4)
                    if since(known, 6):
                        pe.wait_ge(s["taken_step"], (t - 5) * GB)
                        pe.wait_ge(s["place_step"], (t - 5) * 2)
                    if live(known, 1, groups):
                        pe.wait_ge(s["degree_done"], t)
                    for b in range(GB):
                        last = nc.tensor.matmul(ps_r[:, 0, b, :], zrT[:, b * T:(b + 1) * T], wr[:, :],
                                                start=True, stop=True)
                    last.then_inc(s["logits_done"], 1)
                if live(known, 0, groups):
                    pe.wait_ge(s["edge_done"], t + 1)
                    if since(known, 1):
                        pe.wait_ge(s["degree_done"], t)
                    for b in range(GB):
                        last = nc.tensor.matmul(ps_deg[:, b:b + 1], edge[p][:, b, :], ones[:, :], start=True, stop=True)
                    last.then_inc(s["degree_summed"], 1)
            run_steps(pe, step, groups, LAG, PEEL)

        @block.scalar
        def _(act):
            act.wait_ge(s["w_loaded"], 80)

            def step(t, r, p, known):
                if live(known, 1, groups):
                    act.wait_ge(s["z_turned"], t)
                    if since(known, 2):
                        act.wait_ge(s["root1_done"], t - 1)
                    nc.scalar.activation(zT[:, :], ps_z[:, :], ACT.Copy).then_inc(s["zT_done"], 1)
                if live(known, 1, groups):
                    act.wait_ge(s["y1_made"], t)
                    if since(known, 2):
                        act.wait_ge(s["gathered1"], t - 1)
                    nc.scalar.activation(y1[:, :, :], ps_y[:, :, :], ACT.Copy).then_inc(s["y1_done"], 1)
                if live(known, 1, groups):
                    act.wait_ge(s["root1_done"], t)
                    if since(known, 2):
                        act.wait_ge(s["above1_done"], t - 1)
                    nc.scalar.activation(sum1[:, :, :], ps_r1[:, :, :], ACT.Copy).then_inc(s["root1_copied"], 1)
                if live(known, 2, groups):
                    act.wait_ge(s["h_turned"], t - 1)
                    if since(known, 3):
                        act.wait_ge(s["root2_done"], t - 2)
                    nc.scalar.activation(hT[:, :], ps_h[:, :], ACT.Copy).then_inc(s["hT_done"], 1)
                if live(known, 2, groups):
                    act.wait_ge(s["y2_made"], t - 1)
                    if since(known, 3):
                        act.wait_ge(s["gathered2"], t - 2)
                    nc.scalar.activation(y2[:, :, :], ps_y[:, :, :], ACT.Copy).then_inc(s["y2_done"], 1)
                if live(known, 1, groups):
                    act.wait_ge(s["sum1_done"], t)
                    if since(known, 2):
                        act.wait_ge(s["exp1_done"], t - 1)
                        act.wait_ge(s["h_done"], t - 1)
                    nc.scalar.activation(below1[:, :, :], sum1[:, :, :], ACT.Relu, scale=-1.0).then_inc(s["below1_done"], 1)
                    nc.scalar.activation(above1[:, :, :], sum1[:, :, :], ACT.Relu).then_inc(s["above1_done"], 1)
                    act.wait_ge(s["below1_done"], t)
                    nc.scalar.activation(exp1[:, :, :], below1[:, :, :], ACT.Exp, scale=-1.0).then_inc(s["exp1_done"], 1)
                if live(known, 2, groups):
                    act.wait_ge(s["root2_done"], t - 1)
                    if since(known, 3):
                        act.wait_ge(s["above2_done"], t - 2)
                    nc.scalar.activation(sum2[:, :, :], ps_r2[:, :, :], ACT.Copy).then_inc(s["root2_copied"], 1)
                if live(known, 5, groups):
                    act.wait_ge(s["zr_turned"], t - 4)
                    if since(known, 6):
                        act.wait_ge(s["logits_done"], t - 5)
                    nc.scalar.activation(zrT[:, :], ps_z[:, :], ACT.Copy).then_inc(s["zrT_done"], 1)
                if live(known, 2, groups):
                    act.wait_ge(s["sum2_done"], t - 1)
                    if since(known, 3):
                        act.wait_ge(s["exp2_done"], t - 2)
                        act.wait_ge(s["elu2_done"], t - 2)
                    nc.scalar.activation(below2[:, :, :], sum2[:, :, :], ACT.Relu, scale=-1.0).then_inc(s["below2_done"], 1)
                    nc.scalar.activation(above2[:, :, :], sum2[:, :, :], ACT.Relu).then_inc(s["above2_done"], 1)
                    act.wait_ge(s["below2_done"], t - 1)
                    nc.scalar.activation(exp2[:, :, :], below2[:, :, :], ACT.Exp, scale=-1.0).then_inc(s["exp2_done"], 1)
            run_steps(act, step, groups, LAG, PEEL)

        @block.vector
        def _(dve):
            dve.wait_ge(s["w_loaded"], 80)
            dve.wait_ge(s["numbered"], 1)
            nc.vector.tensor_copy(number[:, :], number_i[:, 0, :])
            nc.vector.tensor_scalar(region[:, :], number_i[:, 1, :], 8.0, None, ALU.mult)
            nc.vector.memset(taken[:, :, :], 0.0).then_inc(s["setup"], 1)
            dve.wait_ge(s["setup"], 1)
            dve.wait_ge(s["ones_set"], 1)

            def normalized(out, g, own, first, done):
                for b in range(GB):
                    last = nc.vector.tensor_scalar(out[:, b, :], X[:, bass.ds(g * GB + b, 1), :].squeeze(1),
                                                   meanvar[own][:, first + b, 0:1], rstd[own][:, 0, first + b:first + b + 1],
                                                   ALU.subtract, ALU.mult)
                last.then_inc(done, 1)

            def summed(out, gathered, own, done):
                for b in range(GB):
                    last = nc.vector.scalar_tensor_tensor(out=out[:, b, :], in0=gathered[:, b, :],
                                                          scalar=rdeg[own][:, 1, b:b + 1], in1=out[:, b, :],
                                                          op0=ALU.mult, op1=ALU.add)
                last.then_inc(done, 1)

            def step(t, r, p, known):
                q = 1 - p
                measured = live(known, 0, groups) or live(known, 4, groups)
                if measured:
                    if since(known, 1):
                        dve.wait_ge(s["meanvar_done"], t)
                    if live(known, 0, groups):
                        for b in range(GB):
                            last = nc.vector.bn_stats(stats[:, b, :], X[:, bass.ds(t * GB + b, 1), :].squeeze(1))
                    if live(known, 4, groups):
                        dve.wait_ge(s["x_done"], t - 3)
                        for b in range(GB):
                            last = nc.vector.bn_stats(stats[:, GB + b, :], X[:, bass.ds((t - 4) * GB + b, 1), :].squeeze(1))
                    last.then_inc(s["stats_done"], 1)
                if measured:
                    dve.wait_ge(s["stats_done"], t + 1)
                    nc.vector.tensor_copy(carrier[:, :], ones[:, :])
                    if live(known, 0, groups):
                        for b in range(GB):
                            last = nc.vector.bn_aggr(meanvar[p][:, b, :], stats[:, b, :])
                    if live(known, 4, groups):
                        for b in range(GB):
                            last = nc.vector.bn_aggr(meanvar[p][:, GB + b, :], stats[:, GB + b, :])
                    last.then_inc(s["meanvar_done"], 1)
                if live(known, 6, groups):
                    g = t - 6
                    dve.wait_ge(s["ranked"], g + 1)
                    dve.wait_ge(s["carried"], g + 1)
                    for b in range(GB):
                        if b:
                            dve.wait_ge(s["taken_step"], g * GB + b)
                        nc.vector.tensor_tensor(taken[:, b + 1, :], taken[:, b, :], ps_r[:, 2, b, :],
                                                ALU.add).then_inc(s["taken_step"], 1)
                    dve.wait_ge(s["taken_step"], (g + 1) * GB)
                    nc.vector.tensor_tensor(place[:, 0, :, :], ps_r[:, 1, :, :], taken[:, 0:GB, :],
                                            ALU.add).then_inc(s["place_step"], 1)
                    dve.wait_ge(s["place_step"], g * 2 + 1)
                    nc.vector.tensor_tensor(place[:, 1, :, :], place[:, 0, :, :],
                                            region[:, :].unsqueeze(1).to_broadcast([T, GB, EXPERTS]),
                                            ALU.add).then_inc(s["place_step"], 1)
                    dve.wait_ge(s["place_step"], g * 2 + 2)
                    nc.vector.tensor_tensor(place_of[:, 0, :, :], chosen[:, 0, :, :], place[:, 1, :, :], ALU.mult)
                    nc.vector.tensor_tensor(place_of[:, 1, :, :], chosen[:, 1, :, :], place[:, 1, :, :],
                                            ALU.mult).then_inc(s["placed_done"], 1)
                    dve.wait_ge(s["placed_done"], g + 1)
                    nc.vector.reduce_sum(rows_f[:, :, :].rearrange("p e b -> p (e b)"),
                                         place_of[:, :, :, :].rearrange("p e b x -> p (e b) x"),
                                         AX.X).then_inc(s["rowsf_done"], 1)
                    dve.wait_ge(s["rowsf_done"], g + 1)
                    nc.vector.tensor_copy(sh.row_of[:, bass.ds(g, 1), :].squeeze(1),
                                          rows_f[:, :, :].rearrange("p e b -> p (e b)")).then_inc(s["kept"], 1)
                    nc.vector.tensor_copy(rows[p][:, :],
                                          rows_f[:, :, :].rearrange("p e b -> p (e b)")).then_inc(s["rows_done"], 1)
                if live(known, 1, groups):
                    dve.wait_ge(s["gathered1"], t)
                    dve.wait_ge(s["root1_copied"], t)
                    dve.wait_ge(s["rdeg_done"], t)
                    summed(sum1, ps_g1, q, s["sum1_done"])
                if live(known, 5, groups):
                    dve.wait_ge(s["rstd_done"], t)
                    if since(known, 7):
                        dve.wait_ge(scattered[q], (r + p - 3) * 2 * GB * 16)
                    nc.vector.tensor_copy(sh.mean[:, bass.ds((t - 5) * GB, GB)], meanvar[q][:, GB:2 * GB, 0])
                    nc.vector.tensor_copy(sh.rstd[:, bass.ds((t - 5) * GB, GB)], rstd[q][:, 0, GB:2 * GB])
                    normalized(zr[q], t - 5, q, GB, s["zr_done"])
                if live(known, 1, groups):
                    dve.wait_ge(s["exp1_done"], t)
                    dve.wait_ge(s["above1_done"], t)
                    if since(known, 2):
                        dve.wait_ge(s["h_turned"], t - 1)
                    nc.vector.scalar_tensor_tensor(out=h[:, :, :], in0=exp1[:, :, :], scalar=-1.0,
                                                   in1=above1[:, :, :], op0=ALU.add, op1=ALU.add)\
                      .then_inc(s["h_done"], 1)
                if live(known, 2, groups):
                    dve.wait_ge(s["gathered2"], t - 1)
                    dve.wait_ge(s["root2_copied"], t - 1)
                    summed(sum2, ps_g2, p, s["sum2_done"])
                if live(known, 0, groups):
                    dve.wait_ge(adj_loaded[p], (r + 1) * 16)
                    if since(known, 2):
                        dve.wait_ge(s["gathered2"], t - 1)
                    nc.vector.tensor_scalar(edge[p][:, :, :], adj[p][:, :, :], 1.0, None,
                                            ALU.is_equal).then_inc(s["edge_done"], 1)
                if live(known, 0, groups):
                    dve.wait_ge(s["rstd_done"], t + 1)
                    if since(known, 2):
                        dve.wait_ge(s["z_turned"], t - 1)
                    normalized(z[p], t, p, 0, s["z_done"])
                if live(known, 0, groups):
                    dve.wait_ge(s["degree_summed"], t + 1)
                    nc.vector.tensor_scalar(rdeg[p][:, 0, :], ps_deg, 1.0, None, ALU.max).then_inc(s["degree_done"], 1)
                if live(known, 5, groups):
                    g = t - 5
                    dve.wait_ge(s["logits_done"], g + 1)
                    if live(known, 0, groups):
                        dve.wait_ge(s["degree_summed"], t + 1)
                    nc.vector.tensor_copy(logits[:, :, :], ps_r[:, 0, :, :]).then_inc(s["copied"], 1)
                    dve.wait_ge(s["copied"], g + 1)
                    nc.vector.tensor_copy(taken[:, 0, :], taken[:, GB, :]).then_inc(s["carried"], 1)
                    for b in range(GB):
                        last = nc.vector.max(best[:, b, :], logits[:, b, :])
                    last.then_inc(s["best_done"], 1)
                    dve.wait_ge(s["best_done"], g + 1)
                    nc.vector.tensor_tensor(sh.gap[:, bass.ds(g * GB, GB)], best[:, :, 1], best[:, :, 0],
                                            ALU.subtract)
                    for b in range(GB):
                        last = nc.vector.max_index(which[:, b, :], best[:, b, :], logits[:, b, :])
                    last.then_inc(s["which_done"], 1)
                    dve.wait_ge(s["which_done"], g + 1)
                    nc.vector.tensor_copy(which_f[:, :, :], which[:, :, 0:2].rearrange("p b e -> p e b"))\
                      .then_inc(s["whichf_done"], 1)
                    dve.wait_ge(s["whichf_done"], g + 1)
                    nc.vector.tensor_copy(sh.expert_of[:, bass.ds(g, 1), :].squeeze(1),
                                          which_f[:, :, :].rearrange("p e b -> p (e b)"))
                    nc.vector.tensor_tensor(
                        chosen[:, :, :, :].rearrange("p e b x -> p (e b) x"),
                        which_f[:, :, :].rearrange("p e b -> p (e b)").unsqueeze(2).to_broadcast([T, 2 * GB, EXPERTS]),
                        number[:, :].unsqueeze(1).to_broadcast([T, 2 * GB, EXPERTS]),
                        ALU.is_equal).then_inc(s["chosen_done"], 1)
                    dve.wait_ge(s["chosen_done"], g + 1)
                    nc.vector.tensor_tensor(either[:, :, :], chosen[:, 0, :, :], chosen[:, 1, :, :],
                                            ALU.add).then_inc(s["either_done"], 1)
                if live(known, 2, groups):
                    dve.wait_ge(s["exp2_done"], t - 1)
                    dve.wait_ge(s["above2_done"], t - 1)
                    if since(known, 4):
                        dve.wait_ge(s["x_done"], t - 3)
                    nc.vector.scalar_tensor_tensor(out=elu2[p][:, :, :], in0=exp2[:, :, :], scalar=-1.0,
                                                   in1=above2[:, :, :], op0=ALU.add, op1=ALU.add)\
                      .then_inc(s["elu2_done"], 1)
                if live(known, 0, groups):
                    dve.wait_ge(s["degree_done"], t + 1)
                    nc.vector.reciprocal(rdeg[p][:, 1, :], rdeg[p][:, 0, :]).then_inc(s["rdeg_done"], 1)
            run_steps(dve, step, groups, LAG, PEEL)
            dve.wait_ge(s["kept"], groups)
            nc.vector.tensor_copy(sh.counts[:, :], taken[:, GB, :]).then_inc(s["setup"], 1)
            dve.wait_ge(s["setup"], 2)


def schedule_phase(nc, sem, sh, n_graphs):
    capacity, n_groups = routing_sizes(n_graphs * T)
    spans = capacity // W
    E = EXPERTS
    with ExitStack() as ctx:
        def sb(name, shape, dt=F32):
            return ctx.enter_context(nc.sbuf_tensor(name, shape, dt))

        edges_i = sb("p_edges_i", [T, spans], I32)
        groups_i = sb("p_groups_i", [1, n_groups], I32)
        region_i = sb("p_region_i", [T, E], I32)
        edges, group = sb("p_edges", [T, spans]), sb("p_group", [1, n_groups])
        region = sb("p_region", [T, E])
        full = sb("p_full", [T, E, spans])
        size = sb("p_size", [T, E])
        end = sb("p_end", [T, E + 1])
        past = sb("p_past", [1, n_groups, E])
        mine = sb("p_mine", [1, n_groups, E])
        shift = sb("p_shift", [T, E])
        expert = sb("p_expert", [1, 2, n_groups])
        unused = sb("p_unused", [1, n_groups])
        base = sb("p_base", [1, 5, n_groups])
        back = sb("p_back", [T, 2, n_graphs // GB * 2 * GB])
        tail = sb("p_tail", [T, E])
        tail_i = sb("p_tail_i", [T, E], I32)
        zeros = sb("p_zeros", [T, GB * D])
        odds = sb("p_odds", [T, 2, n_graphs])

        numbered = sem("p_numbered")
        done = sem("p_done")
        tails_ready = sem("p_tails_ready")
        zero_set = sem("p_zero_set")
        odds_done = sem("p_odds_done")
        filled = sem("p_filled")
        block = ctx.enter_context(nc.Block())

        @block.gpsimd
        def _(pool):
            nc.gpsimd.iota(edges_i[:, :], pattern=[[W, spans]], base=0, channel_multiplier=0)
            nc.gpsimd.iota(groups_i[:, :], pattern=[[1, n_groups]], base=0, channel_multiplier=0)
            nc.gpsimd.iota(region_i[:, :], pattern=[[capacity // 8, E]], base=0, channel_multiplier=0)\
              .then_inc(numbered, 1)

        @block.scalar
        def _(act):
            nc.scalar.activation(odds[:, 0, :], sh.gap[:, :], ACT.Exp).then_inc(odds_done, 1)

        @block.vector
        def _(dve):
            n = [0]

            def after(ins):
                n[0] += 1
                ins.then_inc(done, 1)
                dve.wait_ge(done, n[0])

            nc.vector.memset(zeros[:, :], 0.0).then_inc(zero_set, 1)
            dve.wait_ge(numbered, 1)
            nc.vector.tensor_copy(edges[:, :], edges_i[:, :])
            nc.vector.tensor_copy(group[:, :], groups_i[:, :])
            after(nc.vector.tensor_scalar(region[:, :], region_i[:, :], 8.0, None, ALU.mult))
            after(nc.vector.tensor_tensor(tail[:, :], region[:, :], sh.counts[:, :], ALU.add))
            nc.vector.tensor_copy(tail_i[:, :], tail[:, :]).then_inc(tails_ready, 1)
            after(nc.vector.tensor_tensor(full[:, :, :], edges[:, :].unsqueeze(1).to_broadcast([T, E, spans]),
                                          sh.counts[:, :].unsqueeze(2).to_broadcast([T, E, spans]), ALU.is_lt))
            nc.vector.memset(end[:, :], 0.0)
            after(nc.vector.reduce_sum(size[:, :], full[:, :, :], AX.X))
            for e in range(E):
                after(nc.vector.tensor_tensor(end[:, e + 1:e + 2], end[:, e:e + 1], size[:, e:e + 1], ALU.add))
            groups_by = group[:, :].unsqueeze(2).to_broadcast([1, n_groups, E])
            after(nc.vector.tensor_tensor(past[:, :, :], end[0:1, 1:E + 1].unsqueeze(1).to_broadcast([1, n_groups, E]),
                                          groups_by, ALU.is_le))
            after(nc.vector.reduce_sum(expert[:, 0, :], past[:, :, :], AX.X))
            nc.vector.tensor_scalar(unused[:, :], expert[:, 0, :], float(E), None, ALU.is_ge)
            after(nc.vector.tensor_scalar(shift[:, :], end[:, 0:E], -float(W), None, ALU.mult))
            after(nc.vector.tensor_tensor(shift[:, :], shift[:, :], region[:, :], ALU.add))
            after(nc.vector.tensor_tensor(mine[:, :, :], end[0:1, 0:E].unsqueeze(1).to_broadcast([1, n_groups, E]),
                                          groups_by, ALU.is_le))
            after(nc.vector.tensor_tensor(mine[:, :, :], mine[:, :, :], past[:, :, :], ALU.subtract))
            after(nc.vector.tensor_tensor(mine[:, :, :], mine[:, :, :],
                                          shift[0:1, :].unsqueeze(1).to_broadcast([1, n_groups, E]), ALU.mult))
            after(nc.vector.reduce_sum(base[:, 0, :], mine[:, :, :], AX.X))
            after(nc.vector.tensor_scalar(base[:, 1, :], group[:, :], float(W), None, ALU.mult))
            after(nc.vector.tensor_tensor(base[:, 2, :], base[:, 0, :], base[:, 1, :], ALU.add))
            after(nc.vector.tensor_scalar(base[:, 3, :], unused[:, :], -1.0, 1.0, ALU.mult, ALU.add))
            after(nc.vector.tensor_tensor(base[:, 2, :], base[:, 2, :], base[:, 3, :], ALU.mult))
            after(nc.vector.scalar_tensor_tensor(out=base[:, 4, :], in0=unused[:, :], scalar=float(E * capacity),
                                                 in1=base[:, 2, :], op0=ALU.mult, op1=ALU.add))
            after(nc.vector.tensor_scalar(expert[:, 1, :], expert[:, 0, :], float(E - 1), None, ALU.min))
            nc.vector.tensor_copy(sh.plan[:, 0, :], expert[:, 1, :])
            after(nc.vector.tensor_copy(sh.plan[:, 1, :], base[:, 4, :]))
            experts_of = sh.expert_of[:, :, :].rearrange("p g i -> p (g i)")
            rows_of = sh.row_of[:, :, :].rearrange("p g i -> p (g i)")
            for e in range(E):
                after(nc.vector.tensor_scalar(back[:, e % 2, :], experts_of, float(e), shift[:, e:e + 1],
                                              ALU.is_equal, ALU.mult))
                after(nc.vector.tensor_tensor(rows_of, rows_of, back[:, e % 2, :], ALU.subtract))
            dve.wait_ge(odds_done, 1)
            after(nc.vector.tensor_scalar(odds[:, 1, :], odds[:, 0, :], 1.0, None, ALU.add))
            after(nc.vector.reciprocal(sh.gate[:, 0, :], odds[:, 1, :]))
            after(nc.vector.tensor_tensor(sh.gate[:, 1, :], odds[:, 0, :], sh.gate[:, 0, :], ALU.mult))

        @block.sync
        def _(sp):
            sp.wait_ge(zero_set, 1)
            rows = lambda start: sh.sorted_z[bass.ds(start, W), :].rearrange("(p b) d -> p (b d)", b=GB)
            sp.dma_start(rows(E * capacity), zeros[:, :]).then_inc(filled, 16)
            sp.wait_ge(tails_ready, 1)
            for e in range(E):
                start = nc.sync.value_load(tail_i[0:1, e:e + 1], min_val=0, max_val=E * capacity - W)
                sp.dma_start(rows(start), zeros[:, :]).then_inc(filled, 16)
            sp.wait_ge(filled, 16 * (E + 1))


def expert_phase(nc, sem, sh, n_graphs):
    capacity, n_groups = routing_sizes(n_graphs * T)
    with ExitStack() as ctx:
        def sb(name, shape, dt=F32):
            return ctx.enter_context(nc.sbuf_tensor(name, shape, dt))

        def two(name, shape, dt=F32):
            return [sb(f"{name}{i}", shape, dt) for i in range(2)]

        def ps(name, shape):
            return ctx.enter_context(nc.psum_tensor(name, shape, F32))

        w1, w2, b1 = sh.expert_w1, sh.expert_w2, sh.expert_b1
        w1h, w1l = two("e_w1h", [D, FF], F32R), two("e_w1l", [D, FF], F32R)
        w2g, b1g = two("e_w2g", [128, FC * D]), two("e_b1g", [128, FC])
        z = two("e_z", [T, GB, D])
        zTh, zTl = two("e_zTh", [D, W], F32R), two("e_zTl", [D, W], F32R)
        hidden = two("e_hidden", [128, FC, W])
        y = two("e_y", [T, GB, D])
        ps_z = ps("e_ps_z", [D, W])
        ps_1 = [ps(f"e_ps_1{i}", [128, W]) for i in range(2)]
        ps_2 = [ps(f"e_ps_2{i}", [T, GB, D]) for i in range(2)]

        names = ("w1h_done w1_picked w2_picked b1_picked z_turned zTh_done zT_done up_done hidden_done down_done y_done").split()
        s = {n: sem(f"e_{n}") for n in names}
        z_loaded = [sem(f"e_z_loaded{i}") for i in range(2)]
        y_stored = [sem(f"e_y_stored{i}") for i in range(2)]
        block = ctx.enter_context(nc.Block())
        LAG, PEEL = 4, 6

        def rows(tensor, start):
            return tensor[bass.ds(start, W), :].rearrange("(b p) d -> p b d", p=T)

        @block.sync
        def _(sp):
            def step(t, r, p, known):
                if live(known, 0, n_groups):
                    start = nc.sync.value_load(sh.plan[0:1, 1, bass.ds(t, 1)], min_val=0, max_val=EXPERTS * capacity)
                    if since(known, 2):
                        sp.wait_ge(s["z_turned"], t - 1)
                    sp.dma_start(z[p][:, :, :], rows(sh.sorted_z, start)).then_inc(z_loaded[p], 16)
                if live(known, 4, n_groups):
                    sp.wait_ge(s["y_done"], t - 3)
                    sp.dma_start(rows(sh.sorted_y, (t - 4) * W), y[p][:, :, :]).then_inc(y_stored[p], 16)
            run_steps(sp, step, n_groups, LAG, PEEL)
            for p in range(2):
                sp.wait_ge(y_stored[p], n_groups // 2 * 16)

        @block.gpsimd
        def _(pool):
            def step(t, r, p, known):
                q = 1 - p
                if live(known, 1, n_groups):
                    e = nc.gpsimd.value_load(sh.plan[0:1, 0, bass.ds(t - 1, 1)], min_val=0, max_val=EXPERTS - 1)
                    pool.wait_ge(s["w1h_done"], t)
                    nc.gpsimd.tensor_tensor(w1l[q][:, :], w1[:, bass.ds(e, 1), :].squeeze(1), w1h[q][:, :],
                                            ALU.subtract).then_inc(s["w1_picked"], 1)
                    if since(known, 3):
                        pool.wait_ge(s["hidden_done"], (t - 2) * FC)
                    nc.gpsimd.tensor_copy(b1g[q][:, :], b1[:, bass.ds(e, 1), :].squeeze(1)).then_inc(s["b1_picked"], 1)
            run_steps(pool, step, n_groups, LAG, PEEL)

        @block.scalar
        def _(act):
            def step(t, r, p, known):
                for c in range(FC):
                    if c == 2 and live(known, 1, n_groups):
                        act.wait_ge(s["z_turned"], t)
                        if since(known, 3):
                            act.wait_ge(s["up_done"], (t - 2) * FC)
                        nc.scalar.activation(zTh[1 - p][:, :], ps_z[:, :], ACT.Copy).then_inc(s["zTh_done"], 1)
                    if live(known, 2, n_groups):
                        act.wait_ge(s["up_done"], (t - 2) * FC + c + 1)
                        if c == 0:
                            act.wait_ge(s["b1_picked"], t - 1)
                        if c == 0 and since(known, 4):
                            act.wait_ge(s["down_done"], t - 3)
                        nc.scalar.activation(hidden[p][:, c, :], ps_1[c % 2][:, :], ACT.Gelu,
                                             bias=b1g[p][:, c:c + 1]).then_inc(s["hidden_done"], 1)
            run_steps(act, step, n_groups, LAG, PEEL)

        @block.tensor
        def _(pe):
            def step(t, r, p, known):
                q = 1 - p
                for c in range(FC):
                    if live(known, 2, n_groups):
                        if c == 0:
                            pe.wait_ge(s["zT_done"], t - 1)
                            pe.wait_ge(s["w1_picked"], t - 1)
                        if c >= 2 or since(known, 3):
                            pe.wait_ge(s["hidden_done"], (t - 2) * FC + c - 1)
                        ch = slice(c * 128, (c + 1) * 128)
                        split_matmul(nc, ps_1[c % 2][:, :], (w1h[p][:, ch], w1l[p][:, ch]), (zTh[p][:, :], zTl[p][:, :]),
                                     True, True).then_inc(s["up_done"], 1)
                    if c == 1 and live(known, 1, n_groups):
                        pe.wait_ge(z_loaded[q], (r + p) * 16)
                        if since(known, 2):
                            pe.wait_ge(s["zT_done"], t - 1)
                        for b in range(GB):
                            last = nc.tensor.transpose(ps_z[:, b * T:(b + 1) * T], z[q][:, b, :], sh.ident[:, :])
                        last.then_inc(s["z_turned"], 1)
                    if c % 2 == 1 and live(known, 3, n_groups):
                        if c == 1:
                            pe.wait_ge(s["hidden_done"], (t - 2) * FC)
                            pe.wait_ge(s["w2_picked"], t - 2)
                            if since(known, 5):
                                pe.wait_ge(s["y_done"], t - 4)
                        for b in (c - 1, c):
                            for f in range(FC):
                                last = nc.tensor.matmul(ps_2[q][:, b, :], hidden[q][:, f, b * T:(b + 1) * T],
                                                        w2g[q][:, f * D:(f + 1) * D], start=(f == 0), stop=(f == FC - 1))
                        if c == 3:
                            last.then_inc(s["down_done"], 1)
            run_steps(pe, step, n_groups, LAG, PEEL)

        @block.vector
        def _(dve):
            def step(t, r, p, known):
                q = 1 - p
                if live(known, 1, n_groups):
                    e = nc.vector.value_load(sh.plan[0:1, 0, bass.ds(t - 1, 1)], min_val=0, max_val=EXPERTS - 1)
                    if since(known, 3):
                        dve.wait_ge(s["up_done"], (t - 2) * FC)
                    nc.vector.tensor_copy(w1h[q][:, :], w1[:, bass.ds(e, 1), :].squeeze(1)).then_inc(s["w1h_done"], 1)
                if live(known, 2, n_groups):
                    e = nc.vector.value_load(sh.plan[0:1, 0, bass.ds(t - 2, 1)], min_val=0, max_val=EXPERTS - 1)
                    if since(known, 4):
                        dve.wait_ge(s["down_done"], t - 3)
                    nc.vector.tensor_copy(w2g[p][:, :], w2[:, bass.ds(e, 1), :].squeeze(1)).then_inc(s["w2_picked"], 1)
                if live(known, 1, n_groups):
                    dve.wait_ge(s["zTh_done"], t)
                    nc.vector.tensor_tensor(zTl[q][:, :], ps_z[:, :], zTh[q][:, :], ALU.subtract)\
                      .then_inc(s["zT_done"], 1)
                if live(known, 3, n_groups):
                    dve.wait_ge(s["down_done"], t - 2)
                    if since(known, 5):
                        dve.wait_ge(y_stored[q], (r + p - 2) * 16)
                    nc.vector.tensor_copy(y[q][:, :, :], ps_2[q][:, :, :]).then_inc(s["y_done"], 1)
            run_steps(dve, step, n_groups, LAG, PEEL)


def combine_phase(nc, sem, sh, w, out, n_graphs):
    groups = n_graphs // GB
    with ExitStack() as ctx:
        def sb(name, shape, dt=F32):
            return ctx.enter_context(nc.sbuf_tensor(name, shape, dt))

        def two(name, shape, dt=F32):
            return [sb(f"{name}{i}", shape, dt) for i in range(2)]

        def ps(name, shape):
            return ctx.enter_context(nc.psum_tensor(name, shape, F32))

        X = sh.X
        NB2 = EXPERTS + 1
        w1 = sb("c_w1", [D, FF])
        w2 = sb("c_w2", [128, FC, D])
        b1 = sb("c_b1", [128, FC])
        b2 = sb("c_b2", [NB2, D])
        number_i = sb("c_number_i", [T, EXPERTS], I32)
        number = sb("c_number", [T, EXPERTS])
        z = sb("c_z", [T, GB, D])
        spare = sb("c_spare", [T, 2])
        zTh, zTl = two("c_zTh", [D, W], F32R), two("c_zTl", [D, W], F32R)
        w1h, w1l = sb("c_w1h", [D, FF], F32R), sb("c_w1l", [D, FF], F32R)
        chosen = sb("c_chosen", [T, 2 * GB, EXPERTS])
        gated = sb("c_gated", [T, 2 * GB, EXPERTS])
        gates = sb("c_gates", [T, GB, NB2])
        gatesT = two("c_gatesT", [NB2, GB, T])
        hidden = two("c_hidden", [128, FC, W])
        rows = two("c_rows", [T, 2 * GB], U32)
        y = two("c_y", [T, 2 * GB, D])
        ps_z = ps("c_ps_z", [D, W])
        ps_g = ps("c_ps_g", [NB2, GB, T])
        ps_1 = [ps(f"c_ps_1{i}", [128, W]) for i in range(2)]
        ps_2 = [ps(f"c_ps_2{i}", [T, GB, D]) for i in range(2)]

        names = ("w_loaded numbered number_set z_done z_turned zTh_done zT_done "
                 "w1h_done w1_split "
                 "chosen_done gated_done gates_done gates_turned gatesT_done up_done hidden_done down_done rows_done "
                 "shared_added weighted spare_done").split()
        s = {n: sem(f"c_{n}") for n in names}
        y_gathered = [sem(f"c_y_gathered{i}") for i in range(2)]
        stored = sem("c_stored")
        block = ctx.enter_context(nc.Block())
        out_g = out.rearrange("(g b) n d -> g n b d", b=GB)
        LAG, PEEL = 4, 6

        @block.sync
        def _(sp):
            for tile, a in ((w1[:, :], w["W1s"]), (w2[:, :, :], w["W2s"].rearrange("(c p) n -> p c n", p=128)),
                            (b1[:, :], w["b1s"].rearrange("(c p) -> p c", p=128)), (b2[0:EXPERTS, :], w["b2p"]),
                            (b2[EXPERTS:NB2, :], w["b2s"].rearrange("(a n) -> a n", a=1))):
                sp.dma_start(tile, a, allow_slow_non_contiguous=True).then_inc(s["w_loaded"], 16)

            def step(t, r, p, known):
                if live(known, 3, groups):
                    sp.wait_ge(s["shared_added"], t - 2)
                    sp.dma_start(out_g[t - 3], X[:, bass.ds((t - 3) * GB, GB), :]).then_inc(stored, 16)
            run_steps(sp, step, groups, LAG, PEEL)
            sp.wait_ge(stored, 16 * groups)

        @block.gpsimd
        def _(pool):
            nc.gpsimd.iota(number_i[:, :], pattern=[[1, EXPERTS]], base=0, channel_multiplier=0)\
              .then_inc(s["numbered"], 1)

            def step(t, r, p, known):
                q = 1 - p

                if live(known, 1, groups):
                    if since(known, 3):
                        pool.wait_ge(s["weighted"], (t - 2) * 2 * GB)
                        pool.wait_ge(s["spare_done"], t - 2)
                    pool.wait_ge(s["rows_done"], t)
                    nc.gpsimd.tensor_tensor(spare[:, p:p + 1], sh.eps[:, 0:1], sh.eps[:, 0:1], ALU.add)\
                      .then_inc(s["spare_done"], 1)
                    for i in range(2 * GB):
                        nc.gpsimd.indirect_dma_start(
                            y[q][:, i, :], None, sh.sorted_y,
                            bass.IndirectOffsetOnAxis(ap=rows[q][:, i:i + 1], axis=0)).then_inc(y_gathered[q], 16)
            run_steps(pool, step, groups, LAG, PEEL)

        @block.scalar
        def _(act):
            act.wait_ge(s["w_loaded"], 80)

            def step(t, r, p, known):
                if live(known, 3, groups):
                    act.wait_ge(s["gates_turned"], t - 2)
                    if since(known, 5):
                        act.wait_ge(s["down_done"], t - 4)
                    nc.scalar.activation(gatesT[1 - p][:, :, :], ps_g[:, :, :], ACT.Copy).then_inc(s["gatesT_done"], 1)
                for c in range(FC):
                    if c == 2 and live(known, 1, groups):
                        act.wait_ge(s["z_turned"], t)
                        if since(known, 3):
                            act.wait_ge(s["up_done"], (t - 2) * FC)
                        nc.scalar.activation(zTh[1 - p][:, :], ps_z[:, :], ACT.Copy).then_inc(s["zTh_done"], 1)
                    if live(known, 2, groups):
                        act.wait_ge(s["up_done"], (t - 2) * FC + c + 1)
                        if c == 0 and since(known, 4):
                            act.wait_ge(s["down_done"], t - 3)
                        nc.scalar.activation(hidden[p][:, c, :], ps_1[c % 2][:, :], ACT.Gelu,
                                             bias=b1[:, c:c + 1]).then_inc(s["hidden_done"], 1)
            run_steps(act, step, groups, LAG, PEEL)

        @block.tensor
        def _(pe):
            pe.wait_ge(s["w_loaded"], 80)
            pe.wait_ge(s["w1_split"], 1)

            def step(t, r, p, known):
                q = 1 - p
                for c in range(FC):
                    if live(known, 2, groups):
                        if c == 0:
                            pe.wait_ge(s["zT_done"], t - 1)
                        if c >= 2 or since(known, 3):
                            pe.wait_ge(s["hidden_done"], (t - 2) * FC + c - 1)
                        ch = slice(c * 128, (c + 1) * 128)
                        split_matmul(nc, ps_1[c % 2][:, :], (w1h[:, ch], w1l[:, ch]), (zTh[p][:, :], zTl[p][:, :]),
                                     True, True).then_inc(s["up_done"], 1)
                    if c == 1 and live(known, 1, groups):
                        pe.wait_ge(s["z_done"], t)
                        if since(known, 2):
                            pe.wait_ge(s["zT_done"], t - 1)
                        for b in range(GB):
                            last = nc.tensor.transpose(ps_z[:, b * T:(b + 1) * T], z[:, b, :], sh.ident[:, :])
                        last.then_inc(s["z_turned"], 1)
                    if c == 0 and live(known, 3, groups):
                        pe.wait_ge(s["gates_done"], t - 2)
                        if since(known, 4):
                            pe.wait_ge(s["gatesT_done"], t - 3)
                        for b in range(GB):
                            last = nc.tensor.transpose(ps_g[:, b, :], gates[:, b, :], sh.ident[:, :])
                        last.then_inc(s["gates_turned"], 1)
                    if c % 2 == 1 and live(known, 3, groups):
                        if c == 1:
                            pe.wait_ge(s["hidden_done"], (t - 2) * FC)
                            pe.wait_ge(s["gatesT_done"], t - 2)
                            if since(known, 5):
                                pe.wait_ge(s["shared_added"], t - 4)
                        for b in (c - 1, c):
                            for f in range(FC):
                                nc.tensor.matmul(ps_2[q][:, b, :], hidden[q][:, f, b * T:(b + 1) * T],
                                                 w2[:, f, :], start=(f == 0), stop=False)
                            last = nc.tensor.matmul(ps_2[q][:, b, :], gatesT[q][:, b, :], b2[:, :], start=False,
                                                    stop=True)
                        if c == 3:
                            last.then_inc(s["down_done"], 1)
            run_steps(pe, step, groups, LAG, PEEL)

        @block.vector
        def _(dve):
            dve.wait_ge(s["numbered"], 1)
            nc.vector.memset(gates[:, :, EXPERTS:NB2], 1.0)
            nc.vector.tensor_copy(number[:, :], number_i[:, :]).then_inc(s["number_set"], 1)
            dve.wait_ge(s["number_set"], 1)
            dve.wait_ge(s["w_loaded"], 80)
            nc.vector.tensor_copy(w1h[:, :], w1[:, :]).then_inc(s["w1h_done"], 1)
            dve.wait_ge(s["w1h_done"], 1)
            nc.vector.tensor_tensor(w1l[:, :], w1[:, :], w1h[:, :], ALU.subtract).then_inc(s["w1_split"], 1)

            def step(t, r, p, known):
                q = 1 - p
                g = t - 1
                if live(known, 1, groups):
                    if since(known, 2):
                        dve.wait_ge(s["z_turned"], t - 1)
                    for b in range(GB):
                        last = nc.vector.tensor_scalar(z[:, b, :], X[:, bass.ds(g * GB + b, 1), :].squeeze(1),
                                                       sh.mean[:, bass.ds(g * GB + b, 1)], sh.rstd[:, bass.ds(g * GB + b, 1)],
                                                       ALU.subtract, ALU.mult)
                    last.then_inc(s["z_done"], 1)
                if live(known, 2, groups):
                    nc.vector.tensor_tensor(
                        chosen[:, :, :],
                        sh.expert_of[:, bass.ds(t - 2, 1), :].squeeze(1).unsqueeze(2).to_broadcast([T, 2 * GB, EXPERTS]),
                        number[:, :].unsqueeze(1).to_broadcast([T, 2 * GB, EXPERTS]),
                        ALU.is_equal).then_inc(s["chosen_done"], 1)
                    dve.wait_ge(s["chosen_done"], t - 1)
                    for e in range(2):
                        last = nc.vector.tensor_tensor(
                            gated[:, e * GB:(e + 1) * GB, :], chosen[:, e * GB:(e + 1) * GB, :],
                            sh.gate[:, e, bass.ds((t - 2) * GB, GB)].unsqueeze(2).to_broadcast([T, GB, EXPERTS]), ALU.mult)
                    last.then_inc(s["gated_done"], 1)
                    dve.wait_ge(s["gated_done"], t - 1)
                    if since(known, 3):
                        dve.wait_ge(s["gates_turned"], t - 2)
                    nc.vector.tensor_tensor(gates[:, :, 0:EXPERTS], gated[:, 0:GB, :], gated[:, GB:2 * GB, :],
                                            ALU.add).then_inc(s["gates_done"], 1)
                if live(known, 1, groups):
                    dve.wait_ge(s["zTh_done"], t)
                    nc.vector.tensor_tensor(zTl[q][:, :], ps_z[:, :], zTh[q][:, :], ALU.subtract)\
                      .then_inc(s["zT_done"], 1)
                if live(known, 2, groups):
                    dve.wait_ge(y_gathered[p], r * 2 * GB * 16)
                    for e in range(2):
                        if e:
                            dve.wait_ge(s["weighted"], (t - 2) * 2 * GB + GB)
                        for b in range(GB):
                            at = X[:, bass.ds((t - 2) * GB + b, 1), :].squeeze(1)
                            nc.vector.scalar_tensor_tensor(
                                out=at, in0=y[p][:, e * GB + b, :],
                                scalar=sh.gate[:, e, bass.ds((t - 2) * GB + b, 1)], in1=at, op0=ALU.mult,
                                op1=ALU.add).then_inc(s["weighted"], 1)
                if live(known, 0, groups):
                    if since(known, 2):
                        dve.wait_ge(y_gathered[p], r * 2 * GB * 16)
                    nc.vector.tensor_copy(rows[p][:, :], sh.row_of[:, bass.ds(t, 1), :].squeeze(1))\
                      .then_inc(s["rows_done"], 1)
                if live(known, 3, groups):
                    dve.wait_ge(s["down_done"], t - 2)
                    dve.wait_ge(s["weighted"], (t - 2) * 2 * GB)
                    at = X[:, bass.ds((t - 3) * GB, GB), :]
                    nc.vector.tensor_tensor(at, at, ps_2[q][:, :, :], ALU.add).then_inc(s["shared_added"], 1)
            run_steps(dve, step, groups, LAG, PEEL)


def program(nc, x, adj, wts, out):
    n_graphs = x.shape[0]
    with ExitStack() as ctx:
        def sb(name, shape, dt=F32):
            return ctx.enter_context(nc.sbuf_tensor(name, shape, dt))

        sh = Shared()
        sh.X = sb("X", [T, n_graphs, D])
        sh.ident = sb("ident", [128, 128])
        sh.ident_bf = sb("ident_bf", [128, 128], BF16)
        sh.ones_bf = sb("ones_bf", [128, 128], BF16)
        sh.eps = sb("eps", [128, 8])
        sh.half_power = sb("half_power", [128, 8])
        sh.g1col, sh.b1col, sh.g2col, sh.b2col = (sb(n, [128, 1]) for n in ("g1col", "b1col", "g2col", "b2col"))
        sh.g1all, sh.b1all = sb("g1all", [128, D]), sb("b1all", [128, D])
        sh.wlogit = sb("wlogit", [D, HC])
        sh.wfx = sb("wfx", [D, HC])
        sh.wscore = sb("wscore", [128, 128])
        sh.wvalue = sb("wvalue", [128, HP, 128])
        sh.logit_bias = sb("logit_bias", [128, HC], BF16)
        sh.fx_bias = sb("fx_bias", [128, HC], BF16)
        sh.out_bias = sb("out_bias", [128, D], BF16)
        sh.conv1_bias = sb("conv1_bias", [128, D], BF16)
        sh.conv2_bias = sb("conv2_bias", [128, D], BF16)
        ffn0 = {k[len("L0_ffn_"):]: v for k, v in wts.items() if k.startswith("L0_ffn_")}
        gnn0 = {k[len("L0_gnn_"):]: v for k, v in wts.items() if k.startswith("L0_gnn_")}
        gnn1 = {k[len("L1_gnn_"):]: v for k, v in wts.items() if k.startswith("L1_gnn_")}
        ffn1 = {k[len("L1_ffn_"):]: v for k, v in wts.items() if k.startswith("L1_ffn_")}
        with semaphores(nc) as sem:
            setup_phase(nc, sem, sh, {**ffn0, **{k: gnn0[k] for k in ("gamma1", "beta1", "gamma2", "beta2")},
                                      "conv1_b": gnn1["b1"], "conv2_b": gnn1["b2"]})
        with ExitStack() as early:
            sh.X1 = early.enter_context(nc.sbuf_tensor("X1", [T, n_graphs, D], F32))
            with semaphores(nc) as sem:
                attention_phase(nc, sem, sh, x, adj, n_graphs)
            with semaphores(nc) as sem:
                mlp_phase(nc, sem, sh, gnn0, n_graphs)
        with semaphores(nc) as sem:
            slice_phase(nc, sem, sh, n_graphs)
        capacity, n_groups = routing_sizes(n_graphs * T)
        sh.sorted_z = nc.dram_tensor("sorted_z", [EXPERTS * capacity + W, D], F32, kind="Internal").ap()
        sh.sorted_y = nc.dram_tensor("sorted_y", [n_groups * W, D], F32, kind="Internal").ap()
        sh.expert_w1 = sb("expert_w1", [D, EXPERTS, FF])
        sh.expert_w2 = sb("expert_w2", [128, EXPERTS, FC * D])
        sh.expert_b1 = sb("expert_b1", [128, EXPERTS, FC])
        sh.mean = sb("mean", [T, n_graphs])
        sh.rstd = sb("rstd", [T, n_graphs])
        sh.gap = sb("gap", [T, n_graphs])
        sh.gate = sb("gate", [T, 2, n_graphs])
        sh.expert_of = sb("expert_of", [T, n_graphs // GB, 2 * GB])
        sh.row_of = sb("row_of", [T, n_graphs // GB, 2 * GB])
        sh.counts = sb("counts", [T, EXPERTS])
        sh.plan = sb("plan", [1, 2, n_groups], I32)
        with semaphores(nc) as sem:
            graph_phase(nc, sem, sh, adj, gnn1, ffn1, n_graphs)
        with semaphores(nc) as sem:
            schedule_phase(nc, sem, sh, n_graphs)
        with semaphores(nc) as sem:
            expert_phase(nc, sem, sh, n_graphs)
        with semaphores(nc) as sem:
            combine_phase(nc, sem, sh, ffn1, out, n_graphs)


_INS = ['x', 'adj', 'L0_gnn_gamma1', 'L0_gnn_beta1', 'L0_gnn_gamma2', 'L0_gnn_beta2', 'L0_gnn_W1', 'L0_gnn_b1',
        'L0_gnn_W2', 'L0_gnn_b2', 'L0_ffn_W_fx', 'L0_ffn_b_fx', 'L0_ffn_W_x', 'L0_ffn_b_x', 'L0_ffn_W_slice',
        'L0_ffn_b_slice', 'L0_ffn_W_q', 'L0_ffn_W_k', 'L0_ffn_W_v', 'L0_ffn_W_out', 'L0_ffn_b_out',
        'L0_ffn_temperature', 'L1_gnn_w_rel1', 'L1_gnn_w_root1', 'L1_gnn_b1', 'L1_gnn_w_rel2', 'L1_gnn_w_root2',
        'L1_gnn_b2', 'L1_ffn_Wr', 'L1_ffn_W1s', 'L1_ffn_b1s', 'L1_ffn_W2s', 'L1_ffn_b2s', 'L1_ffn_W1p',
        'L1_ffn_b1p', 'L1_ffn_W2p', 'L1_ffn_b2p']


def kernel(**inputs):
    import numpy as _np
    import concourse.bacc as _bacc
    from concourse import mybir as _mybir
    from concourse.bass_utils import run_bass_kernel_spmd as _run

    nc = _bacc.Bacc("TRN2", target_bir_lowering=False, num_devices=1)
    arrays, aps = {}, {}
    for name in _INS:
        a = _np.ascontiguousarray(inputs[name])
        arrays[f"in_{name}_dram"] = a
        aps[name] = nc.dram_tensor(f"in_{name}_dram", a.shape, _mybir.dt.from_np(a.dtype), kind="ExternalInput").ap()
    out = nc.dram_tensor("out_0_dram", inputs["x"].shape, _mybir.dt.float32, kind="ExternalOutput").ap()
    program(nc, aps["x"], aps["adj"], {n: aps[n] for n in _INS[2:]}, out)
    r = _run(nc, [arrays], core_ids=[0])
    return r.results[0]["out_0_dram"]
```
